# Optimizing a Trainium2 kernel written in Bass

```python
import numpy as np
import jax
import jax.numpy as jnp

def _softmax(x, axis=-1):
    return jax.nn.softmax(x, axis=axis)

def _gelu(x):
    return jax.nn.gelu(x, approximate=True)

def _silu(x):
    return jax.nn.silu(x)

def _sigmoid(x):
    return jax.nn.sigmoid(x)

def _layernorm(x, axis=-1, eps=1e-05):
    m = jnp.mean(x, axis=axis, keepdims=True)
    v = jnp.var(x, axis=axis, keepdims=True)
    return (x - m) / jnp.sqrt(v + eps)

def _scatter_add(tgt, idx, src, axis=0):
    return tgt.at[idx].add(src)

def _segment_sum(src, seg, n):
    return jax.ops.segment_sum(src, seg, n)
kernel_name = 'mk_gnn_ffn_d1_gnn_r8_d194c6'

def setup_inputs(seed: int=0):
    np.random.seed(seed)
    _w = jnp.asarray

    def _rec_inputs():
        import jax
        import jax.numpy as jnp
        _gk = jax.random.key(seed)
        x = -0.0003713 + 1 * jax.random.normal(jax.random.fold_in(_gk, 1), (6250, 256), jnp.float32)
        src = jax.random.randint(jax.random.fold_in(_gk, 2), (200000,), 0, 6250, jnp.int32)
        dst = jax.random.randint(jax.random.fold_in(_gk, 3), (200000,), 0, 6250, jnp.int32)
        _o = jnp.argsort(dst, stable=True)
        src = src[_o]
        dst = dst[_o]
        return (x, src, dst)
    x, src, dst = _rec_inputs()

    def _L0_gnn_setup():
        import jax, jax.numpy as jnp
        import numpy as np
        N_NODES = 6250
        N_EDGES = 100000
        D = 256
        key = jax.random.key(seed)
        k_x, k_e, k_w1, k_w2 = jax.random.split(key, 4)
        x = jax.random.normal(k_x, (N_NODES, D), dtype=jnp.float32)
        edge_index = jax.random.randint(k_e, (2, N_EDGES), 0, N_NODES, dtype=jnp.int64)
        W1 = jax.random.normal(k_w1, (D, D // 2), dtype=jnp.float32) * (1.0 / np.sqrt(D))
        b1 = jnp.zeros((D // 2,), dtype=jnp.float32)
        W2 = jax.random.normal(k_w2, (D // 2, 1), dtype=jnp.float32) * (1.0 / np.sqrt(D // 2))
        b2 = jnp.zeros((1,), dtype=jnp.float32)
        return {'x': x, 'edge_index': edge_index, 'W1': W1, 'b1': b1, 'W2': W2, 'b2': b2}
    _L0_gnn_all = _L0_gnn_setup()
    _L0_gnn_in = {k: v for k, v in _L0_gnn_all.items() if k in ('W1', 'b1', 'W2', 'b2')}
    del _L0_gnn_all

    def _L0_ffn_setup():
        import jax, jax.numpy as jnp
        import numpy as np
        BN_EPS = 0.001

        def _bn(h, g, b, m, v):
            return g * (h - m) * jax.lax.rsqrt(v + BN_EPS) + b
        key = jax.random.key(seed)
        ks = jax.random.split(key, 8)
        B, F, Df = (256, 64, 256)
        E, H, D = (8, 256, 256)
        s1 = 1.0 / np.sqrt(Df)
        s2 = 1.0 / np.sqrt(H)
        return {'x': jax.random.normal(ks[0], (B, F, Df), jnp.float32), 'Wr': jax.random.normal(ks[1], (Df, E), jnp.float32) * s1, 'br': jnp.zeros((E,), jnp.float32), 'W1': jax.random.normal(ks[2], (E, Df, H), jnp.float32) * s1, 'b1': jnp.zeros((E, H), jnp.float32), 'g1': jnp.ones((E, H), jnp.float32), 'be1': jnp.zeros((E, H), jnp.float32), 'm1': jnp.zeros((E, H), jnp.float32), 'v1': jnp.ones((E, H), jnp.float32), 'W2': jax.random.normal(ks[3], (E, H, H), jnp.float32) * s2, 'b2': jnp.zeros((E, H), jnp.float32), 'g2': jnp.ones((E, H), jnp.float32), 'be2': jnp.zeros((E, H), jnp.float32), 'm2': jnp.zeros((E, H), jnp.float32), 'v2': jnp.ones((E, H), jnp.float32), 'Wo': jax.random.normal(ks[4], (E, H, D), jnp.float32) * s2, 'bo': jnp.zeros((E, D), jnp.float32)}
    _L0_ffn_all = _L0_ffn_setup()
    _L0_ffn_in = {k: v for k, v in _L0_ffn_all.items() if k in ('Wr', 'br', 'W1', 'b1', 'g1', 'be1', 'm1', 'v1', 'W2', 'b2', 'g2', 'be2', 'm2', 'v2', 'Wo', 'bo')}
    del _L0_ffn_all
    return {'x': x, 'src': src, 'dst': dst, 'L0_gnn_W1': _L0_gnn_in['W1'], 'L0_gnn_b1': _L0_gnn_in['b1'], 'L0_gnn_W2': _L0_gnn_in['W2'], 'L0_gnn_b2': _L0_gnn_in['b2'], 'L0_ffn_Wr': _L0_ffn_in['Wr'], 'L0_ffn_br': _L0_ffn_in['br'], 'L0_ffn_W1': _L0_ffn_in['W1'], 'L0_ffn_b1': _L0_ffn_in['b1'], 'L0_ffn_g1': _L0_ffn_in['g1'], 'L0_ffn_be1': _L0_ffn_in['be1'], 'L0_ffn_m1': _L0_ffn_in['m1'], 'L0_ffn_v1': _L0_ffn_in['v1'], 'L0_ffn_W2': _L0_ffn_in['W2'], 'L0_ffn_b2': _L0_ffn_in['b2'], 'L0_ffn_g2': _L0_ffn_in['g2'], 'L0_ffn_be2': _L0_ffn_in['be2'], 'L0_ffn_m2': _L0_ffn_in['m2'], 'L0_ffn_v2': _L0_ffn_in['v2'], 'L0_ffn_Wo': _L0_ffn_in['Wo'], 'L0_ffn_bo': _L0_ffn_in['bo']}

def reference(x, src, dst, L0_gnn_W1, L0_gnn_b1, L0_gnn_W2, L0_gnn_b2, L0_ffn_Wr, L0_ffn_br, L0_ffn_W1, L0_ffn_b1, L0_ffn_g1, L0_ffn_be1, L0_ffn_m1, L0_ffn_v1, L0_ffn_W2, L0_ffn_b2, L0_ffn_g2, L0_ffn_be2, L0_ffn_m2, L0_ffn_v2, L0_ffn_Wo, L0_ffn_bo):
    import jax
    import jax.numpy as jnp

    def _L0_gnn_ref(x, edge_index, W1, b1, W2, b2):
        import jax, jax.numpy as jnp
        import numpy as np
        N_NODES = 6250
        N_EDGES = 100000
        D = 256
        row, col = (edge_index[0], edge_index[1])
        neigh = x[col]
        h = jax.nn.relu(neigh @ W1 + b1)
        w = jax.nn.sigmoid(h @ W2 + b2)
        num = jax.ops.segment_sum(neigh * w, row, num_segments=N_NODES)
        den = jax.ops.segment_sum(w, row, num_segments=N_NODES)
        out = jnp.where(den > 0, num / jnp.maximum(den, 1e-12), 0.0)
        return out

    def _L0_ffn_ref(x, Wr, br, W1, b1, g1, be1, m1, v1, W2, b2, g2, be2, m2, v2, Wo, bo):
        import jax, jax.numpy as jnp
        import numpy as np
        BN_EPS = 0.001

        def _bn(h, g, b, m, v):
            return g * (h - m) * jax.lax.rsqrt(v + BN_EPS) + b
        feat = jnp.mean(x, axis=0)
        w = jax.nn.softmax(feat @ Wr + br, axis=-1)
        h = jnp.einsum('bfd,edh->bfeh', x, W1) + b1
        h = jax.nn.relu(_bn(h, g1, be1, m1, v1))
        h = jnp.einsum('bfeh,ehk->bfek', h, W2) + b2
        h = jax.nn.relu(_bn(h, g2, be2, m2, v2))
        y = jnp.einsum('bfeh,ehd->bfed', h, Wo) + bo
        return jnp.einsum('bfed,fe->bfd', y, w)
    edge_index = jnp.stack([src, dst])
    x = x + _L0_gnn_ref(_layernorm(x, axis=-1), edge_index, L0_gnn_W1, L0_gnn_b1, L0_gnn_W2, L0_gnn_b2)
    x = x + _L0_ffn_ref(_layernorm(x, axis=-1)[None], L0_ffn_Wr, L0_ffn_br, L0_ffn_W1, L0_ffn_b1, L0_ffn_g1, L0_ffn_be1, L0_ffn_m1, L0_ffn_v1, L0_ffn_W2, L0_ffn_b2, L0_ffn_g2, L0_ffn_be2, L0_ffn_m2, L0_ffn_v2, L0_ffn_Wo, L0_ffn_bo)[0]
    return x

_drawn_inputs = setup_inputs


def setup_inputs(seed=0):
    import zlib

    import numpy as np

    out = dict(_drawn_inputs(seed))
    spreads = {'L0_gnn_b1': (0.0, 2.0),
     'L0_ffn_br': (0.0, 0.1),
     'L0_ffn_b1': (0.0, 0.325),
     'L0_ffn_g1': (1.0, 0.2),
     'L0_ffn_be1': (0.0, 0.332),
     'L0_ffn_m1': (0.0, 0.324),
     'L0_ffn_v1': (1.0, 0.6),
     'L0_ffn_b2': (0.0, 0.1),
     'L0_ffn_g2': (1.0, 0.2),
     'L0_ffn_be2': (0.0, 0.1),
     'L0_ffn_m2': (0.0, 0.1),
     'L0_ffn_v2': (1.0, 0.569),
     'L0_ffn_bo': (0.0, 0.1)}
    factors = {}
    for name, (base, spread) in spreads.items():
        noise = np.random.default_rng([zlib.crc32(name.encode()), seed]).standard_normal(out[name].shape)
        drawn = base * np.exp(spread * noise) if base else spread * noise
        out[name] = jnp.asarray(drawn.astype(out[name].dtype))
    for name, factor in factors.items():
        out[name] = (out[name] * factor).astype(out[name].dtype)
    return out
```

```python
import concourse.bass as bass
from concourse import mybir
from contextlib import ExitStack

P = 128
N_NODES = 6250
N_EDGES = 200000
D = 256
HID = 128
N_EXP = 8
KC = D // P
NT = -(-N_NODES // P)
NPAIR = (NT + 1) // 2
NT2 = 2 * NPAIR
SLOT = 64
WIN = SLOT + 1
BLK = 512
NBLK = -(-N_EDGES // BLK)
E_PAD = (NBLK + 1) * BLK
FRONT = SLOT
SORT_P = 125
SORT_N = N_EDGES // SORT_P
DST_ROWS = FRONT + E_PAD + SORT_N
SPILL_CH = -(-N_EDGES // P)
DST_PAD = 16384
GT = 7
NG = NT // GT
VW = D + 2
SG = 5
NSG = NT2 // SG
NHI = NT
NONE_HI = 127
CG = 16
NCG = P // CG
HS = 7
NS = NHI // HS
LN_EPS = 1e-5
BN_EPS = 1e-3
CH = 4
N_SHORT = -NT % CH
N_CHUNK = -(-NT // CH)
LAYERS = 2


def program(nc, x, dst, edges, g_w1, g_b1, g_w2, g_b2, f_wr, f_br, f_w1, f_b1, f_g1, f_be1, f_m1, f_v1,
            f_w2, f_b2, f_g2, f_be2, f_m2, f_v2, f_wo, f_bo, out, values):
    f32, bf16, i32, f32r = mybir.dt.float32, mybir.dt.bfloat16, mybir.dt.int32, mybir.dt.float32r
    ALU, ACT, AX = mybir.AluOpType, mybir.ActivationFunctionType, mybir.AxisListType

    stack = ExitStack()
    with stack:
        def sem(name):
            return stack.enter_context(nc.semaphore(name))

        def sb(where, name, shape, dt):
            return where.enter_context(nc.sbuf_tensor(name, shape, dt))

        ident = sb(stack, "ident", [P, P], f32)
        ident16 = sb(stack, "ident16", [P, P], bf16)
        ones_row = sb(stack, "ones_row", [1, P], f32)
        eps_ln = sb(stack, "eps_ln", [P, 1], f32)
        stats = sb(stack, "stats", [P, NT, 6], f32)
        mean_var = sb(stack, "mean_var", [P, NT, 2], f32)
        rstd = sb(stack, "rstd", [P, NT], f32)
        bn_cols = sb(stack, "bn_cols", [P, 2 * LAYERS, N_EXP * KC], f32)
        wr_sb = sb(stack, "wr_sb", [P, KC, N_EXP], f32)
        wr_split = [sb(stack, f"wr_{n}", [P, KC, N_EXP], f32r) for n in ("hi", "lo")]
        br_sb = sb(stack, "br_sb", [P, N_EXP], f32)
        bo_sb = sb(stack, "bo_sb", [N_EXP, D], f32)
        eps_bn = sb(stack, "eps_bn", [P, 1], f32)
        den = sb(stack, "den", [P, 3, HS], f32)
        logits = sb(stack, "logits", [P, CH, N_EXP], f32)
        top = sb(stack, "top", [P, CH], f32)
        expert_w = [sb(stack, f"expert_w{i}", [P, CH, N_EXP], f32) for i in range(2)]
        expert_wt = sb(stack, "expert_wt", [N_EXP, CH * P], f32)
        ones_sq = sb(stack, "ones_sq", [P, P], f32)
        flags = sb(stack, "flags", [P, 2], f32)
        unsorted = sb(stack, "unsorted", [P, 1], f32)
        general = sb(stack, "general", [P, 1], f32)
        general_i = sb(stack, "general_i", [P, 1], i32)
        lists = ExitStack()
        hi_list = sb(lists, "hi_list", [P, NPAIR, P], bf16)
        lo_list = sb(lists, "lo_list", [P, NPAIR, P], bf16)
        psum = stack.enter_context(nc.psum_tensor("psum", [P, 8, 512], f32))

        ph1 = ExitStack()
        x_sb = sb(ph1, "x_sb", [P, NT, D], f32)
        xn = [sb(ph1, f"xn{i}", [P, GT, D], f32) for i in range(2)]
        xt = sb(ph1, "xt", [P, KC, GT * P], f32)
        hid = sb(ph1, "hid", [P, GT * P], f32)
        gate = sb(ph1, "gate", [P, NT], f32)
        vf = sb(ph1, "vf", [P, GT, VW], f32)
        vs = [sb(ph1, f"vs{i}", [P, GT, 2, VW], f32r) for i in range(2)]
        w1_sb = sb(ph1, "w1_sb", [P, KC, HID], f32)
        b1_sb = sb(ph1, "b1_sb", [HID, 1], f32)
        bn_rows = sb(ph1, "bn_rows", [N_EXP * KC, 5 * LAYERS, P], f32)
        bn_tmp = sb(ph1, "bn_tmp", [N_EXP * KC, 2 * LAYERS, P], f32)
        w2_sb = sb(ph1, "w2_sb", [HID, 1], f32)
        b2_sb = sb(ph1, "b2_sb", [P, 1], f32)
        hi_bias = sb(ph1, "hi_bias", [P, 1], f32)
        node_i = sb(ph1, "node_i", [P, NT2], i32)
        node_id = sb(ph1, "node_id", [P, NT2], f32)
        order_i = sb(ph1, "order_i", [SORT_P, SORT_N + 1], i32)
        node_cmp = sb(ph1, "node_cmp", [P, NT2], f32)
        samp_i = sb(ph1, "samp_i", [1, NBLK], i32)
        samp_f = sb(ph1, "samp_f", [1, NBLK], f32)
        samp = sb(ph1, "samp", [P, NBLK], f32)
        less = sb(ph1, "less", [P, BLK], f32)
        n_blocks = sb(ph1, "n_blocks", [P, NT2], f32)
        block_f = sb(ph1, "block_f", [P, NT2], f32)
        block_i = sb(ph1, "block_i", [P, NT2], i32)
        n_less = sb(ph1, "n_less", [P, NT2], f32)
        row_f = sb(ph1, "row_f", [P, NT2], f32)
        row_i = sb(ph1, "row_i", [P, NT2], i32)
        blk_i = [sb(ph1, f"blk_i{i}", [P, SG, BLK], i32) for i in range(2)]
        blk_f = sb(ph1, "blk_f", [P, SG, BLK], f32)
        order_f = blk_f[0:SORT_P, :, :].rearrange("p g k -> p (g k)")[:, 0:SORT_N]
        win = sb(ph1, "win", [P, NT2, 2 * WIN], i32)
        ph1.close()
        ph1b = ExitStack()
        slot_dst = sb(ph1b, "slot_dst", [P, NT2, WIN], f32)
        slot_ok = sb(ph1b, "slot_ok", [P, NT2, WIN], f32)
        slot_hi = sb(ph1b, "slot_hi", [P, NT2, SLOT], i32)
        slot_lo = sb(ph1b, "slot_lo", [P, NT2, SLOT], i32)
        hi16 = sb(ph1b, "hi16", [P, NT2, SLOT], bf16)
        lo16 = sb(ph1b, "lo16", [P, NT2, SLOT], bf16)
        ph1b.close()

        ph2 = ExitStack()
        acc = sb(ph2, "acc", [P, NT, VW], f32)
        counts = [sb(ph2, f"counts{i}", [P, 2 * NHI, P], bf16) for i in range(2)]
        counts_t = [sb(ph2, f"counts_t{i}", [P, NHI * P], f32r) for i in range(2)]
        vring = [sb(ph2, f"vring{i}", [P, 2, 2 * VW], f32r) for i in range(2)]
        iota_lo = sb(ph2, "iota_lo", [P, P, CG], bf16)
        iota_hi = sb(ph2, "iota_hi", [P, 2 * NHI, CG], bf16)
        hot_lo = [sb(ph2, f"hot_lo{i}", [P, P, CG], bf16) for i in range(2)]
        hot_hi = [sb(ph2, f"hot_hi{i}", [P, 2 * NHI, CG], bf16) for i in range(2)]
        ph2.close()
        ph2s = ExitStack()
        sb(ph2s, "acc_below3", [P, NT, VW], f32)
        sp_edge = sb(ph2s, "sp_edge", [P, 2], i32)
        sp_prev = sb(ph2s, "sp_prev", [P, 1], i32)
        sp_f = sb(ph2s, "sp_f", [P, 8], f32)
        sp_int = sb(ph2s, "sp_int", [P, 4], i32)
        sp_iota_i = sb(ph2s, "sp_iota_i", [P, P], i32)
        sp_iota = sb(ph2s, "sp_iota", [P, P], f32)
        sp_idle = sb(ph2s, "sp_idle", [P, 1], f32)
        sp_hot = sb(ph2s, "sp_hot", [P, P], f32)
        sp_rows = sb(ph2s, "sp_rows", [P, 2 * VW], f32)
        sp_val = sb(ph2s, "sp_val", [P, VW], f32)
        sp_pick = sb(ph2s, "sp_pick", [P, HS, VW], f32)
        ph2s.close()
        ph2b = ExitStack()
        sb(ph2b, "acc_below", [P, NT, VW], f32)
        sb(ph2b, "counts_below", [P, 2, 2 * NHI * P], bf16)
        iota_i = [sb(ph2b, f"iota_i{i}", [P, w * CG], i32) for i, w in enumerate((P, 2 * NHI))]
        ph2b.close()
        ph2c = ExitStack()
        sb(ph2c, "acc_below2", [P, NT, VW], f32)
        sb(ph2c, "counts_below2", [P, 2, 2 * NHI * P], bf16)
        sb(ph2c, "counts_t_below2", [P, 2, NHI * P], f32)
        sb(ph2c, "vring_below2", [P, 2, 2, 2 * VW], f32)
        sb(ph2c, "iota_below2", [P, P + 2 * NHI, CG], bf16)
        x_again = [sb(ph2c, f"x_again{i}", [P, HS, D], f32) for i in range(2)]
        ph2c.close()
        lists.close()

        ph3 = ExitStack()
        xn2 = sb(ph3, "xn2", [P, CH, D], f32)
        relu_out = [[sb(ph3, f"relu_out{l}{m}", [P, CH * P], f32) for m in range(KC)] for l in range(LAYERS)]
        sb(ph3, "lists_rest", [P, 2 * NPAIR * P - 2 * (CH * D + LAYERS * KC * CH * P)], bf16)
        sb(ph3, "acc_kept", [P, NT, VW], f32)
        w_split = [[sb(ph3, f"w{l}_{n}", [P, N_EXP, KC, D], f32r) for n in ("hi", "lo")] for l in range(LAYERS + 1)]
        stage = ExitStack()
        w_stage = [sb(stage, f"w_stage{i}", [P, N_EXP, KC, D], f32) for i in range(2)]
        stage.close()
        xt2 = [[sb(ph3, f"xt2_{n}{i}", [P, KC, CH * P], f32r) for n in ("hi", "lo")] for i in range(2)]
        h1 = [[sb(ph3, f"h1_{n}{i}", [P, KC, CH * P], f32r) for n in ("hi", "lo")] for i in range(2)]
        h2 = [sb(ph3, f"h2_{n}", [P, KC, CH * P], f32r) for n in ("hi", "lo")]
        ph3.close()

        consts_ready = sem("consts_ready")
        x_in = sem("x_in")
        gate_w_in = sem("gate_w_in")
        samp_in = sem("samp_in")
        chain = sem("chain")
        pool_chain = sem("pool_chain")
        order_in = sem("order_in")
        order_ready = sem("order_ready")
        order_total = sem("order_total")
        general_count = sem("general_count")
        general_total = sem("general_total")
        general_ready = sem("general_ready")
        sp_iota_ready = sem("sp_iota_ready")
        sp_chain = sem("sp_chain")
        sp_edge_in = sem("sp_edge_in")
        sp_prev_in = sem("sp_prev_in")
        sp_index = sem("sp_index")
        sp_rows_in = sem("sp_rows_in")
        sp_picked = sem("sp_picked")
        sp_ps = sem("sp_ps")
        sp_added = sem("sp_added")
        sp_chunk_done = sem("sp_chunk_done")
        var_ready = sem("var_ready")
        std_ready = sem("std_ready")
        samp_f_ready = sem("samp_f_ready")
        samp_bc = sem("samp_bc")
        block_ready = sem("block_ready")
        blk_in = [sem(f"blk_in{i}") for i in range(2)]
        blk_conv = sem("blk_conv")
        blk_counted = sem("blk_counted")
        row_ready = sem("row_ready")
        win_in = sem("win_in")
        slots_ready = sem("slots_ready")
        lists_tp = sem("lists_tp")
        lists_ready = sem("lists_ready")
        xn_ready = sem("xn_ready")
        xt_ps = sem("xt_ps")
        xt_ready = sem("xt_ready")
        hid_ps = sem("hid_ps")
        hid_ready = sem("hid_ready")
        logit_ps = sem("logit_ps")
        gate_ready = sem("gate_ready")
        vs_ready = sem("vs_ready")
        vs_out = [sem(f"vs_out{i}") for i in range(2)]
        phase1_done = sem("phase1_done")
        iota_ready = sem("iota_ready")
        iota16_ready = sem("iota16_ready")
        acc_zero = sem("acc_zero")
        hot_used = sem("hot_used")
        hot_lo_ready = sem("hot_lo_ready")
        hot_hi_ready = sem("hot_hi_ready")
        cnt_ps = sem("cnt_ps")
        cnt_ps_free = sem("cnt_ps_free")
        tp_ps = sem("tp_ps")
        tp_ps_free = sem("tp_ps_free")
        v_in = [sem(f"v_in{i}") for i in range(2)]
        v_used = sem("v_used")
        sum_ps = sem("sum_ps")
        sum_ps_free = sem("sum_ps_free")
        fin_ready = sem("fin_ready")
        x_again_in = [sem(f"x_again_in{i}") for i in range(2)]
        x_again_used = sem("x_again_used")
        bn_in = sem("bn_in")
        bn_var = sem("bn_var")
        bn_std = sem("bn_std")
        bn_row_ready = sem("bn_row_ready")
        bn_tp = sem("bn_tp")
        bn_ready = sem("bn_ready")
        phase2_done = sem("phase2_done")
        w_in = [sem(f"w_in{i}") for i in range(2)]
        w_hi = sem("w_hi")
        w_ready = sem("w_ready")
        var2_ready = sem("var2_ready")
        std2_ready = sem("std2_ready")
        xn2_ready = sem("xn2_ready")
        xt2_ps = sem("xt2_ps")
        xt2_hi = sem("xt2_hi")
        xt2_ready = sem("xt2_ready")
        soft = sem("soft")
        route_ps = sem("route_ps")
        route_shifted = sem("route_shifted")
        route_exp = sem("route_exp")
        route_ready = sem("route_ready")
        route_tp = sem("route_tp")
        route_t_ready = sem("route_t_ready")
        bias_ps = sem("bias_ps")
        bias_read = sem("bias_read")
        layer_ps = [sem(f"layer_ps{l}") for l in range(LAYERS)]
        layer_read = [sem(f"layer_read{l}") for l in range(LAYERS)]
        h_ready = [sem(f"h_ready{l}") for l in range(LAYERS)]
        y_ps = sem("y_ps")
        y_read = sem("y_read")
        rows_ready = sem("rows_ready")
        out_done = sem("out_done")

        block = stack.enter_context(nc.Block())
        x_tiles = x.rearrange("(t p) d -> p t d", p=P)
        v_rows = values.rearrange("(t p) w -> p t w", p=P)

        def groups_of(s):
            return range(NCG * s // NS, NCG * (s + 1) // NS)

        def chunk(c, par):
            if isinstance(c, int) and c < N_SHORT:
                return c, par, CH - 1, c * (CH - 1)
            return c, par, CH, c * CH - N_SHORT

        def chunks(eng, step):
            def one(c, par, first, last):
                prev = None if first else chunk(c - 1, 1 - par)
                if isinstance(c, int) and c == N_SHORT and not first:
                    prev = chunk(N_SHORT - 1, 1 - par)
                nxt = None if last else chunk(c + 1, 1 - par)
                for e in range(N_EXP):
                    step(prev, chunk(c, par), nxt, e)
            head = N_SHORT + 1
            pairs = (N_CHUNK - head - 1) // 2
            for c in range(head):
                one(c, c % 2, c == 0, False)
            with eng.Fori(0, pairs) as i:
                for k in range(2):
                    one(2 * i + (head + k), (head + k) % 2, False, False)
            for c in range(head + 2 * pairs, N_CHUNK):
                one(c, c % 2, False, c == N_CHUNK - 1)

        def rounds(eng, body):
            with eng.Fori(0, (NPAIR - 3) // 2) as i:
                for par in range(2):
                    body(2 * i + par, par, True, True, 2)
            for b in range((NPAIR - 3) // 2 * 2, NPAIR):
                body(b, b % 2, b + 1 < NPAIR, b + 2 < NPAIR, 2 if b + 1 < NPAIR else NT - 2 * (NPAIR - 1))

        @block.sync
        def _(sp):
            sp.dma_start(samp_i[:, :], dst[FRONT:FRONT + NBLK * BLK, 0:1].rearrange("(b k) o -> o b k", k=BLK)[:, :, 0],
                         allow_slow_non_contiguous=True).then_inc(samp_in, 16)
            sp.dma_start(order_i[:, 0:SORT_N], dst[FRONT:FRONT + N_EDGES, 0:1].rearrange("(p k) o -> p (k o)", k=SORT_N)).then_inc(order_in, 16)
            sp.dma_start(order_i[:, SORT_N:SORT_N + 1],
                         dst[FRONT + SORT_N:FRONT + SORT_N + N_EDGES, 0:1].rearrange("(p k) o -> p (k o)", k=SORT_N)[:, 0:1],
                         allow_slow_non_contiguous=True).then_inc(order_in, 16)
            for g in range(NG):
                sp.dma_start(x_sb[:, g * GT:(g + 1) * GT, :], x_tiles[:, g * GT:(g + 1) * GT, :]).then_inc(x_in, 16)
            for l, params in enumerate(((f_g1, f_b1, f_m1, f_be1, f_v1), (f_g2, f_b2, f_m2, f_be2, f_v2))):
                for k, prm in enumerate(params):
                    sp.dma_start(bn_rows[:, 5 * l + k, :], prm.rearrange("e (m p) -> (e m) p", p=P)).then_inc(bn_in, 16)
            sp.dma_start(wr_sb[:, :, :], f_wr.rearrange("(k p) e -> p k e", p=P)).then_inc(bn_in, 16)
            sp.dma_start(br_sb[:, :], f_br.rearrange("(o e) -> o e", o=1).broadcast_to([P, N_EXP])).then_inc(bn_in, 16)
            sp.dma_start(bo_sb[:, :], f_bo).then_inc(bn_in, 16)
            sp.dma_start(w1_sb[:, :, :], g_w1.rearrange("(k p) h -> p k h", p=P)).then_inc(gate_w_in, 16)
            sp.dma_start(b1_sb[:, :], g_b1.rearrange("(p o) -> p o", o=1)).then_inc(gate_w_in, 16)
            sp.dma_start(w2_sb[:, :], g_w2).then_inc(gate_w_in, 16)
            sp.dma_start(b2_sb[:, :], g_b2.rearrange("(p o) -> p o", o=1).broadcast_to([P, 1])).then_inc(gate_w_in, 16)

            def store(b, par):
                sp.wait_ge(vs_ready, b + 1)
                sp.dma_start(v_rows[:, bass.ds(b * GT, GT), :],
                             vs[par][:, :, :, :].rearrange("p t h w -> p t (h w)").bitcast(f32)).then_inc(vs_out[par], 16)
            with sp.Fori(0, NG // 2) as i:
                for par in range(2):
                    store(2 * i + par, par)
            store(NG - 1, 0)
            sp.wait_ge(vs_out[0], 16 * (NG // 2 + 1))
            sp.wait_ge(vs_out[1], 16 * (NG // 2))
            sp.sem_inc(phase1_done, 1)
            sp.wait_ge(phase1_done, 5)

            def load_values(b, par, has_next, has_next2, tiles):
                sp.wait_ge(v_used, b + 1)
                sp.dma_start(vring[par][:, 0:tiles, :].bitcast(f32), v_rows[:, bass.ds(2 * b, tiles), :]).then_inc(v_in[par], 16)
            rounds(sp, load_values)

            for s in range(NS):
                if s < 2:
                    sp.wait_ge(hot_used, NPAIR * NCG + 2)
                else:
                    sp.wait_ge(x_again_used, s - 1)
                sp.dma_start(x_again[s % 2][:, :, :], x_tiles[:, s * HS:(s + 1) * HS, :]).then_inc(x_again_in[s % 2], 16)
            sp.sem_inc(phase2_done, 1)
            sp.wait_ge(phase2_done, 5)
            for l, w in enumerate((f_w1, f_w2, f_wo)):
                if l >= 2:
                    sp.wait_ge(w_ready, l - 1)
                sp.dma_start(w_stage[l % 2][:, :, :, :], w.rearrange("e (k p) h -> p e k h", p=P)).then_inc(w_in[l % 2], 16)

            out_tiles = out.rearrange("(t p) d -> p t d", p=P)

            def step(prev, cur, nxt, e):
                if e == 0 and prev is not None:
                    c, par, n, t0 = prev
                    sp.wait_ge(rows_ready, c + 1)
                    sp.dma_start(out_tiles[:, bass.ds(t0, n), :], acc[:, bass.ds(t0, n), 0:D]).then_inc(out_done, 16)
            chunks(sp, step)
            c, par, n, t0 = chunk(N_CHUNK - 1, (N_CHUNK - 1) % 2)
            sp.wait_ge(rows_ready, c + 1)
            sp.dma_start(out_tiles[:, bass.ds(t0, n), :], acc[:, bass.ds(t0, n), 0:D]).then_inc(out_done, 16)
            sp.wait_ge(out_done, 16 * N_CHUNK)

        @block.gpsimd
        def _(pool):
            pool.memset(ident[:, :], 0.0).then_inc(pool_chain, 1)
            pool.memset(ident16[:, :], 0.0).then_inc(pool_chain, 1)
            pool.iota(node_i[:, :], pattern=[[P, NT2]], base=0, channel_multiplier=1).then_inc(pool_chain, 1)
            pool.wait_ge(pool_chain, 3)
            for m in (ident, ident16):
                pool.affine_select(out=m[:, :], in_=m[:, :], compare_op=ALU.not_equal, fill=1.0, base=0,
                                   pattern=[[-1, P]], channel_multiplier=1).then_inc(consts_ready, 1)
            pool.tensor_copy(node_id[:, :], node_i[:, :]).then_inc(consts_ready, 1)
            pool.memset(hi_bias[:, :], float(NONE_HI)).then_inc(consts_ready, 1)
            pool.memset(ones_row[:, :], 1.0).then_inc(consts_ready, 1)
            pool.memset(ones_sq[:, :], 1.0).then_inc(consts_ready, 1)
            pool.memset(eps_ln[:, :], LN_EPS).then_inc(consts_ready, 1)
            pool.memset(eps_bn[:, :], BN_EPS).then_inc(consts_ready, 1)
            pool.wait_ge(consts_ready, 8)
            pool.memset(hi_bias[SLOT:P, :], float(NONE_HI + NHI)).then_inc(consts_ready, 1)

            pool.wait_ge(block_ready, 1)

            def fetch_blocks(g, par):
                pool.wait_ge(blk_conv, g + 1)
                for j in range(SG):
                    pool.indirect_dma_start(out=blk_i[par][:, j, :], out_offset=None, in_=dst[:, :],
                                            in_offset=bass.IndirectOffsetOnAxis(ap=block_i[:, bass.ds(g * SG + j, 1)], axis=0),
                                            ).then_inc(blk_in[par], 16)
            for g in range(NSG):
                fetch_blocks(g, g % 2)
            pool.wait_ge(row_ready, 1)
            for t in range(NT2):
                pool.indirect_dma_start(out=win[:, t, :], out_offset=None, in_=edges[:, :],
                                        in_offset=bass.IndirectOffsetOnAxis(ap=row_i[:, t:t + 1], axis=0),
                                        ).then_inc(win_in, 16)
            pool.drain().then_inc(phase1_done, 1)
            pool.wait_ge(phase1_done, 5)

            pool.wait_ge(general_ready, 1)
            with pool.If(pool.value_load(general_i[0:1, 0:1], min_val=0, max_val=1) > 0):
                pool.iota(sp_iota_i[:, :], pattern=[[1, P]], base=0, channel_multiplier=0).then_inc(sp_iota_ready, 1)
                pool.wait_ge(sp_iota_ready, 1)
                pool.tensor_copy(sp_iota[:, :], sp_iota_i[:, :]).then_inc(sp_iota_ready, 1)
                with pool.Fori(0, SPILL_CH) as k:
                    pool.wait_ge(sp_chunk_done, k + 1)
                    pool.dma_start(sp_edge[:, :], edges[bass.ds(k * P, P), :]).then_inc(sp_edge_in, 16)
                    pool.dma_start(sp_prev[:, :], dst[bass.ds(k * P, P), :]).then_inc(sp_prev_in, 16)
                    pool.wait_ge(sp_index, k + 1)
                    pool.tensor_tensor(sp_idle[:, :], sp_iota[:, 0:1], sp_iota[:, 0:1], ALU.subtract)
                    pool.indirect_dma_start(out=sp_rows[:, :], out_offset=None, in_=values[:, :],
                                            in_offset=bass.IndirectOffsetOnAxis(ap=sp_int[:, 0:1], axis=0)).then_inc(sp_rows_in, 16)

            pool.iota(iota_i[0][:, :], pattern=[[1, P], [0, CG]], base=0, channel_multiplier=0).then_inc(iota_ready, 1)
            pool.iota(iota_i[1][:, :], pattern=[[1, 2 * NHI], [0, CG]], base=0, channel_multiplier=0).then_inc(iota_ready, 1)
            pool.wait_ge(iota_ready, 2)
            pool.tensor_copy(iota_lo[:, :, :].rearrange("p a c -> p (a c)"), iota_i[0][:, :]).then_inc(iota16_ready, 1)
            pool.tensor_copy(iota_hi[:, :, :].rearrange("p a c -> p (a c)"), iota_i[1][:, :]).then_inc(iota16_ready, 1)
            pool.drain().then_inc(phase2_done, 1)

        @block.scalar
        def _(act):
            act.sem_inc(blk_conv, 2)
            act.wait_ge(bn_in, 16 * (5 * LAYERS + 3))
            act.wait_ge(consts_ready, 9)
            for l in range(LAYERS):
                act.activation(bn_tmp[:, 2 * l, :], bn_rows[:, 5 * l + 4, :], ACT.Sqrt, bias=eps_bn[0:N_EXP * KC, :]).then_inc(bn_std, 1)
            act.activation(wr_split[0][:, :, :], wr_sb[:, :, :], ACT.Copy).then_inc(bn_std, 1)
            act.wait_ge(bn_tp, 1)
            act.activation(bn_cols[:, :, :].rearrange("p a b -> p (a b)"), psum[:, 7, 0:2 * LAYERS * N_EXP * KC], ACT.Copy).then_inc(bn_ready, 1)
            act.wait_ge(var_ready, 1)
            act.activation(rstd[:, :], mean_var[:, :, 1], ACT.Sqrt, bias=eps_ln[:, :]).then_inc(std_ready, 1)

            def gate_act(b):
                for q in range(4):
                    k, lo, n = q // 2, 512 * (q % 2), (512, GT * P - 512)[q % 2]
                    if q == 0:
                        act.wait_ge(xt_ps, b + 1)
                    act.activation(xt[:, k, lo:lo + n], psum[:, q, 0:n], ACT.Copy).then_inc(xt_ready, 1)
                act.wait_ge(hid_ps, b + 1)
                for q in range(2):
                    lo, n = 512 * q, (512, GT * P - 512)[q]
                    act.activation(hid[:, lo:lo + n], psum[:, 4 + q, 0:n], ACT.Relu, bias=b1_sb[:, :]).then_inc(hid_ready, 1)
                act.wait_ge(logit_ps, b + 1)
                act.activation(gate[:, bass.ds(b * GT, GT)], psum[:, 6, 0:GT], ACT.Sigmoid, bias=b2_sb[:, :]).then_inc(gate_ready, 1)
            act.wait_ge(gate_w_in, 64)
            with act.Fori(0, NG) as b:
                gate_act(b)
            for g in range(NSG):
                act.wait_ge(blk_in[g % 2], 16 * SG * (g // 2 + 1))
                act.wait_ge(blk_counted, g + 1)
                act.activation(blk_f[:, :, :], blk_i[g % 2][:, :, :], ACT.Copy).then_inc(blk_conv, 1)

            for q in range(-(-NPAIR // 4)):
                n = min(4, NPAIR - 4 * q)
                act.wait_ge(lists_tp, 2 * q + 1)
                act.activation(hi_list[:, 4 * q:4 * q + n, :].rearrange("p t c -> p (t c)"),
                               psum[:, (2 * q) % 4, :].bitcast(bf16)[:, 0:n * P], ACT.Identity, bias=hi_bias[:, :]).then_inc(lists_ready, 1)
                act.wait_ge(lists_tp, 2 * q + 2)
                act.activation(lo_list[:, 4 * q:4 * q + n, :].rearrange("p t c -> p (t c)"),
                               psum[:, (2 * q + 1) % 4, :].bitcast(bf16)[:, 0:n * P], ACT.Copy).then_inc(lists_ready, 1)
            act.drain().then_inc(phase1_done, 1)
            act.wait_ge(phase1_done, 5)
            act.sem_inc(cnt_ps_free, 2)
            act.sem_inc(tp_ps_free, 2)
            act.wait_ge(iota16_ready, 2)

            def take_counts(b, par, g):
                for h in range(2):
                    act.wait_ge(cnt_ps, b * 2 * NCG + 2 * g + h + 1)
                    src = psum[:, 2 * h:2 * h + 2, 0:4 * 2 * NHI].rearrange("p k (c j) -> p j k c", c=4)
                    c0 = g * CG + h * 8
                    dstv = counts[par][:, :, c0:c0 + 8].rearrange("p j (k c) -> p j k c", k=2)
                    act.activation(dstv, src, ACT.Copy).then_inc(cnt_ps_free, 1)

            def take_transposed(b, s):
                for tile in range(2):
                    act.wait_ge(tp_ps, b * 2 * NS + 2 * s + tile + 1)
                    act.activation(counts_t[tile][:, s * HS * P:(s + 1) * HS * P],
                                   psum[:, 4 + tile, :].bitcast(bf16)[:, 0:HS * P], ACT.Copy).then_inc(tp_ps_free, 1)

            for g in range(NCG):
                take_counts(0, 0, g)
            for s in range(NS):
                take_transposed(0, s)
            for g in range(NCG):
                take_counts(1, 1, g)

            def body(b, par, has_next, has_next2, tiles):
                for s in range(NS):
                    if has_next:
                        take_transposed(b + 1, s)
                    if has_next2:
                        for g in groups_of(s):
                            take_counts(b + 2, par, g)
            rounds(act, body)

            act.wait_ge(var2_ready, 1)
            act.activation(rstd[:, :], mean_var[:, :, 1], ACT.Sqrt, bias=eps_ln[:, :]).then_inc(std2_ready, 1)
            act.drain().then_inc(phase2_done, 1)
            act.wait_ge(phase2_done, 5)
            for l in range(LAYERS + 1):
                act.wait_ge(w_in[l % 2], 16 * (l // 2 + 1))
                act.activation(w_split[l][0][:, :, :, :], w_stage[l % 2][:, :, :, :], ACT.Copy).then_inc(w_hi, 1)
            act.wait_ge(w_ready, LAYERS + 1)

            def prep_rows(ch):
                c, par, n, t0 = ch
                for k in range(KC):
                    act.wait_ge(xt2_ps, c * KC + k + 1)
                    act.activation(xt2[par][0][:, k, 0:n * P], psum[:, 6 + k, 0:n * P], ACT.Copy).then_inc(xt2_hi, 1)

            def prep_exp(ch):
                c, par, n, t0 = ch
                act.wait_ge(route_shifted, c + 1)
                act.activation(expert_w[par][:, 0:n, :], logits[:, 0:n, :], ACT.Exp).then_inc(route_exp, 1)

            def prep_wt(ch):
                c, par, n, t0 = ch
                act.wait_ge(route_tp, c + 1)
                act.activation(expert_wt[:, 0:n * P], psum[0:N_EXP, 7, 0:n * P], ACT.Copy).then_inc(route_t_ready, 1)

            def relu(layer, ch, e):
                c, par, n, t0 = ch
                q = c * N_EXP + e
                h = h1[e % 2] if layer == 0 else h2
                for m in range(KC):
                    col = e * KC + m
                    scale, shift = bn_cols[:, 2 * layer, col:col + 1], bn_cols[:, 2 * layer + 1, col:col + 1]
                    act.wait_ge(layer_ps[layer], q * KC + m + 1)
                    act.wait_ge(h_ready[layer], q * KC + m + 1)
                    act.activation(relu_out[layer][m][:, 0:n * P], psum[:, 2 * layer + m, 0:n * P], ACT.Relu,
                                   bias=shift, scale=scale)
                    act.activation(h[0][:, m, 0:n * P], psum[:, 2 * layer + m, 0:n * P], ACT.Relu,
                                   bias=shift, scale=scale).then_inc(layer_read[layer], 1)

            first = chunk(0, 0)
            prep_rows(first)
            prep_exp(first)
            prep_wt(first)
            relu(0, first, 0)

            def step(prev, cur, nxt, e):
                if e + 1 < N_EXP:
                    relu(0, cur, e + 1)
                elif nxt is not None:
                    relu(0, nxt, 0)
                relu(1, cur, e)
                if nxt is not None:
                    if e == 1:
                        prep_rows(nxt)
                    if e == 3:
                        prep_exp(nxt)
                    if e == 4:
                        prep_wt(nxt)
            chunks(act, step)

        @block.tensor
        def _(pe):
            pe.wait_ge(consts_ready, 9)
            pe.wait_ge(samp_f_ready, 1)
            pe.matmul(psum[:, 7, 0:NBLK], ones_row[:, :], samp_f[:, :], start=True, stop=True).then_inc(samp_bc, 1)

            pe.wait_ge(bn_row_ready, 1)
            pe.wait_ge(bn_ready, 1)
            for k in range(2 * LAYERS):
                w = N_EXP * KC
                last = pe.transpose(psum[:, 7, k * w:(k + 1) * w], bn_tmp[:, k, :], ident[0:w, 0:w])
            last.then_inc(bn_tp, 1)

            def gate_pe(b, par):
                pe.wait_ge(xn_ready, b + 1)
                if True:
                    pe.wait_ge(xt_ready, 4 * b + 4)
                for k in range(KC):
                    for j in range(GT):
                        last = pe.transpose(psum[:, 2 * k + j // 4, (j % 4) * P:(j % 4 + 1) * P],
                                            xn[par][:, j, k * P:(k + 1) * P], ident[:, :])
                last.then_inc(xt_ps, 1)
                pe.wait_ge(xt_ready, 4 * b + 8)
                pe.wait_ge(hid_ready, 2 * b + 2)
                for q in range(2):
                    lo, n = 512 * q, (512, GT * P - 512)[q]
                    for k in range(KC):
                        last = pe.matmul(psum[:, 4 + q, 0:n], w1_sb[:, k, :], xt[:, k, lo:lo + n],
                                         start=(k == 0), stop=(k == KC - 1))
                last.then_inc(hid_ps, 1)
                pe.wait_ge(hid_ready, 2 * b + 4)
                pe.wait_ge(gate_ready, b + 1)
                for j in range(GT):
                    last = pe.matmul(psum[:, 6, j:j + 1], hid[:, j * P:(j + 1) * P], w2_sb[:, :], start=True, stop=True)
                last.then_inc(logit_ps, 1)
            pe.sem_inc(xt_ready, 4)
            pe.sem_inc(hid_ready, 2)
            pe.sem_inc(gate_ready, 1)
            pe.wait_ge(gate_w_in, 64)
            with pe.Fori(0, NG // 2) as i:
                for par in range(2):
                    gate_pe(2 * i + par, par)
            gate_pe(NG - 1, 0)

            pe.wait_ge(order_ready, 1)
            pe.matmul(psum[:, 7, 0:1], ones_sq[:, :], flags[:, 0:1], start=True, stop=True).then_inc(order_total, 1)
            pe.wait_ge(general_count, 1)
            pe.matmul(psum[:, 7, 8:10], ones_sq[:, :], flags[:, :], start=True, stop=True).then_inc(general_total, 1)
            pe.wait_ge(slots_ready, 1)
            for q in range(-(-NPAIR // 4)):
                n = min(4, NPAIR - 4 * q)
                for m, lst in ((2 * q, hi16), (2 * q + 1, lo16)):
                    if m >= 4:
                        pe.wait_ge(lists_ready, m - 3)
                    for u in range(n):
                        t = 2 * (4 * q + u)
                        last = pe.transpose(psum[:, m % 4, :].bitcast(bf16)[:, u * P:(u + 1) * P],
                                            lst[:, t:t + 2, :].rearrange("p t s -> p (t s)"), ident16[:, :])
                    last.then_inc(lists_tp, 1)
            pe.drain().then_inc(phase1_done, 1)
            pe.wait_ge(phase1_done, 5)
            pe.wait_ge(general_ready, 1)
            with pe.If(pe.value_load(general_i[0:1, 0:1], min_val=0, max_val=1) > 0):
                with pe.Fori(0, SPILL_CH) as k:
                    with pe.Fori(0, NS) as s:
                        pe.wait_ge(sp_picked, k * NS + s + 1)
                        for r in range(HS):
                            last = pe.matmul(psum[:, r, 0:VW], sp_hot[:, :], sp_pick[:, r, :], start=True, stop=True)
                        last.then_inc(sp_ps, 1)
            pe.sem_inc(hot_used, 2)
            pe.sem_inc(v_used, 2)

            def count(b, g):
                pe.wait_ge(hot_lo_ready, b * NCG + g + 1)
                pe.wait_ge(hot_hi_ready, b * NCG + g + 1)
                for c in range(CG):
                    h = c // 8
                    if c % 8 == 0:
                        pe.wait_ge(cnt_ps_free, b * 2 * NCG + 2 * g + h + 1)
                    col = (c % 4) * 2 * NHI
                    last = pe.matmul(psum[:, 2 * h + (c % 8) // 4, col:col + 2 * NHI], hot_lo[g % 2][:, :, c],
                                     hot_hi[g % 2][:, :, c], start=True, stop=True)
                    if c % 8 == 7:
                        last.then_inc(cnt_ps, 1)
                pe.wait_ge(cnt_ps, b * 2 * NCG + 2 * g + 2)
                pe.sem_inc(hot_used, 1)

            def transpose_counts(b, par, s):
                for tile in range(2):
                    pe.wait_ge(tp_ps_free, b * 2 * NS + 2 * s + tile + 1)
                    for r in range(HS):
                        last = pe.transpose(psum[:, 4 + tile, :].bitcast(bf16)[:, r * P:(r + 1) * P],
                                            counts[par][:, tile * NHI + s * HS + r, :], ident16[:, :])
                    last.then_inc(tp_ps, 1)

            def sums(b, par, s, tiles):
                pe.wait_ge(tp_ps_free, b * 2 * NS + 2 * s + 4)
                if s == 0:
                    pe.wait_ge(v_in[par], 16 * ((b - par) // 2 + 1) if isinstance(b, int) else v_value(b, par))
                for r in range(HS):
                    hi = s * HS + r
                    bank = 6 + (par + hi) % 2
                    pe.wait_ge(sum_ps_free, b * NT + hi + 1)
                    for tile in range(tiles):
                        for half in range(2):
                            last = pe.matmul(psum[:, bank, 0:VW], counts_t[tile][:, hi * P:(hi + 1) * P],
                                             vring[par][:, tile, half * VW:(half + 1) * VW],
                                             start=(tile == 0 and half == 0), stop=(tile == tiles - 1 and half == 1))
                    last.then_inc(sum_ps, 1)

            def v_value(b, par):
                return (b - par) * 8 + 16

            for g in range(NCG):
                count(0, g)
            pe.wait_ge(cnt_ps_free, 2 * NCG + 2)
            for s in range(NS):
                transpose_counts(0, 0, s)
            for g in range(NCG):
                count(1, g)

            def body(b, par, has_next, has_next2, tiles):
                for s in range(NS):
                    sums(b, par, s, tiles)
                    if has_next:
                        if s == 0:
                            pe.wait_ge(cnt_ps_free, (b + 2) * 2 * NCG + 2)
                        transpose_counts(b + 1, 1 - par, s)
                    if has_next2:
                        for g in groups_of(s):
                            count(b + 2, g)
                pe.wait_ge(sum_ps, (b + 1) * NT)
                pe.sem_inc(v_used, 1)
            rounds(pe, body)

            pe.drain().then_inc(phase2_done, 1)
            pe.wait_ge(phase2_done, 5)
            for l in range(LAYERS):
                pe.sem_inc(layer_read[l], KC)
            pe.sem_inc(y_read, 2)
            pe.sem_inc(bias_read, 2)
            pe.wait_ge(w_ready, LAYERS + 1)
            TERMS = ((0, 0), (0, 1), (1, 0))

            def prep_tp(ch):
                c, par, n, t0 = ch
                pe.wait_ge(xn2_ready, c + 1)
                pe.wait_ge(bias_read, 2 * c + 2)
                for k in range(KC):
                    for j in range(n):
                        last = pe.transpose(psum[:, 6 + k, j * P:(j + 1) * P], xn2[:, j, k * P:(k + 1) * P], ident[:, :])
                    last.then_inc(xt2_ps, 1)

            def prep_route(ch):
                c, par, n, t0 = ch
                pe.wait_ge(xt2_ready, c * KC + KC)
                for j in range(n):
                    for i, (a, w) in enumerate(TERMS):
                        for k in range(KC):
                            last = pe.matmul(psum[:, 6, j * N_EXP:(j + 1) * N_EXP], xt2[par][a][:, k, j * P:(j + 1) * P],
                                             wr_split[w][:, k, :], start=(i == 0 and k == 0),
                                             stop=(i == len(TERMS) - 1 and k == KC - 1))
                last.then_inc(route_ps, 1)

            def prep_wt(ch):
                c, par, n, t0 = ch
                pe.wait_ge(route_ready, c + 1)
                for j in range(n):
                    last = pe.transpose(psum[0:N_EXP, 7, j * P:(j + 1) * P], expert_w[par][:, j, :], ident[:, :])
                last.then_inc(route_tp, 1)

            def prep_bias(ch):
                c, par, n, t0 = ch
                pe.wait_ge(route_t_ready, c + 1)
                for j in range(n):
                    last = pe.matmul(psum[:, 6 + j // 2, (j % 2) * D:(j % 2 + 1) * D], expert_wt[:, j * P:(j + 1) * P],
                                     bo_sb[:, :], start=True, stop=True)
                last.then_inc(bias_ps, 1)

            def layer(l, ch, e):
                c, par, n, t0 = ch
                q = c * N_EXP + e
                src = xt2[par] if l == 0 else h1[e % 2]
                if l == 0:
                    pe.wait_ge(xt2_ready, c * KC + KC)
                else:
                    pe.wait_ge(h_ready[0], q * KC + 2 * KC)
                for m in range(KC):
                    pe.wait_ge(layer_read[l], q * KC + m + 1)
                    for i, (a, w) in enumerate(TERMS):
                        for k in range(KC):
                            last = pe.matmul(psum[:, 2 * l + m, 0:n * P], w_split[l][w][:, e, k, m * P:(m + 1) * P],
                                             src[a][:, k, 0:n * P], start=(i == 0 and k == 0),
                                             stop=(i == len(TERMS) - 1 and k == KC - 1))
                    last.then_inc(layer_ps[l], 1)

            def layer3(ch, e):
                c, par, n, t0 = ch
                q = c * N_EXP + e
                pe.wait_ge(h_ready[1], q * KC + 2 * KC)
                for j in range(n):
                    if j % 2 == 0:
                        pe.wait_ge(y_read, 2 * q + j // 2 + 1)
                    for i, (a, w) in enumerate(TERMS):
                        for k in range(KC):
                            last = pe.matmul(psum[:, 4 + j // 2, (j % 2) * D:(j % 2 + 1) * D], h2[a][:, k, j * P:(j + 1) * P],
                                             w_split[2][w][:, e, k, :], start=(i == 0 and k == 0),
                                             stop=(i == len(TERMS) - 1 and k == KC - 1))
                    if j % 2 == 1 or j == n - 1:
                        last.then_inc(y_ps, 1)

            first = chunk(0, 0)
            prep_tp(first)
            prep_route(first)
            prep_wt(first)
            prep_bias(first)
            layer(0, first, 0)

            def step(prev, cur, nxt, e):
                if e + 1 < N_EXP:
                    layer(0, cur, e + 1)
                elif nxt is not None:
                    layer(0, nxt, 0)
                if e > 0:
                    layer3(cur, e - 1)
                elif prev is not None:
                    layer3(prev, N_EXP - 1)
                layer(1, cur, e)
                if nxt is not None:
                    if e == 1:
                        prep_tp(nxt)
                    if e == 2:
                        prep_route(nxt)
                    if e == 4:
                        prep_wt(nxt)
                    if e == 5:
                        prep_bias(nxt)
            chunks(pe, step)
            layer3(chunk(N_CHUNK - 1, (N_CHUNK - 1) % 2), N_EXP - 1)

        @block.vector
        def _(dve):
            n = [0]

            def after(ins):
                n[0] += 1
                ins.then_inc(chain, 1)

            def settle():
                dve.wait_ge(chain, n[0])

            dve.wait_ge(samp_in, 16)
            dve.tensor_copy(samp_f[:, :], samp_i[:, :]).then_inc(samp_f_ready, 1)
            after(dve.memset(vf[:, :, :], 0.0))
            dve.wait_ge(samp_bc, 1)
            after(dve.tensor_copy(samp[:, :], psum[:, 7, 0:NBLK]))
            dve.wait_ge(consts_ready, 9)
            settle()
            dve.sem_inc(bn_ready, 1)
            dve.wait_ge(bn_std, LAYERS + 1)
            for l in range(LAYERS):
                g, bb, m, be = (bn_rows[:, 5 * l + k, :] for k in range(4))
                scale, shift = bn_tmp[:, 2 * l, :], bn_tmp[:, 2 * l + 1, :]
                after(dve.reciprocal(scale, scale))
                after(dve.tensor_tensor(shift, bb, m, ALU.subtract))
                settle()
                after(dve.tensor_tensor(scale, scale, g, ALU.mult))
                settle()
                after(dve.tensor_tensor(shift, shift, scale, ALU.mult))
                settle()
                after(dve.tensor_tensor(shift, shift, be, ALU.add))
                settle()
            dve.sem_inc(bn_row_ready, 1)
            after(dve.tensor_tensor(wr_split[1][:, :, :], wr_sb[:, :, :], wr_split[0][:, :, :].bitcast(f32), ALU.subtract))
            for t in range(NT2):
                after(dve.tensor_scalar(less[:, 0:NBLK], samp[:, :], node_id[:, t:t + 1], None, ALU.is_lt, ALU.add,
                                        accum_out=n_blocks[:, t:t + 1]))
                settle()
            after(dve.tensor_scalar(block_f[:, :], n_blocks[:, :], -1.0, 0.0, ALU.add, ALU.max))
            settle()
            after(dve.tensor_scalar(block_f[:, :], block_f[:, :], float(BLK), None, ALU.mult))
            settle()
            dve.tensor_scalar(block_i[:, :], block_f[:, :], float(FRONT), None, ALU.add).then_inc(block_ready, 1)

            dve.wait_ge(x_in, 16 * NG)
            for t in range(NT):
                after(dve.bn_stats(stats[:, t, :], x_sb[:, t, :]))
            settle()
            for t in range(NT):
                last = dve.bn_aggr(mean_var[:, t, :], stats[:, t, :])
            last.then_inc(var_ready, 1)
            dve.wait_ge(std_ready, 1)
            after(dve.reciprocal(rstd[:, :], rstd[:, :]))
            settle()

            def normalise(b, par):
                for j in range(GT):
                    last = dve.tensor_scalar(xn[par][:, j, :], x_sb[:, b * GT + j, :], mean_var[:, b * GT + j, 0:1],
                                             rstd[:, b * GT + j:b * GT + j + 1], ALU.subtract, ALU.mult)
                last.then_inc(xn_ready, 1)

            def weigh(b, par):
                dve.wait_ge(gate_ready, b + 2)
                for j in range(GT):
                    after(dve.tensor_scalar(vf[:, j, 0:D], xn[par][:, j, :], gate[:, b * GT + j:b * GT + j + 1], None, ALU.mult))
                after(dve.tensor_copy(vf[:, :, D], gate[:, b * GT:(b + 1) * GT]))
                settle()
                if b >= 2:
                    dve.wait_ge(vs_out[par], 16 * (b // 2))
                after(dve.tensor_copy(vs[par][:, :, 0, :], vf[:, :, :]))
                settle()
                dve.tensor_tensor(vs[par][:, :, 1, :], vf[:, :, :], vs[par][:, :, 0, :].bitcast(f32), ALU.subtract).then_inc(vs_ready, 1)

            normalise(0, 0)
            for b in range(NG):
                if b + 1 < NG:
                    normalise(b + 1, (b + 1) % 2)
                weigh(b, b % 2)
                dve.wait_ge(vs_ready, b + 1)

            dve.sem_inc(blk_counted, 1)
            for g in range(NSG):
                dve.wait_ge(blk_conv, g + 3)
                for j in range(SG):
                    t = g * SG + j
                    after(dve.tensor_scalar(less[:, :], blk_f[:, j, :], node_id[:, t:t + 1], None, ALU.is_lt, ALU.add,
                                            accum_out=n_less[:, t:t + 1]))
                    settle()
                dve.sem_inc(blk_counted, 1)
            after(dve.tensor_tensor(row_f[:, :], block_f[:, :], n_less[:, :], ALU.add))
            settle()
            dve.tensor_copy(row_i[:, :], row_f[:, :]).then_inc(row_ready, 1)

            after(dve.memset(flags[:, :], 0.0))
            dve.wait_ge(order_in, 32)
            after(dve.tensor_tensor(order_f, order_i[:, 0:SORT_N], order_i[:, 1:SORT_N + 1], ALU.is_gt))
            settle()
            dve.tensor_reduce(out=flags[0:SORT_P, 0:1], in_=order_f, axis=AX.X, op=ALU.max).then_inc(order_ready, 1)
            dve.wait_ge(order_total, 1)
            after(dve.tensor_scalar(unsorted[:, :], psum[:, 7, 0:1], 1.0, None, ALU.min))
            settle()
            after(dve.scalar_tensor_tensor(out=node_cmp[:, :], in0=node_id[:, :], scalar=1.0, in1=unsorted[:, :].broadcast_to([P, NT2]),
                                           op0=ALU.add, op1=ALU.mult))
            settle()
            after(dve.tensor_tensor(node_cmp[:, :], node_id[:, :], node_cmp[:, :], ALU.subtract))
            dve.wait_ge(win_in, 16 * NT2)
            dve.wait_ge(vs_out[0], 16 * (NG // 2 + 1))
            dve.wait_ge(vs_out[1], 16 * (NG // 2))
            wv = win[:, :, :].rearrange("p t (s two) -> p t s two", two=2)
            after(dve.tensor_copy(slot_dst[:, :, :], wv[:, :, :, 0]))
            after(dve.tensor_scalar(slot_hi[:, :, :], wv[:, :, 0:SLOT, 1], 7, None, ALU.arith_shift_right))
            after(dve.tensor_scalar(slot_lo[:, :, :], wv[:, :, 0:SLOT, 1], P - 1, None, ALU.bitwise_and))
            settle()
            after(dve.tensor_tensor(slot_ok[:, :, :], slot_dst[:, :, :], node_cmp[:, :].unsqueeze(2).broadcast_to([P, NT2, WIN]), ALU.is_equal))
            after(dve.tensor_copy(lo16[:, :, :], slot_lo[:, :, :]))
            settle()
            after(dve.scalar_tensor_tensor(out=hi16[:, :, :], in0=slot_hi[:, :, :], scalar=-float(NONE_HI),
                                           in1=slot_ok[:, :, 0:SLOT], op0=ALU.add, op1=ALU.mult))
            settle()
            dve.tensor_reduce(out=flags[:, 1:2], in_=slot_ok[:, :, SLOT], axis=AX.X, op=ALU.max).then_inc(general_count, 1)
            dve.sem_inc(slots_ready, 1)
            dve.wait_ge(general_total, 1)
            after(dve.tensor_tensor(general[:, :], psum[:, 7, 9:10], unsorted[:, :], ALU.add))
            settle()
            after(dve.tensor_scalar(general[:, :], general[:, :], 1.0, None, ALU.min))
            settle()
            dve.tensor_copy(general_i[:, :], general[:, :]).then_inc(general_ready, 1)
            dve.drain().then_inc(phase1_done, 1)
            dve.wait_ge(phase1_done, 5)
            dve.wait_ge(general_ready, 1)
            dve.sem_inc(sum_ps_free, 2)

            with dve.If(dve.value_load(general_i[0:1, 0:1], min_val=0, max_val=1) > 0):
                dve.memset(acc[:, :, :], 0.0).then_inc(sp_chain, 1)
                dve.wait_ge(sp_chain, 1)
                dve.wait_ge(sp_iota_ready, 2)
                dve.sem_inc(sp_chunk_done, 1)
                with dve.Fori(0, SPILL_CH) as k:
                    dve.wait_ge(sp_edge_in, 16 * k + 16)
                    dve.wait_ge(sp_prev_in, 16 * k + 16)
                    DST, PREV, LO, HI, TAKE, REAL, CLIP, SAME = (sp_f[:, c:c + 1] for c in range(8))
                    CHAIN = 4
                    dve.tensor_copy(DST, sp_edge[:, 0:1])
                    dve.tensor_copy(PREV, sp_prev[:, :])
                    dve.tensor_scalar(sp_int[:, 1:2], sp_edge[:, 1:2], 7, None, ALU.arith_shift_right)
                    dve.tensor_scalar(sp_int[:, 2:3], sp_edge[:, 1:2], P - 1, None, ALU.bitwise_and).then_inc(sp_chain, 1)
                    dve.wait_ge(sp_chain, CHAIN * k + 2)
                    dve.tensor_scalar(CLIP, DST, float(N_NODES - 1), None, ALU.min)
                    dve.tensor_tensor(SAME, DST, PREV, ALU.is_equal)
                    dve.tensor_scalar(REAL, DST, float(DST_PAD), None, ALU.is_lt)
                    dve.tensor_copy(HI, sp_int[:, 1:2])
                    dve.tensor_copy(LO, sp_int[:, 2:3]).then_inc(sp_chain, 1)
                    dve.wait_ge(sp_chain, CHAIN * k + 3)
                    dve.tensor_copy(sp_int[:, 0:1], CLIP).then_inc(sp_index, 1)
                    dve.scalar_tensor_tensor(out=TAKE, in0=SAME, scalar=unsorted[:, :], in1=REAL, op0=ALU.max, op1=ALU.mult).then_inc(sp_chain, 1)
                    dve.wait_ge(sp_chain, CHAIN * k + 4)
                    dve.wait_ge(sp_rows_in, 16 * k + 16)
                    dve.tensor_tensor(sp_val[:, :], sp_rows[:, 0:VW], sp_rows[:, VW:2 * VW], ALU.add).then_inc(sp_chain, 1)
                    dve.wait_ge(sp_chain, CHAIN * k + 5)
                    dve.tensor_scalar(sp_hot[:, :], sp_iota[:, :], LO, TAKE, ALU.is_equal, ALU.mult)
                    with dve.Fori(0, NS) as s:
                        for r in range(HS):
                            last = dve.scalar_tensor_tensor(out=sp_pick[:, r, :], in0=sp_iota[:, bass.ds(s * HS + r, 1)].broadcast_to([P, VW]),
                                                            scalar=HI, in1=sp_val[:, :], op0=ALU.is_equal, op1=ALU.mult)
                        last.then_inc(sp_picked, 1)
                        dve.wait_ge(sp_ps, k * NS + s + 1)
                        rows = acc[:, bass.ds(s * HS, HS), :]
                        dve.tensor_tensor(rows, rows, psum[:, 0:HS, 0:VW], ALU.add).then_inc(sp_added, 1)
                        dve.wait_ge(sp_added, k * NS + s + 1)
                    dve.sem_inc(sp_chunk_done, 1)
            dve.wait_ge(iota16_ready, 2)

            def hot(b, g):
                dve.wait_ge(hot_used, b * NCG + g + 1)
                dve.tensor_tensor(hot_lo[g % 2][:, :, :],
                                  lo_list[:, bass.ds(b, 1), g * CG:(g + 1) * CG].broadcast_to([P, P, CG]),
                                  iota_lo[:, :, :], ALU.is_equal).then_inc(hot_lo_ready, 1)
                dve.tensor_tensor(hot_hi[g % 2][:, :, :],
                                  hi_list[:, bass.ds(b, 1), g * CG:(g + 1) * CG].broadcast_to([P, 2 * NHI, CG]),
                                  iota_hi[:, :, :], ALU.is_equal).then_inc(hot_hi_ready, 1)

            def take_sum(b, par, hi):
                dve.wait_ge(sum_ps, b * NT + hi + 1)
                dve.tensor_tensor(acc[:, hi, :], acc[:, hi, :], psum[:, 6 + (par + hi) % 2, 0:VW], ALU.add).then_inc(sum_ps_free, 1)

            for b in range(2):
                for g in range(NCG):
                    hot(b, g)
                    if b == 0 and g == 1:
                        with dve.If(dve.value_load(general_i[0:1, 0:1], min_val=0, max_val=1) < 1):
                            dve.memset(acc[:, :, :], 0.0)
                        dve.drain().then_inc(acc_zero, 1)
            dve.wait_ge(acc_zero, 1)

            def residual(s):
                t0 = s * HS
                dve.wait_ge(sum_ps_free, (NPAIR - 1) * NT + t0 + HS + 2)
                after(dve.tensor_scalar(den[:, 0, :], acc[:, t0:t0 + HS, D], 1e-12, None, ALU.max))
                after(dve.tensor_scalar(den[:, 1, :], acc[:, t0:t0 + HS, D], 0.0, None, ALU.is_gt))
                settle()
                after(dve.reciprocal(den[:, 2, :], den[:, 0, :]))
                settle()
                after(dve.tensor_tensor(den[:, 0, :], den[:, 2, :], den[:, 1, :], ALU.mult))
                settle()
                dve.wait_ge(x_again_in[s % 2], 16 * (s // 2 + 1))
                for r in range(HS):
                    last = dve.scalar_tensor_tensor(out=acc[:, t0 + r, 0:D], in0=acc[:, t0 + r, 0:D], scalar=den[:, 0, r:r + 1],
                                                    in1=x_again[s % 2][:, r, :], op0=ALU.mult, op1=ALU.add)
                last.then_inc(x_again_used, 1)
                dve.wait_ge(x_again_used, s + 1)
                for r in range(HS):
                    after(dve.bn_stats(stats[:, t0 + r, :], acc[:, t0 + r, 0:D]))
                settle()
                for r in range(HS):
                    last = dve.bn_aggr(mean_var[:, t0 + r, :], stats[:, t0 + r, :])
                after(last)
                settle()

            def body(b, par, has_next, has_next2, tiles):
                for s in range(NS):
                    if has_next2:
                        for g in groups_of(s):
                            hot(b + 2, g)
                    for r in range(HS):
                        take_sum(b, par, s * HS + r)
                    if not has_next:
                        residual(s)
            rounds(dve, body)

            dve.sem_inc(var2_ready, 1)
            dve.wait_ge(std2_ready, 1)
            after(dve.reciprocal(rstd[:, :], rstd[:, :]))
            settle()
            dve.drain().then_inc(phase2_done, 1)
            dve.wait_ge(phase2_done, 5)
            for l in range(LAYERS + 1):
                dve.wait_ge(w_hi, l + 1)
                dve.tensor_tensor(w_split[l][1][:, :, :, :], w_stage[l % 2][:, :, :, :], w_split[l][0][:, :, :, :].bitcast(f32),
                                  ALU.subtract).then_inc(w_ready, 1)
            dve.wait_ge(w_ready, LAYERS + 1)
            for l in range(LAYERS):
                dve.sem_inc(h_ready[l], KC)

            def prep_norm(ch):
                c, par, n, t0 = ch
                if not (isinstance(c, int) and c == 0):
                    dve.wait_ge(xt2_ps, c * KC)
                for j in range(n):
                    last = dve.tensor_scalar(xn2[:, j, :], acc[:, bass.ds(t0 + j, 1), 0:D], mean_var[:, bass.ds(t0 + j, 1), 0],
                                             rstd[:, bass.ds(t0 + j, 1)], ALU.subtract, ALU.mult)
                last.then_inc(xn2_ready, 1)

            def prep_rest(ch):
                c, par, n, t0 = ch
                for k in range(KC):
                    dve.wait_ge(xt2_hi, c * KC + k + 1)
                    dve.tensor_tensor(xt2[par][1][:, k, 0:n * P], psum[:, 6 + k, 0:n * P], xt2[par][0][:, k, 0:n * P].bitcast(f32),
                                      ALU.subtract).then_inc(xt2_ready, 1)

            def prep_softmax(ch):
                c, par, n, t0 = ch
                dve.wait_ge(route_ps, c + 1)
                dve.tensor_tensor(logits[:, 0:n, :], psum[:, 6, 0:n * N_EXP].rearrange("p (t e) -> p t e", e=N_EXP),
                                  br_sb[:, :].unsqueeze(1).broadcast_to([P, n, N_EXP]), ALU.add).then_inc(soft, 1)
                dve.wait_ge(soft, 4 * c + 1)
                dve.tensor_reduce(out=top[:, 0:n], in_=logits[:, 0:n, :], axis=AX.X, op=ALU.max).then_inc(soft, 1)
                dve.wait_ge(soft, 4 * c + 2)
                dve.tensor_tensor(logits[:, 0:n, :], logits[:, 0:n, :], top[:, 0:n].unsqueeze(2).broadcast_to([P, n, N_EXP]),
                                  ALU.subtract).then_inc(route_shifted, 1)

            def prep_weights(ch):
                c, par, n, t0 = ch
                dve.wait_ge(route_exp, c + 1)
                dve.tensor_reduce(out=top[:, 0:n], in_=expert_w[par][:, 0:n, :], axis=AX.X, op=ALU.add).then_inc(soft, 1)
                dve.wait_ge(soft, 4 * c + 3)
                dve.reciprocal(top[:, 0:n], top[:, 0:n]).then_inc(soft, 1)
                dve.wait_ge(soft, 4 * c + 4)
                dve.tensor_tensor(expert_w[par][:, 0:n, :], expert_w[par][:, 0:n, :],
                                  top[:, 0:n].unsqueeze(2).broadcast_to([P, n, N_EXP]), ALU.mult).then_inc(route_ready, 1)

            def prep_bias(ch):
                c, par, n, t0 = ch
                dve.wait_ge(bias_ps, c + 1)
                for b in range(2):
                    m = min(2, n - 2 * b)
                    rows = acc[:, bass.ds(t0 + 2 * b, m), 0:D]
                    dve.tensor_tensor(rows, rows, psum[:, 6 + b, 0:m * D].rearrange("p (t d) -> p t d", d=D), ALU.add).then_inc(bias_read, 1)

            def rest(l, ch, e):
                c, par, n, t0 = ch
                q = c * N_EXP + e
                h = h1[e % 2] if l == 0 else h2
                for m in range(KC):
                    dve.wait_ge(layer_read[l], q * KC + m + 1 + KC)
                    dve.tensor_tensor(h[1][:, m, 0:n * P], relu_out[l][m][:, 0:n * P], h[0][:, m, 0:n * P].bitcast(f32),
                                      ALU.subtract).then_inc(h_ready[l], 1)

            def take_y(ch, e):
                c, par, n, t0 = ch
                q = c * N_EXP + e
                for j in range(n):
                    if j % 2 == 0:
                        dve.wait_ge(y_ps, 2 * q + j // 2 + 1)
                    row = acc[:, bass.ds(t0 + j, 1), 0:D]
                    last = dve.scalar_tensor_tensor(out=row, in0=psum[:, 4 + j // 2, (j % 2) * D:(j % 2 + 1) * D].unsqueeze(1),
                                                    scalar=expert_w[par][:, j, e:e + 1], in1=row, op0=ALU.mult, op1=ALU.add)
                    if j % 2 == 1 or j == n - 1:
                        last.then_inc(y_read, 1)
                if e == N_EXP - 1:
                    dve.wait_ge(y_read, 2 * q + 4)
                    dve.sem_inc(rows_ready, 1)

            first = chunk(0, 0)
            prep_norm(first)
            prep_rest(first)
            prep_softmax(first)
            prep_weights(first)
            prep_bias(first)
            dve.wait_ge(bias_read, 4)
            rest(0, first, 0)

            def step(prev, cur, nxt, e):
                if e + 1 < N_EXP:
                    rest(0, cur, e + 1)
                elif nxt is not None:
                    rest(0, nxt, 0)
                if e > 0:
                    take_y(cur, e - 1)
                elif prev is not None:
                    take_y(prev, N_EXP - 1)
                rest(1, cur, e)
                if nxt is not None:
                    if e == 0:
                        prep_norm(nxt)
                    if e == 1:
                        prep_rest(nxt)
                    if e == 2:
                        prep_softmax(nxt)
                    if e == 3:
                        prep_weights(nxt)
                    if e == 5:
                        prep_bias(nxt)
            chunks(dve, step)
            take_y(chunk(N_CHUNK - 1, (N_CHUNK - 1) % 2), N_EXP - 1)


_INS = ['x', 'dst', 'edges', 'L0_gnn_W1', 'L0_gnn_b1', 'L0_gnn_W2', 'L0_gnn_b2', 'L0_ffn_Wr', 'L0_ffn_br', 'L0_ffn_W1',
        'L0_ffn_b1', 'L0_ffn_g1', 'L0_ffn_be1', 'L0_ffn_m1', 'L0_ffn_v1', 'L0_ffn_W2', 'L0_ffn_b2', 'L0_ffn_g2',
        'L0_ffn_be2', 'L0_ffn_m2', 'L0_ffn_v2', 'L0_ffn_Wo', 'L0_ffn_bo']


def kernel(**inputs):
    import numpy as np
    import concourse.bacc as bacc
    from concourse.bass_utils import run_bass_kernel_spmd

    nc = bacc.Bacc("TRN2", target_bir_lowering=False, num_devices=1)
    laid = {n: np.ascontiguousarray(a) for n, a in inputs.items() if n not in ("src", "dst")}
    laid["x"] = np.zeros((NT * P, D), inputs["x"].dtype)
    laid["x"][:N_NODES] = inputs["x"]
    laid["edges"] = np.full((E_PAD, 2), DST_PAD, inputs["dst"].dtype)
    laid["edges"][:N_EDGES, 0] = inputs["dst"]
    laid["edges"][:N_EDGES, 1] = inputs["src"]
    laid["dst"] = np.full((DST_ROWS, 1), DST_PAD, inputs["dst"].dtype)
    laid["dst"][:FRONT] = -1
    laid["dst"][FRONT:FRONT + N_EDGES, 0] = inputs["dst"]
    arrays, args = {}, []
    for name in _INS:
        a = laid[name]
        arrays[f"in_{name}_dram"] = a
        args.append(nc.dram_tensor(f"in_{name}_dram", a.shape, mybir.dt.from_np(a.dtype), kind="ExternalInput").ap())
    args.append(nc.dram_tensor("out_0_dram", (NT * P, D), mybir.dt.float32, kind="ExternalOutput").ap())
    args.append(nc.dram_tensor("values_scratch", (NT * P, 2 * VW), mybir.dt.float32).ap())
    program(nc, *args)
    r = run_bass_kernel_spmd(nc, [arrays], core_ids=[0])
    return r.results[0]["out_0_dram"][:N_NODES]
```

```python
import concourse.bass as bass
from concourse import mybir
from contextlib import ExitStack

P = 128
N_NODES = 6250
N_EDGES = 200000
D = 256
HID = 128
N_EXP = 8
KC = D // P
NT = -(-N_NODES // P)
NPAIR = (NT + 1) // 2
NT2 = 2 * NPAIR
SLOT = 64
WIN = SLOT + 1
BLK = 512
NBLK = -(-N_EDGES // BLK)
E_PAD = (NBLK + 1) * BLK
FRONT = SLOT
SORT_P = 125
SORT_N = N_EDGES // SORT_P
DST_ROWS = FRONT + E_PAD + SORT_N
SPILL_CH = -(-N_EDGES // P)
DST_PAD = 16384
GT = 7
NG = NT // GT
VW = D + 2
SG = 5
NSG = NT2 // SG
LG = 10
NLG = NT2 // LG
NHI = NT
NONE_HI = 127
VROW = 2 * VW + 2
VSCALE = 1024.0
CG = 16
NCG = P // CG
RING = 4
LEAD = 2
HOT_OPS = 4
UC = 4
NU = P // UC
HS = 7
NS = NHI // HS
SLOTS_OF = ((0, 2), (2, 2), (4, 2), (6, 1))
NSL = len(SLOTS_OF)
SPR = NS * NSL
EXP_BITS = 0x7F800000
LN_EPS = 1e-5
BN_EPS = 1e-3
CH = 4
N_SHORT = -NT % CH
N_CHUNK = -(-NT // CH)
LAYERS = 2
N_PART = 2 * (LAYERS + 1)
STAGES = 3
LAST_ORDER = (("sum", 0), ("rows", 0), ("norm", 0), ("sum", 1), ("sum", 2), ("rows", 1), ("first", 0), ("sum", 3),
              ("sum", 4), ("rows", 2), ("sum", 5), ("sum", 6), ("rows", 3), ("rows", 4), ("rows", 5), ("rows", 6))
NORM_AT = {(0, 4): 1, (0, 5): 2, (1, 2): 3, (1, 4): 4, (1, 6): 5, (2, 2): 6}
NORM_END = {(0, 6): (1, 2), (2, 4): (3, 6)}


def program(nc, x, dst, edges, g_w1, g_b1, g_w2, g_b2, f_wr, f_br, f_w1, f_b1, f_g1, f_be1, f_m1, f_v1,
            f_w2, f_b2, f_g2, f_be2, f_m2, f_v2, f_wo, f_bo, out, values):
    f32, bf16, f16 = mybir.dt.float32, mybir.dt.bfloat16, mybir.dt.float16
    i32, u16, f32r = mybir.dt.int32, mybir.dt.uint16, mybir.dt.float32r
    ALU, ACT, AX = mybir.AluOpType, mybir.ActivationFunctionType, mybir.AxisListType

    stack = ExitStack()
    with stack:
        def sem(name):
            return stack.enter_context(nc.semaphore(name))

        def sb(where, name, shape, dt):
            return where.enter_context(nc.sbuf_tensor(name, shape, dt))

        ident = sb(stack, "ident", [P, P], f32)
        ident16 = sb(stack, "ident16", [P, P], bf16)
        ones_row = sb(stack, "ones_row", [1, P], f32)
        eps_ln = sb(stack, "eps_ln", [P, 1], f32)
        stats = sb(stack, "stats", [P, NT, 6], f32)
        mean_var = sb(stack, "mean_var", [P, NT, 2], f32)
        rstd = sb(stack, "rstd", [P, NT], f32)
        bn_cols = sb(stack, "bn_cols", [P, 2 * LAYERS, N_EXP * KC], f32)
        wr_sb = sb(stack, "wr_sb", [P, KC, N_EXP], f32)
        wr_split = [sb(stack, f"wr_{n}", [P, KC, N_EXP], f32r) for n in ("hi", "lo")]
        br_sb = sb(stack, "br_sb", [P, N_EXP], f32)
        bo_sb = sb(stack, "bo_sb", [N_EXP, D], f32)
        eps_bn = sb(stack, "eps_bn", [P, 1], f32)
        den = sb(stack, "den", [P, 3, HS], f32)
        logits = sb(stack, "logits", [P, CH, N_EXP], f32)
        top = sb(stack, "top", [P, CH], f32)
        expert_w = [sb(stack, f"expert_w{i}", [P, CH, N_EXP], f32) for i in range(2)]
        ones_sq = sb(stack, "ones_sq", [P, P], f32)
        flags = sb(stack, "flags", [P, 2], f32)
        unsorted = sb(stack, "unsorted", [P, 1], f32)
        general = sb(stack, "general", [P, 1], f32)
        general_i = sb(stack, "general_i", [P, 1], i32)
        gate_p2 = sb(stack, "gate_p2", [P, NT2], f32)
        p2_round = [sb(stack, f"p2_round{i}", [P, 2], f32) for i in range(2)]
        lists = ExitStack()
        hi_list = sb(lists, "hi_list", [P, NPAIR, P], bf16)
        iota_lo = sb(lists, "iota_lo", [P, P, CG], bf16)
        iota_hi = sb(lists, "iota_hi", [P, 2 * NHI, CG], bf16)
        lo_list = sb(lists, "lo_list", [P, NPAIR, P], bf16)
        psum = stack.enter_context(nc.psum_tensor("psum", [P, 8, 512], f32))

        ph1 = ExitStack()
        x_sb = sb(ph1, "x_sb", [P, NT, D], f32)
        xn = [sb(ph1, f"xn{i}", [P, GT, D], f32) for i in range(2)]
        xt = sb(ph1, "xt", [P, KC, GT * P], f32)
        hid = sb(ph1, "hid", [P, GT * P], f32)
        gate = sb(ph1, "gate", [P, NT], f32)
        p2_inv = sb(ph1, "p2_inv", [P, GT], i32)
        gate_m = sb(ph1, "gate_m", [P, GT], f32)
        vf = sb(ph1, "vf", [P, GT, VW], f32)
        vs = [sb(ph1, f"vs{i}", [P, GT, VROW], f16) for i in range(2)]
        w1_sb = sb(ph1, "w1_sb", [P, KC, HID], f32)
        b1_sb = sb(ph1, "b1_sb", [HID, 1], f32)
        w2_sb = sb(ph1, "w2_sb", [HID, 1], f32)
        b2_neg = sb(ph1, "b2_neg", [P, 1], f32)
        b2_sb = sb(ph1, "b2_sb", [P, 1], f32)
        hi_bias = sb(ph1, "hi_bias", [P, 1], f32)
        node_i = sb(ph1, "node_i", [P, NT2], i32)
        node_id = sb(ph1, "node_id", [P, NT2], f32)
        node_cmp = sb(ph1, "node_cmp", [P, NT2], f32)
        less = sb(ph1, "less", [P, 2, BLK], bf16)
        n_blocks = sb(ph1, "n_blocks", [P, NT2], f32)
        block_f = sb(ph1, "block_f", [P, NT2], f32)
        block_i = sb(ph1, "block_i", [P, NT2], i32)
        n_less = sb(ph1, "n_less", [P, NT2], f32)
        row_f = sb(ph1, "row_f", [P, NT2], f32)
        row_i = sb(ph1, "row_i", [P, NT2], i32)
        blk_i = [sb(ph1, f"blk_i{i}", [P, SG, BLK], i32) for i in range(2)]
        slot_ok = sb(ph1, "slot_ok", [P, NT2, WIN], bf16)
        slot_hi = sb(ph1, "slot_hi", [P, LG, SLOT], i32)
        slot_lo = sb(ph1, "slot_lo", [P, LG, SLOT], i32)
        hi16 = sb(ph1, "hi16", [P, NT2, SLOT], bf16)
        lo16 = sb(ph1, "lo16", [P, NT2, SLOT], bf16)
        early = ExitStack()
        bn_rows = sb(early, "bn_rows", [N_EXP * KC, 5 * LAYERS, P], f32)
        bn_tmp = sb(early, "bn_tmp", [N_EXP * KC, 2 * LAYERS, P], f32)
        order_i = sb(early, "order_i", [SORT_P, SORT_N + 1], i32)
        samp_i = sb(early, "samp_i", [1, NBLK], i32)
        samp_f = sb(early, "samp_f", [1, NBLK], f32)
        samp = sb(early, "samp", [P, NBLK], f32)
        order_f = sb(early, "order_f", [SORT_P, SORT_N], bf16)
        early.close()
        win = sb(ph1, "win", [P, NT2, 2 * WIN], i32)
        ph1.close()
        ph2 = ExitStack()
        acc = sb(ph2, "acc", [P, NT, VW], f32)
        counts = [None, None]
        counts_t = [None, None]
        for i in (1, 0):
            counts[i] = sb(ph2, f"counts{i}", [P, 2 * NHI, P], bf16)
        for i in (1, 0):
            counts_t[i] = [sb(ph2, f"counts_t{i}{k}", [P, NHI * P], bf16) for k in range(2)]
        vring = [sb(ph2, f"vring{i}", [P, 2, 2 * VW], f16) for i in range(2)]
        hot_lo = [sb(ph2, f"hot_lo{i}", [P, P, CG], bf16) for i in range(RING)]
        hot_hi = [sb(ph2, f"hot_hi{i}", [P, 2 * NHI, CG], bf16) for i in range(RING)]
        ph2.close()
        ph2s = ExitStack()
        sb(ph2s, "acc_below3", [P, NT, VW], f32)
        sp_edge = sb(ph2s, "sp_edge", [P, 2], i32)
        sp_prev = sb(ph2s, "sp_prev", [P, 1], i32)
        sp_f = sb(ph2s, "sp_f", [P, 10], f32)
        sp_int = sb(ph2s, "sp_int", [P, 4], i32)
        sp_iota_i = sb(ph2s, "sp_iota_i", [P, P], i32)
        sp_iota = sb(ph2s, "sp_iota", [P, P], f32)
        sp_idle = sb(ph2s, "sp_idle", [P, 1], f32)
        sp_hot = sb(ph2s, "sp_hot", [P, P], f32)
        sp_rows = sb(ph2s, "sp_rows", [P, VROW], f16)
        sp_val = sb(ph2s, "sp_val", [P, VW], f32)
        sp_pick = sb(ph2s, "sp_pick", [P, HS, VW], f32)
        ph2s.close()
        lists.close()
        first_rows = ExitStack()
        sb(first_rows, "xn2_below", [P, CH, D], f32)
        x_again = [sb(first_rows, f"x_again{i}", [P, HS, D], f32) for i in range(2)]
        first_rows.close()

        ph3 = ExitStack()
        xn2 = sb(ph3, "xn2", [P, CH, D], f32)
        relu_out = [[sb(ph3, f"relu_out{l}{m}", [P, CH * P], f32) for m in range(KC)] for l in range(LAYERS)]
        expert_wt = sb(ph3, "expert_wt", [N_EXP, CH * P], f32)
        h2_lo = sb(ph3, "h2_lo", [P, KC, CH * P], f32r)
        sb(ph3, "lists_rest", [P, 2 * NPAIR * P + (P + 2 * NHI) * CG - 2 * (CH * D + (LAYERS * KC + 1 + KC) * CH * P)], bf16)
        sb(ph3, "acc_kept", [P, NT, VW], f32)
        w_split = [[sb(ph3, f"w{l}_{n}", [P, N_EXP, KC, D], f32r) for n in ("hi", "lo")] for l in range(LAYERS + 1)]
        xt2, h1 = [None, None], [None, None]
        stage = ExitStack()
        sb(stage, "xt2_below", [P, 2 * KC, CH * P], f32)
        w_stage = [sb(stage, f"w_stage{i}", [P, N_EXP // 2, KC, D], f32) for i in range(STAGES)]
        stage.close()
        for i in range(2):
            xt2[i] = [sb(ph3, f"xt2_{n}{i}", [P, KC, CH * P], f32r) for n in ("hi", "lo")]
            h1[i] = [sb(ph3, f"h1_{n}{i}", [P, KC, CH * P], f32r) for n in ("hi", "lo")]
        h2 = [sb(ph3, "h2_hi", [P, KC, CH * P], f32r), h2_lo]
        ph3.close()

        consts_ready = sem("consts_ready")
        x_in = sem("x_in")
        gate_w_in = sem("gate_w_in")
        samp_in = sem("samp_in")
        chain = sem("chain")
        pool_chain = sem("pool_chain")
        order_in = sem("order_in")
        order_ready = sem("order_ready")
        order_total = sem("order_total")
        general_count = sem("general_count")
        general_total = sem("general_total")
        general_ready = sem("general_ready")
        sp_iota_ready = sem("sp_iota_ready")
        sp_chain = sem("sp_chain")
        sp_edge_in = sem("sp_edge_in")
        sp_prev_in = sem("sp_prev_in")
        sp_index = sem("sp_index")
        sp_rows_in = sem("sp_rows_in")
        sp_idled = sem("sp_idled")
        sp_picked = sem("sp_picked")
        sp_ps = sem("sp_ps")
        sp_added = sem("sp_added")
        sp_chunk_done = sem("sp_chunk_done")
        var_ready = sem("var_ready")
        std_ready = sem("std_ready")
        samp_f_ready = sem("samp_f_ready")
        samp_bc = sem("samp_bc")
        block_ready = sem("block_ready")
        blk_in = [sem(f"blk_in{i}") for i in range(2)]
        blk_counted = sem("blk_counted")
        row_ready = sem("row_ready")
        win_in = [sem(f"win_in{g}") for g in range(NLG)]
        slots_ready = sem("slots_ready")
        lists_tp = sem("lists_tp")
        lists_ready = sem("lists_ready")
        xn_ready = sem("xn_ready")
        xt_ps = sem("xt_ps")
        xt_ready = sem("xt_ready")
        hid_ps = sem("hid_ps")
        hid_ready = sem("hid_ready")
        logit_ps = sem("logit_ps")
        gate_ready = sem("gate_ready")
        vs_ready = sem("vs_ready")
        vs_out = [sem(f"vs_out{i}") for i in range(2)]
        phase1_done = sem("phase1_done")
        iota_ready = sem("iota_ready")
        exp_ready = sem("exp_ready")
        acc_zero = sem("acc_zero")
        hot_ready = sem("hot_ready")
        p2_ready = sem("p2_ready")
        cnt_ps = sem("cnt_ps")
        cnt_ps_free = sem("cnt_ps_free")
        tp_ps = sem("tp_ps")
        tp_ps_free = sem("tp_ps_free")
        v_in = [sem(f"v_in{i}") for i in range(2)]
        sum_ps = sem("sum_ps")
        sum_ps_free = sem("sum_ps_free")
        fin_ready = sem("fin_ready")
        x_again_in = [sem(f"x_again_in{i}") for i in range(2)]
        x_again_used = sem("x_again_used")
        bn_in = sem("bn_in")
        bn_var = sem("bn_var")
        bn_std = sem("bn_std")
        bn_row_ready = sem("bn_row_ready")
        bn_tp = sem("bn_tp")
        bn_ready = sem("bn_ready")
        w_in = [sem(f"w_in{i}") for i in range(STAGES)]
        w_hi = sem("w_hi")
        w_ready = sem("w_ready")
        var2_ready = sem("var2_ready")
        std2_ready = sem("std2_ready")
        xn2_ready = sem("xn2_ready")
        xt2_ps = sem("xt2_ps")
        xt2_hi = sem("xt2_hi")
        xt2_ready = sem("xt2_ready")
        soft = sem("soft")
        route_ps = sem("route_ps")
        route_shifted = sem("route_shifted")
        route_exp = sem("route_exp")
        route_ready = sem("route_ready")
        route_tp = sem("route_tp")
        route_t_ready = sem("route_t_ready")
        bias_ps = sem("bias_ps")
        bias_read = sem("bias_read")
        layer_ps = [sem(f"layer_ps{l}") for l in range(LAYERS)]
        layer_read = [sem(f"layer_read{l}") for l in range(LAYERS)]
        h_ready = [sem(f"h_ready{l}") for l in range(LAYERS)]
        y_ps = sem("y_ps")
        y_read = sem("y_read")
        rows_ready = sem("rows_ready")
        out_done = sem("out_done")

        block = stack.enter_context(nc.Block())
        x_tiles = x.rearrange("(t p) d -> p t d", p=P)
        v_rows = values.rearrange("(t p) w -> p t w", p=P)

        def units_of(slot):
            return range(NU * slot // SPR, NU * (slot + 1) // SPR)

        def chunk(c, par):
            if isinstance(c, int) and c < N_SHORT:
                return c, par, CH - 1, c * (CH - 1)
            return c, par, CH, c * CH - N_SHORT

        def chunks(eng, step):
            def one(c, par, first, last):
                prev = None if first else chunk(c - 1, 1 - par)
                if isinstance(c, int) and c == N_SHORT and not first:
                    prev = chunk(N_SHORT - 1, 1 - par)
                nxt = None if last else chunk(c + 1, 1 - par)
                for e in range(N_EXP):
                    step(prev, chunk(c, par), nxt, e)
            head = N_SHORT + 1
            pairs = (N_CHUNK - head - 1) // 2
            for c in range(head):
                one(c, c % 2, c == 0, False)
            with eng.Fori(0, pairs) as i:
                for k in range(2):
                    one(2 * i + (head + k), (head + k) % 2, False, False)
            for c in range(head + 2 * pairs, N_CHUNK):
                one(c, c % 2, False, c == N_CHUNK - 1)

        def weight_part(i):
            l, half = divmod(i, 2)
            e = slice(half * (N_EXP // 2), (half + 1) * (N_EXP // 2))
            return (f_w1, f_w2, f_wo)[l][e], w_split[l][0][:, e, :, :], w_split[l][1][:, e, :, :]

        def rounds(eng, body):
            with eng.Fori(0, (NPAIR - 3) // 2) as i:
                for par in range(2):
                    body(2 * i + par, par, True, True, 2)
            for b in range((NPAIR - 3) // 2 * 2, NPAIR):
                body(b, b % 2, b + 1 < NPAIR, b + 2 < NPAIR, 2 if b + 1 < NPAIR else NT - 2 * (NPAIR - 1))

        @block.sync
        def _(sp):
            sp.dma_start(samp_i[:, :], dst[FRONT:FRONT + NBLK * BLK, 0:1].rearrange("(b k) o -> o b k", k=BLK)[:, :, 0],
                         allow_slow_non_contiguous=True).then_inc(samp_in, 16)
            sp.dma_start(order_i[:, 0:SORT_N], dst[FRONT:FRONT + N_EDGES, 0:1].rearrange("(p k) o -> p (k o)", k=SORT_N)).then_inc(order_in, 16)
            sp.dma_start(order_i[:, SORT_N:SORT_N + 1],
                         dst[FRONT + SORT_N:FRONT + SORT_N + N_EDGES, 0:1].rearrange("(p k) o -> p (k o)", k=SORT_N)[:, 0:1],
                         allow_slow_non_contiguous=True).then_inc(order_in, 16)
            for g in range(NG):
                sp.dma_start(x_sb[:, g * GT:(g + 1) * GT, :], x_tiles[:, g * GT:(g + 1) * GT, :]).then_inc(x_in, 16)
            for l, params in enumerate(((f_g1, f_b1, f_m1, f_be1, f_v1), (f_g2, f_b2, f_m2, f_be2, f_v2))):
                for k, prm in enumerate(params):
                    sp.dma_start(bn_rows[:, 5 * l + k, :], prm.rearrange("e (m p) -> (e m) p", p=P)).then_inc(bn_in, 16)
            sp.dma_start(wr_sb[:, :, :], f_wr.rearrange("(k p) e -> p k e", p=P)).then_inc(bn_in, 16)
            sp.dma_start(br_sb[:, :], f_br.rearrange("(o e) -> o e", o=1).broadcast_to([P, N_EXP])).then_inc(bn_in, 16)
            sp.dma_start(bo_sb[:, :], f_bo).then_inc(bn_in, 16)
            sp.dma_start(w1_sb[:, :, :], g_w1.rearrange("(k p) h -> p k h", p=P)).then_inc(gate_w_in, 16)
            sp.dma_start(b1_sb[:, :], g_b1.rearrange("(p o) -> p o", o=1)).then_inc(gate_w_in, 16)
            sp.dma_start(w2_sb[:, :], g_w2).then_inc(gate_w_in, 16)
            sp.dma_start(b2_sb[:, :], g_b2.rearrange("(p o) -> p o", o=1).broadcast_to([P, 1])).then_inc(gate_w_in, 16)

            def store(b, par):
                sp.wait_ge(vs_ready, b + 1)
                sp.dma_start(v_rows[:, bass.ds(b * GT, GT), :],
                             vs[par][:, :, :]).then_inc(vs_out[par], 16)
            with sp.Fori(0, NG // 2) as i:
                for par in range(2):
                    store(2 * i + par, par)
            store(NG - 1, 0)
            sp.wait_ge(vs_out[0], 16 * (NG // 2 + 1))
            sp.wait_ge(vs_out[1], 16 * (NG // 2))
            sp.sem_inc(phase1_done, 1)
            sp.wait_ge(phase1_done, 5)

            def load_values(b, par, tiles):
                sp.dma_start(vring[par][:, 0:tiles, :], v_rows[:, bass.ds(2 * b, tiles), 0:2 * VW]).then_inc(v_in[par], 16)
            load_values(0, 0, 2)
            load_values(1, 1, 2)

            def body(b, par, has_next, has_next2, tiles):
                if has_next2:
                    sp.wait_ge(sum_ps, SPR * (b + 1))
                    load_values(b + 2, par, 2 if not isinstance(b, int) or b + 3 < NPAIR else NT - 2 * (NPAIR - 1))
            rounds(sp, body)

            def load_rows(s):
                if s >= 2:
                    sp.wait_ge(x_again_used, s - 1)
                sp.dma_start(x_again[s % 2][:, :, :], x_tiles[:, s * HS:(s + 1) * HS, :]).then_inc(x_again_in[s % 2], 16)

            def load_weights(i):
                if i >= STAGES:
                    sp.wait_ge(w_ready, i - STAGES + 1)
                sp.dma_start(w_stage[i % STAGES][:, :, :, :],
                             weight_part(i)[0].rearrange("e (k p) h -> p e k h", p=P)).then_inc(w_in[i % STAGES], 16)
            sp.wait_ge(cnt_ps_free, NPAIR * NU + 2)
            for load, i in ((load_rows, 0), (load_rows, 1), (load_weights, 0), (load_weights, 1), (load_weights, 2),
                            (load_rows, 2), (load_weights, 3), (load_rows, 3), (load_weights, 4), (load_rows, 4),
                            (load_weights, 5), (load_rows, 5), (load_rows, 6)):
                load(i)

            out_tiles = out.rearrange("(t p) d -> p t d", p=P)

            def step(prev, cur, nxt, e):
                if e == 0 and prev is not None:
                    c, par, n, t0 = prev
                    sp.wait_ge(rows_ready, c + 1)
                    sp.dma_start(out_tiles[:, bass.ds(t0, n), :], acc[:, bass.ds(t0, n), 0:D]).then_inc(out_done, 16)
            chunks(sp, step)
            c, par, n, t0 = chunk(N_CHUNK - 1, (N_CHUNK - 1) % 2)
            sp.wait_ge(rows_ready, c + 1)
            sp.dma_start(out_tiles[:, bass.ds(t0, n), :], acc[:, bass.ds(t0, n), 0:D]).then_inc(out_done, 16)
            sp.wait_ge(out_done, 16 * N_CHUNK)

        @block.gpsimd
        def _(pool):
            pool.memset(ident[:, :], 0.0).then_inc(pool_chain, 1)
            pool.memset(ident16[:, :], 0.0).then_inc(pool_chain, 1)
            pool.iota(node_i[:, :], pattern=[[P, NT2]], base=0, channel_multiplier=1).then_inc(pool_chain, 1)
            pool.wait_ge(pool_chain, 3)
            for m in (ident, ident16):
                pool.affine_select(out=m[:, :], in_=m[:, :], compare_op=ALU.not_equal, fill=1.0, base=0,
                                   pattern=[[-1, P]], channel_multiplier=1).then_inc(consts_ready, 1)
            pool.tensor_copy(node_id[:, :], node_i[:, :]).then_inc(consts_ready, 1)
            pool.memset(hi_bias[:, :], float(NONE_HI)).then_inc(consts_ready, 1)
            pool.memset(ones_row[:, :], 1.0).then_inc(consts_ready, 1)
            pool.memset(ones_sq[:, :], 1.0).then_inc(consts_ready, 1)
            pool.memset(eps_ln[:, :], LN_EPS).then_inc(consts_ready, 1)
            pool.memset(eps_bn[:, :], BN_EPS).then_inc(consts_ready, 1)
            pool.wait_ge(consts_ready, 8)
            pool.memset(hi_bias[SLOT:P, :], float(NONE_HI + NHI)).then_inc(consts_ready, 1)

            pool.wait_ge(consts_ready, 9)
            pool.iota(iota_lo[:, :, :], pattern=[[1, P], [0, CG]], base=0, channel_multiplier=0,
                      allow_small_or_imprecise_dtypes=True).then_inc(iota_ready, 1)
            pool.iota(iota_hi[:, :, :], pattern=[[1, 2 * NHI], [0, CG]], base=0, channel_multiplier=0,
                      allow_small_or_imprecise_dtypes=True).then_inc(iota_ready, 1)

            pool.wait_ge(block_ready, 1)

            def fetch_blocks(g, par):
                if g >= 2:
                    pool.wait_ge(blk_counted, g - 1)
                for j in range(SG):
                    pool.indirect_dma_start(out=blk_i[par][:, j, :], out_offset=None, in_=dst[:, :],
                                            in_offset=bass.IndirectOffsetOnAxis(ap=block_i[:, bass.ds(g * SG + j, 1)], axis=0),
                                            ).then_inc(blk_in[par], 16)
            for g in range(NSG):
                fetch_blocks(g, g % 2)
            pool.wait_ge(row_ready, 1)
            for t in range(NT2):
                pool.indirect_dma_start(out=win[:, t, :], out_offset=None, in_=edges[:, :],
                                        in_offset=bass.IndirectOffsetOnAxis(ap=row_i[:, t:t + 1], axis=0),
                                        ).then_inc(win_in[t // LG], 16)
            pool.drain().then_inc(phase1_done, 1)
            pool.wait_ge(phase1_done, 5)

            pool.wait_ge(general_ready, 1)
            with pool.If(pool.value_load(general_i[0:1, 0:1], min_val=0, max_val=1) > 0):
                pool.iota(sp_iota_i[:, :], pattern=[[1, P]], base=0, channel_multiplier=0).then_inc(sp_iota_ready, 1)
                pool.wait_ge(sp_iota_ready, 1)
                pool.tensor_copy(sp_iota[:, :], sp_iota_i[:, :]).then_inc(sp_iota_ready, 1)
                with pool.Fori(0, SPILL_CH) as k:
                    pool.wait_ge(sp_chunk_done, k + 1)
                    pool.dma_start(sp_edge[:, :], edges[bass.ds(k * P, P), :]).then_inc(sp_edge_in, 16)
                    pool.dma_start(sp_prev[:, :], dst[bass.ds(k * P, P), :]).then_inc(sp_prev_in, 16)
                    pool.wait_ge(sp_index, k + 1)
                    pool.tensor_tensor(sp_idle[:, :], sp_iota[:, 0:1], sp_iota[:, 0:1], ALU.subtract).then_inc(sp_idled, 1)
                    pool.indirect_dma_start(out=sp_rows[:, :], out_offset=None, in_=values[:, :],
                                            in_offset=bass.IndirectOffsetOnAxis(ap=sp_int[:, 0:1], axis=0)).then_inc(sp_rows_in, 16)

            with pool.If(pool.value_load(general_i[0:1, 0:1], min_val=0, max_val=1) < 1):
                pool.memset(acc[:, :, :], 0.0)
            pool.drain().then_inc(acc_zero, 1)

            for i in range(N_PART):
                pool.wait_ge(w_hi, i + 1)
                _, hi, lo = weight_part(i)
                pool.tensor_tensor(lo, w_stage[i % STAGES][:, :, :, :], hi.bitcast(f32), ALU.subtract).then_inc(w_ready, 1)

        @block.scalar
        def _(act):
            act.wait_ge(bn_in, 16 * (5 * LAYERS + 3))
            act.wait_ge(consts_ready, 9)
            for l in range(LAYERS):
                act.activation(bn_tmp[:, 2 * l, :], bn_rows[:, 5 * l + 4, :], ACT.Sqrt, bias=eps_bn[0:N_EXP * KC, :]).then_inc(bn_std, 1)
            act.activation(wr_split[0][:, :, :], wr_sb[:, :, :], ACT.Copy).then_inc(bn_std, 1)
            act.wait_ge(bn_tp, 1)
            act.activation(bn_cols[:, :, :].rearrange("p a b -> p (a b)"), psum[:, 7, 0:2 * LAYERS * N_EXP * KC], ACT.Copy).then_inc(bn_ready, 1)
            act.wait_ge(var_ready, 1)
            act.activation(rstd[:, :], mean_var[:, :, 1], ACT.Sqrt, bias=eps_ln[:, :]).then_inc(std_ready, 1)

            def gate_act(b):
                for q in range(4):
                    k, lo, n = q // 2, 512 * (q % 2), (512, GT * P - 512)[q % 2]
                    if q == 0:
                        act.wait_ge(xt_ps, b + 1)
                    act.activation(xt[:, k, lo:lo + n], psum[:, q, 0:n], ACT.Copy).then_inc(xt_ready, 1)
                act.wait_ge(hid_ps, b + 1)
                for q in range(2):
                    lo, n = 512 * q, (512, GT * P - 512)[q]
                    act.activation(hid[:, lo:lo + n], psum[:, 4 + q, 0:n], ACT.Relu, bias=b1_sb[:, :]).then_inc(hid_ready, 1)
                act.wait_ge(logit_ps, b + 1)
                act.activation(gate[:, bass.ds(b * GT, GT)], psum[:, 7, 0:GT], ACT.Exp, scale=-1.0, bias=b2_neg[:, :]).then_inc(gate_ready, 1)
            act.wait_ge(gate_w_in, 64)
            act.wait_ge(exp_ready, 1)
            with act.Fori(0, NG) as b:
                gate_act(b)
            for g in range(NLG):
                t0, w = g * LG // 2, LG // 2
                act.wait_ge(lists_tp, 2 * g + 1)
                act.activation(hi_list[:, t0:t0 + w, :].rearrange("p t c -> p (t c)"),
                               psum[:, 5, :].bitcast(bf16)[:, 0:w * P], ACT.Identity, bias=hi_bias[:, :]).then_inc(lists_ready, 1)
                act.wait_ge(lists_tp, 2 * g + 2)
                act.activation(lo_list[:, t0:t0 + w, :].rearrange("p t c -> p (t c)"),
                               psum[:, 6, :].bitcast(bf16)[:, 0:w * P], ACT.Copy).then_inc(lists_ready, 1)
            act.drain().then_inc(phase1_done, 1)
            act.wait_ge(phase1_done, 5)
            act.sem_inc(cnt_ps_free, 2)
            act.sem_inc(tp_ps_free, 2)

            def take_counts(b, par, u):
                act.wait_ge(cnt_ps, b * NU + u + 1)
                src = psum[:, u % 2, 0:UC * 2 * NHI].rearrange("p (c j) -> p j c", c=UC)
                act.activation(counts[par][:, :, u * UC:(u + 1) * UC], src, ACT.Copy).then_inc(cnt_ps_free, 1)

            def take_transposed(b, par, s, tile):
                if s == 0 and tile == 0:
                    act.wait_ge(p2_ready, b + 1)
                act.wait_ge(tp_ps, b * 2 * NS + 2 * s + tile + 1)
                act.activation(counts_t[par][tile][:, s * HS * P:(s + 1) * HS * P], psum[:, 2 + tile, :].bitcast(bf16)[:, 0:HS * P],
                               ACT.Copy, scale=p2_round[par][:, tile:tile + 1]).then_inc(tp_ps_free, 1)

            for u in range(NU):
                take_counts(0, 0, u)
            for s in range(NS):
                for tile in range(2):
                    take_transposed(0, 0, s, tile)
            for u in range(NU):
                take_counts(1, 1, u)

            def body(b, par, has_next, has_next2, tiles):
                for s in range(NS):
                    for k in range(NSL):
                        if has_next2:
                            for u in units_of(s * NSL + k):
                                take_counts(b + 2, par, u)
                        if has_next and k % 2 == 0:
                            take_transposed(b + 1, 1 - par, s, k // 2)
            rounds(act, body)

            def round_weights(i):
                act.wait_ge(w_in[i % STAGES], 16 * (i // STAGES + 1))
                act.activation(weight_part(i)[1], w_stage[i % STAGES][:, :, :, :], ACT.Copy).then_inc(w_hi, 1)

            def deviations(s0, s1, n):
                act.wait_ge(var2_ready, n)
                tiles = slice(s0 * HS, (s1 + 1) * HS)
                act.activation(rstd[:, tiles], mean_var[:, tiles, 1], ACT.Sqrt, bias=eps_ln[:, :]).then_inc(std2_ready, 1)

            act.wait_ge(sum_ps, (NPAIR - 1) * SPR)
            round_weights(0)
            round_weights(1)
            deviations(0, 0, 1)
            round_weights(2)
            round_weights(3)
            act.wait_ge(sum_ps, NPAIR * SPR)
            round_weights(4)
            round_weights(5)

            def prep_rows(ch):
                c, par, n, t0 = ch
                for k in range(KC):
                    act.wait_ge(xt2_ps, c * KC + k + 1)
                    act.activation(xt2[par][0][:, k, 0:n * P], psum[:, 6 + k, 0:n * P], ACT.Copy).then_inc(xt2_hi, 1)

            def prep_exp(ch):
                c, par, n, t0 = ch
                act.wait_ge(route_shifted, c + 1)
                act.activation(expert_w[par][:, 0:n, :], logits[:, 0:n, :], ACT.Exp).then_inc(route_exp, 1)

            def prep_wt(ch):
                c, par, n, t0 = ch
                act.wait_ge(route_tp, c + 1)
                act.activation(expert_wt[:, 0:n * P], psum[0:N_EXP, 7, 0:n * P], ACT.Copy).then_inc(route_t_ready, 1)

            def relu(layer, ch, e):
                c, par, n, t0 = ch
                q = c * N_EXP + e
                h = h1[e % 2] if layer == 0 else h2
                for m in range(KC):
                    col = e * KC + m
                    scale, shift = bn_cols[:, 2 * layer, col:col + 1], bn_cols[:, 2 * layer + 1, col:col + 1]
                    act.wait_ge(layer_ps[layer], q * KC + m + 1)
                    act.wait_ge(h_ready[layer], q * KC + m + 1)
                    act.activation(relu_out[layer][m][:, 0:n * P], psum[:, 2 * layer + m, 0:n * P], ACT.Relu,
                                   bias=shift, scale=scale)
                    act.activation(h[0][:, m, 0:n * P], psum[:, 2 * layer + m, 0:n * P], ACT.Relu,
                                   bias=shift, scale=scale).then_inc(layer_read[layer], 1)

            first = chunk(0, 0)
            prep_rows(first)
            prep_exp(first)
            act.wait_ge(x_again_used, NS)
            act.wait_ge(w_ready, 4)
            relu(0, first, 0)
            prep_wt(first)
            act.wait_ge(w_ready, N_PART)

            def step(prev, cur, nxt, e):
                if e + 1 < N_EXP:
                    relu(0, cur, e + 1)
                elif nxt is not None:
                    relu(0, nxt, 0)
                relu(1, cur, e)
                if nxt is not None:
                    if e == 1:
                        prep_rows(nxt)
                    if e == 3:
                        prep_exp(nxt)
                    if e == 4:
                        prep_wt(nxt)
                if isinstance(cur[0], int) and (cur[0], e) in NORM_END:
                    s0, s1 = NORM_END[(cur[0], e)]
                    deviations(s0, s1, 2 + list(NORM_END).index((cur[0], e)))
            chunks(act, step)

        @block.tensor
        def _(pe):
            pe.wait_ge(consts_ready, 9)
            pe.wait_ge(samp_f_ready, 1)
            pe.matmul(psum[:, 7, 0:NBLK], ones_row[:, :], samp_f[:, :], start=True, stop=True).then_inc(samp_bc, 1)

            pe.wait_ge(bn_row_ready, 1)
            pe.wait_ge(bn_ready, 1)
            for k in range(2 * LAYERS):
                w = N_EXP * KC
                last = pe.transpose(psum[:, 7, k * w:(k + 1) * w], bn_tmp[:, k, :], ident[0:w, 0:w])
            last.then_inc(bn_tp, 1)

            pe.wait_ge(order_ready, 1)
            pe.wait_ge(bn_ready, 2)
            pe.matmul(psum[:, 7, 0:1], ones_sq[:, :], flags[:, 0:1], start=True, stop=True).then_inc(order_total, 1)

            def gate_pe(b, par):
                pe.wait_ge(xn_ready, b + 1)
                if True:
                    pe.wait_ge(xt_ready, 4 * b + 4)
                for k in range(KC):
                    for j in range(GT):
                        last = pe.transpose(psum[:, 2 * k + j // 4, (j % 4) * P:(j % 4 + 1) * P],
                                            xn[par][:, j, k * P:(k + 1) * P], ident[:, :])
                last.then_inc(xt_ps, 1)
                pe.wait_ge(xt_ready, 4 * b + 8)
                pe.wait_ge(hid_ready, 2 * b + 2)
                for q in range(2):
                    lo, n = 512 * q, (512, GT * P - 512)[q]
                    for k in range(KC):
                        last = pe.matmul(psum[:, 4 + q, 0:n], w1_sb[:, k, :], xt[:, k, lo:lo + n],
                                         start=(k == 0), stop=(k == KC - 1))
                last.then_inc(hid_ps, 1)
                pe.wait_ge(hid_ready, 2 * b + 4)
                pe.wait_ge(gate_ready, b + 1)
                for j in range(GT):
                    last = pe.matmul(psum[:, 7, j:j + 1], hid[:, j * P:(j + 1) * P], w2_sb[:, :], start=True, stop=True)
                last.then_inc(logit_ps, 1)
            pe.sem_inc(xt_ready, 4)
            pe.sem_inc(hid_ready, 2)
            pe.sem_inc(gate_ready, 1)
            pe.wait_ge(gate_w_in, 64)
            with pe.Fori(0, NG // 2) as i:
                for par in range(2):
                    gate_pe(2 * i + par, par)
            gate_pe(NG - 1, 0)

            for g in range(NLG):
                for m, lst, bank in ((2 * g, hi16, 5), (2 * g + 1, lo16, 6)):
                    if m % 2 == 0:
                        pe.wait_ge(slots_ready, g + 1)
                    if m >= 2:
                        pe.wait_ge(lists_ready, m - 1)
                    for u in range(LG // 2):
                        t = g * LG + 2 * u
                        last = pe.transpose(psum[:, bank, :].bitcast(bf16)[:, u * P:(u + 1) * P],
                                            lst[:, t:t + 2, :].rearrange("p t s -> p (t s)"), ident16[:, :])
                    last.then_inc(lists_tp, 1)
            pe.wait_ge(general_count, 1)
            pe.matmul(psum[:, 7, 8:10], ones_sq[:, :], flags[:, :], start=True, stop=True).then_inc(general_total, 1)
            pe.drain().then_inc(phase1_done, 1)
            pe.wait_ge(phase1_done, 5)
            pe.wait_ge(general_ready, 1)
            with pe.If(pe.value_load(general_i[0:1, 0:1], min_val=0, max_val=1) > 0):
                with pe.Fori(0, SPILL_CH) as k:
                    with pe.Fori(0, NS) as s:
                        pe.wait_ge(sp_picked, k * NS + s + 1)
                        for r in range(HS):
                            last = pe.matmul(psum[:, r, 0:VW], sp_hot[:, :], sp_pick[:, r, :], start=True, stop=True)
                        last.then_inc(sp_ps, 1)

            def count(b, u):
                g = u // (CG // UC)
                if u % (CG // UC) == 0:
                    pe.wait_ge(hot_ready, b * NCG + g + 1)
                pe.wait_ge(cnt_ps_free, b * NU + u + 1)
                for c in range(UC):
                    col = u % (CG // UC) * UC + c
                    last = pe.matmul(psum[:, u % 2, c * 2 * NHI:(c + 1) * 2 * NHI], hot_lo[g % RING][:, :, col],
                                     hot_hi[g % RING][:, :, col], start=True, stop=True)
                last.then_inc(cnt_ps, 1)

            def transpose_counts(b, par, s, tile):
                if s == 0 and tile == 0:
                    pe.wait_ge(cnt_ps_free, (b + 1) * NU + 2)
                pe.wait_ge(tp_ps_free, b * 2 * NS + 2 * s + tile + 1)
                for r in range(HS):
                    last = pe.transpose(psum[:, 2 + tile, :].bitcast(bf16)[:, r * P:(r + 1) * P],
                                        counts[par][:, tile * NHI + s * HS + r, :], ident16[:, :])
                last.then_inc(tp_ps, 1)

            def sums(b, par, s, k, tiles):
                if k == 0:
                    pe.wait_ge(tp_ps_free, b * 2 * NS + 2 * s + 4)
                if s == 0 and k == 0:
                    pe.wait_ge(v_in[par], (b - par) * 8 + 16)
                slot = s * NSL + k
                pe.wait_ge(sum_ps_free, b * SPR + slot + 1)
                first, n = SLOTS_OF[k]
                for r in range(n):
                    hi = s * HS + first + r
                    for tile in range(tiles):
                        for half in range(2):
                            last = pe.matmul(psum[:, 4 + 2 * (slot % 2) + r, 0:VW], counts_t[par][tile][:, hi * P:(hi + 1) * P],
                                             vring[par][:, tile, half * VW:(half + 1) * VW],
                                             start=(tile == 0 and half == 0), stop=(tile == tiles - 1 and half == 1))
                last.then_inc(sum_ps, 1)

            for u in range(NU):
                count(0, u)
            for s in range(NS):
                for tile in range(2):
                    transpose_counts(0, 0, s, tile)
            for u in range(NU):
                count(1, u)

            def body(b, par, has_next, has_next2, tiles):
                for s in range(NS):
                    for k in range(NSL):
                        sums(b, par, s, k, tiles)
                        if has_next2:
                            for u in units_of(s * NSL + k):
                                count(b + 2, u)
                        if has_next and k % 2 == 0:
                            transpose_counts(b + 1, 1 - par, s, k // 2)
            rounds(pe, body)

            pe.wait_ge(sum_ps_free, NPAIR * SPR + 2)
            pe.wait_ge(cnt_ps_free, NPAIR * NU + 2)
            pe.wait_ge(tp_ps_free, NPAIR * 2 * NS + 2)
            for l in range(LAYERS):
                pe.sem_inc(layer_read[l], KC)
            pe.sem_inc(y_read, 2)
            pe.sem_inc(bias_read, 2)
            TERMS = ((0, 0), (0, 1), (1, 0))

            def prep_tp(ch):
                c, par, n, t0 = ch
                pe.wait_ge(xn2_ready, c + 1)
                pe.wait_ge(bias_read, 2 * c + 2)
                for k in range(KC):
                    for j in range(n):
                        last = pe.transpose(psum[:, 6 + k, j * P:(j + 1) * P], xn2[:, j, k * P:(k + 1) * P], ident[:, :])
                    last.then_inc(xt2_ps, 1)

            def prep_route(ch):
                c, par, n, t0 = ch
                pe.wait_ge(xt2_ready, c * KC + KC)
                for j in range(n):
                    for i, (a, w) in enumerate(TERMS):
                        for k in range(KC):
                            last = pe.matmul(psum[:, 6, j * N_EXP:(j + 1) * N_EXP], xt2[par][a][:, k, j * P:(j + 1) * P],
                                             wr_split[w][:, k, :], start=(i == 0 and k == 0),
                                             stop=(i == len(TERMS) - 1 and k == KC - 1))
                last.then_inc(route_ps, 1)

            def prep_wt(ch):
                c, par, n, t0 = ch
                pe.wait_ge(route_ready, c + 1)
                for j in range(n):
                    last = pe.transpose(psum[0:N_EXP, 7, j * P:(j + 1) * P], expert_w[par][:, j, :], ident[:, :])
                last.then_inc(route_tp, 1)

            def prep_bias(ch):
                c, par, n, t0 = ch
                pe.wait_ge(route_t_ready, c + 1)
                for j in range(n):
                    last = pe.matmul(psum[:, 6 + j // 2, (j % 2) * D:(j % 2 + 1) * D], expert_wt[:, j * P:(j + 1) * P],
                                     bo_sb[:, :], start=True, stop=True)
                last.then_inc(bias_ps, 1)

            def layer(l, ch, e):
                c, par, n, t0 = ch
                q = c * N_EXP + e
                src = xt2[par] if l == 0 else h1[e % 2]
                if l == 0:
                    pe.wait_ge(xt2_ready, c * KC + KC)
                else:
                    pe.wait_ge(h_ready[0], q * KC + 2 * KC)
                for m in range(KC):
                    pe.wait_ge(layer_read[l], q * KC + m + 1)
                    for i, (a, w) in enumerate(TERMS):
                        for k in range(KC):
                            last = pe.matmul(psum[:, 2 * l + m, 0:n * P], w_split[l][w][:, e, k, m * P:(m + 1) * P],
                                             src[a][:, k, 0:n * P], start=(i == 0 and k == 0),
                                             stop=(i == len(TERMS) - 1 and k == KC - 1))
                    last.then_inc(layer_ps[l], 1)

            def layer3(ch, e):
                c, par, n, t0 = ch
                q = c * N_EXP + e
                pe.wait_ge(h_ready[1], q * KC + 2 * KC)
                for j in range(n):
                    if j % 2 == 0:
                        pe.wait_ge(y_read, 2 * q + j // 2 + 1)
                    for i, (a, w) in enumerate(TERMS):
                        for k in range(KC):
                            last = pe.matmul(psum[:, 4 + j // 2, (j % 2) * D:(j % 2 + 1) * D], h2[a][:, k, j * P:(j + 1) * P],
                                             w_split[2][w][:, e, k, :], start=(i == 0 and k == 0),
                                             stop=(i == len(TERMS) - 1 and k == KC - 1))
                    if j % 2 == 1 or j == n - 1:
                        last.then_inc(y_ps, 1)

            first = chunk(0, 0)
            prep_tp(first)
            prep_route(first)
            pe.wait_ge(w_ready, 2)
            layer(0, first, 0)
            prep_wt(first)
            prep_bias(first)

            def step(prev, cur, nxt, e):
                if e + 1 < N_EXP:
                    layer(0, cur, e + 1)
                elif nxt is not None:
                    layer(0, nxt, 0)
                if prev is None and e == 0:
                    pe.wait_ge(w_ready, 4)
                if prev is None and e == 1:
                    pe.wait_ge(w_ready, N_PART)
                if e > 0:
                    layer3(cur, e - 1)
                elif prev is not None:
                    layer3(prev, N_EXP - 1)
                layer(1, cur, e)
                if nxt is not None:
                    if e == 1:
                        prep_tp(nxt)
                    if e == 2:
                        prep_route(nxt)
                    if e == 4:
                        prep_wt(nxt)
                    if e == 5:
                        prep_bias(nxt)
            chunks(pe, step)
            layer3(chunk(N_CHUNK - 1, (N_CHUNK - 1) % 2), N_EXP - 1)

        @block.vector
        def _(dve):
            n = [0]

            def after(ins):
                n[0] += 1
                ins.then_inc(chain, 1)

            def settle():
                dve.wait_ge(chain, n[0])

            def count_less(values, t, width, out_):
                dve.wait_ge(chain, n[0] - 1)
                after(dve.tensor_scalar(less[:, t % 2, 0:width], values, node_id[:, t:t + 1], None, ALU.is_lt, ALU.add,
                                        accum_out=out_[:, t:t + 1]))

            dve.wait_ge(samp_in, 16)
            dve.tensor_copy(samp_f[:, :], samp_i[:, :]).then_inc(samp_f_ready, 1)
            after(dve.memset(vf[:, :, :], 0.0))
            after(dve.memset(gate_p2[:, :], 0.0))
            after(dve.memset(flags[:, :], 0.0))
            dve.wait_ge(samp_bc, 1)
            after(dve.tensor_copy(samp[:, :], psum[:, 7, 0:NBLK]))
            dve.wait_ge(consts_ready, 9)
            settle()
            dve.sem_inc(bn_ready, 1)
            for t in range(NT2):
                count_less(samp[:, :], t, NBLK, n_blocks)
            settle()
            after(dve.tensor_scalar(block_f[:, :], n_blocks[:, :], -1.0, 0.0, ALU.add, ALU.max))
            settle()
            after(dve.tensor_scalar(block_f[:, :], block_f[:, :], float(BLK), None, ALU.mult))
            settle()
            dve.tensor_scalar(block_i[:, :], block_f[:, :], float(FRONT), None, ALU.add).then_inc(block_ready, 1)

            def search(g):
                dve.wait_ge(blk_in[g % 2], 16 * SG * (g // 2 + 1))
                for j in range(SG):
                    count_less(blk_i[g % 2][:, j, :].bitcast(u16).rearrange("p (k two) -> p k two", two=2)[:, :, 0],
                               g * SG + j, BLK, n_less)
                settle()
                dve.sem_inc(blk_counted, 1)

            def check_order():
                dve.wait_ge(order_in, 32)
                after(dve.tensor_tensor(order_f[:, :], order_i[:, 0:SORT_N], order_i[:, 1:SORT_N + 1], ALU.is_gt))
                settle()
                dve.tensor_reduce(out=flags[0:SORT_P, 0:1], in_=order_f[:, :], axis=AX.X, op=ALU.max).then_inc(order_ready, 1)

            def mask_nodes():
                dve.wait_ge(order_total, 1)
                after(dve.tensor_scalar(unsorted[:, :], psum[:, 7, 0:1], 1.0, None, ALU.min))
                settle()
                after(dve.scalar_tensor_tensor(out=node_cmp[:, :], in0=node_id[:, :], scalar=1.0, in1=unsorted[:, :].broadcast_to([P, NT2]),
                                               op0=ALU.add, op1=ALU.mult))
                settle()
                after(dve.tensor_tensor(node_cmp[:, :], node_id[:, :], node_cmp[:, :], ALU.subtract))

            def fold_batch_norm():
                dve.wait_ge(bn_std, LAYERS + 1)
                rows = [[bn_rows[:, 5 * l + k, :] for k in range(4)] + [bn_tmp[:, 2 * l, :], bn_tmp[:, 2 * l + 1, :]]
                        for l in range(LAYERS)]
                for g, bb, m, be, scale, shift in rows:
                    after(dve.reciprocal(scale, scale))
                    after(dve.tensor_tensor(shift, bb, m, ALU.subtract))
                settle()
                for g, bb, m, be, scale, shift in rows:
                    after(dve.tensor_tensor(scale, scale, g, ALU.mult))
                settle()
                for g, bb, m, be, scale, shift in rows:
                    after(dve.tensor_tensor(shift, shift, scale, ALU.mult))
                settle()
                for g, bb, m, be, scale, shift in rows:
                    after(dve.tensor_tensor(shift, shift, be, ALU.add))
                after(dve.tensor_tensor(wr_split[1][:, :, :], wr_sb[:, :, :], wr_split[0][:, :, :].bitcast(f32), ALU.subtract))
                settle()
                dve.sem_inc(bn_row_ready, 1)
                dve.wait_ge(gate_w_in, 64)
                dve.tensor_scalar(b2_neg[:, :], b2_sb[:, :], -1.0, None, ALU.mult).then_inc(exp_ready, 1)

            def statistics():
                dve.wait_ge(x_in, 16 * NG)
                for t in range(NT):
                    after(dve.bn_stats(stats[:, t, :], x_sb[:, t, :]))
                settle()
                for t in range(NT):
                    last = dve.bn_aggr(mean_var[:, t, :], stats[:, t, :])
                last.then_inc(var_ready, 1)

            def normalise(b):
                for j in range(GT):
                    last = dve.tensor_scalar(xn[b % 2][:, j, :], x_sb[:, b * GT + j, :], mean_var[:, b * GT + j, 0:1],
                                             rstd[:, b * GT + j:b * GT + j + 1], ALU.subtract, ALU.mult)
                last.then_inc(xn_ready, 1)

            def weigh(b):
                par = b % 2
                dve.wait_ge(gate_ready, b + 2)
                w = gate[:, b * GT:(b + 1) * GT]
                p2 = gate_p2[:, b * GT:(b + 1) * GT]
                after(dve.tensor_scalar(w, w, 1.0, None, ALU.add))
                settle()
                after(dve.reciprocal(w, w))
                settle()
                after(dve.tensor_scalar(p2.bitcast(i32), w.bitcast(i32), EXP_BITS, None, ALU.bitwise_and))
                settle()
                after(dve.tensor_scalar(p2_inv[:, :], p2.bitcast(i32), -1.0, float(254 << 23), ALU.mult, ALU.add))
                settle()
                after(dve.scalar_tensor_tensor(out=gate_m[:, :], in0=w, scalar=VSCALE, in1=p2_inv[:, :].bitcast(f32),
                                               op0=ALU.mult, op1=ALU.mult))
                settle()
                if b >= 1:
                    dve.wait_ge(vs_ready, b)
                for j in range(GT):
                    after(dve.tensor_scalar(vf[:, j, 0:D], xn[par][:, j, :], gate_m[:, j:j + 1], None, ALU.mult))
                after(dve.tensor_copy(vf[:, :, D], gate_m[:, :]))
                settle()
                if b >= 2:
                    dve.wait_ge(vs_out[par], 16 * (b // 2))
                after(dve.tensor_copy(vs[par][:, :, 0:VW], vf[:, :, :]))
                settle()
                dve.tensor_copy(vs[par][:, :, 2 * VW:VROW].bitcast(f32)[:, :, 0], p2)
                dve.tensor_tensor(vs[par][:, :, VW:2 * VW], vf[:, :, :], vs[par][:, :, 0:VW], ALU.subtract).then_inc(vs_ready, 1)

            def fill_slots(g):
                t0, t1 = g * LG, (g + 1) * LG
                dve.wait_ge(win_in[g], 16 * LG)
                source = win[:, t0:t1, :].rearrange("p t (s two) -> p t s two", two=2)[:, :, 0:SLOT, 1]
                dest = win[:, t0:t1, :].bitcast(u16).rearrange("p t (s four) -> p t s four", four=4)[:, :, :, 0]
                settle()
                after(dve.tensor_scalar(slot_hi[:, :, :], source, 7, None, ALU.arith_shift_right))
                after(dve.tensor_scalar(slot_lo[:, :, :], source, P - 1, None, ALU.bitwise_and))
                after(dve.tensor_tensor(slot_ok[:, t0:t1, :], dest, node_cmp[:, t0:t1].unsqueeze(2).broadcast_to([P, LG, WIN]), ALU.is_equal))
                settle()
                after(dve.tensor_copy(lo16[:, t0:t1, :], slot_lo[:, :, :]))
                after(dve.scalar_tensor_tensor(out=hi16[:, t0:t1, :], in0=slot_hi[:, :, :], scalar=-float(NONE_HI),
                                               in1=slot_ok[:, t0:t1, 0:SLOT], op0=ALU.add, op1=ALU.mult))
                settle()
                dve.sem_inc(slots_ready, 1)

            check_order()
            fold_batch_norm()
            statistics()
            search(0)
            mask_nodes()
            dve.wait_ge(std_ready, 1)
            after(dve.reciprocal(rstd[:, :], rstd[:, :]))
            settle()
            normalise(0)
            search(1)
            normalise(1)
            for g in range(2, 6):
                search(g)
            weigh(0)
            search(6)
            normalise(2)
            search(7)
            weigh(1)
            search(8)
            normalise(3)
            search(9)
            after(dve.tensor_tensor(row_f[:, :], block_f[:, :], n_less[:, :], ALU.add))
            settle()
            dve.tensor_copy(row_i[:, :], row_f[:, :]).then_inc(row_ready, 1)
            weigh(2)
            normalise(4)
            weigh(3)
            fill_slots(0)
            normalise(5)
            weigh(4)
            fill_slots(1)
            normalise(6)
            weigh(5)
            fill_slots(2)
            weigh(6)
            fill_slots(3)
            fill_slots(4)
            dve.tensor_reduce(out=flags[:, 1:2], in_=slot_ok[:, :, SLOT], axis=AX.X, op=ALU.max).then_inc(general_count, 1)
            dve.wait_ge(general_total, 1)
            after(dve.tensor_tensor(general[:, :], psum[:, 7, 9:10], unsorted[:, :], ALU.add))
            settle()
            after(dve.tensor_scalar(general[:, :], general[:, :], 1.0, None, ALU.min))
            settle()
            dve.tensor_copy(general_i[:, :], general[:, :]).then_inc(general_ready, 1)
            dve.drain().then_inc(phase1_done, 1)
            dve.wait_ge(phase1_done, 5)
            dve.wait_ge(general_ready, 1)
            dve.sem_inc(sum_ps_free, 2)

            with dve.If(dve.value_load(general_i[0:1, 0:1], min_val=0, max_val=1) > 0):
                dve.memset(acc[:, :, :], 0.0).then_inc(sp_chain, 1)
                dve.wait_ge(sp_chain, 1)
                dve.wait_ge(sp_iota_ready, 2)
                dve.sem_inc(sp_chunk_done, 1)
                with dve.Fori(0, SPILL_CH) as k:
                    dve.wait_ge(sp_edge_in, 16 * k + 16)
                    dve.wait_ge(sp_prev_in, 16 * k + 16)
                    DST, PREV, LO, HI, TAKE, REAL, CLIP, SAME, SCALE = (sp_f[:, c:c + 1] for c in range(9))
                    CHAIN = 5
                    dve.tensor_copy(DST, sp_edge[:, 0:1])
                    dve.tensor_copy(PREV, sp_prev[:, :])
                    dve.tensor_scalar(sp_int[:, 1:2], sp_edge[:, 1:2], 7, None, ALU.arith_shift_right)
                    dve.tensor_scalar(sp_int[:, 2:3], sp_edge[:, 1:2], P - 1, None, ALU.bitwise_and).then_inc(sp_chain, 1)
                    dve.wait_ge(sp_chain, CHAIN * k + 2)
                    dve.tensor_scalar(CLIP, DST, float(N_NODES - 1), None, ALU.min)
                    dve.tensor_tensor(SAME, DST, PREV, ALU.is_equal)
                    dve.tensor_scalar(REAL, DST, float(DST_PAD), None, ALU.is_lt)
                    dve.tensor_copy(HI, sp_int[:, 1:2])
                    dve.tensor_copy(LO, sp_int[:, 2:3]).then_inc(sp_chain, 1)
                    dve.wait_ge(sp_chain, CHAIN * k + 3)
                    dve.tensor_copy(sp_int[:, 0:1], CLIP).then_inc(sp_index, 1)
                    dve.scalar_tensor_tensor(out=TAKE, in0=SAME, scalar=unsorted[:, :], in1=REAL, op0=ALU.max, op1=ALU.mult).then_inc(sp_chain, 1)
                    dve.wait_ge(sp_chain, CHAIN * k + 4)
                    dve.wait_ge(sp_idled, k + 1)
                    dve.wait_ge(sp_rows_in, 16 * k + 16)
                    dve.tensor_copy(SCALE, sp_rows[:, 2 * VW:VROW].bitcast(f32))
                    dve.tensor_tensor(sp_val[:, :], sp_rows[:, 0:VW], sp_rows[:, VW:2 * VW], ALU.add).then_inc(sp_chain, 1)
                    dve.wait_ge(sp_chain, CHAIN * k + 5)
                    dve.tensor_tensor(TAKE, TAKE, SCALE, ALU.mult).then_inc(sp_chain, 1)
                    dve.wait_ge(sp_chain, CHAIN * k + 6)
                    dve.tensor_scalar(sp_hot[:, :], sp_iota[:, :], LO, TAKE, ALU.is_equal, ALU.mult)
                    with dve.Fori(0, NS) as s:
                        for r in range(HS):
                            last = dve.scalar_tensor_tensor(out=sp_pick[:, r, :], in0=sp_iota[:, bass.ds(s * HS + r, 1)].broadcast_to([P, VW]),
                                                            scalar=HI, in1=sp_val[:, :], op0=ALU.is_equal, op1=ALU.mult)
                        last.then_inc(sp_picked, 1)
                        dve.wait_ge(sp_ps, k * NS + s + 1)
                        rows = acc[:, bass.ds(s * HS, HS), :]
                        dve.tensor_tensor(rows, rows, psum[:, 0:HS, 0:VW], ALU.add).then_inc(sp_added, 1)
                        dve.wait_ge(sp_added, k * NS + s + 1)
                    dve.sem_inc(sp_chunk_done, 1)
            dve.wait_ge(iota_ready, 2)

            def hot(b, op):
                g, kind, half = op // HOT_OPS, op % HOT_OPS // 2, op % 2
                if op % HOT_OPS == 0 and not (isinstance(b, int) and b == 0 and g < RING):
                    dve.wait_ge(cnt_ps, b * NU + (g + 1 - RING) * (CG // UC))
                src, out_, iota, w = ((lo_list, hot_lo, iota_lo, P), (hi_list, hot_hi, iota_hi, 2 * NHI))[kind]
                n, c0 = CG // 2, half * (CG // 2)
                last = dve.tensor_tensor(out_[g % RING][:, :, c0:c0 + n],
                                         src[:, bass.ds(b, 1), g * CG + c0:g * CG + c0 + n].broadcast_to([P, w, n]),
                                         iota[:, :, c0:c0 + n], ALU.is_equal)
                if op % HOT_OPS == HOT_OPS - 1:
                    last.then_inc(hot_ready, 1)

            def take_sum(b, s, k):
                slot = s * NSL + k
                first, n = SLOTS_OF[k]
                rows = acc[:, s * HS + first:s * HS + first + n, :]
                dve.wait_ge(sum_ps, b * SPR + slot + 1)
                bank = 4 + 2 * (slot % 2)
                dve.tensor_tensor(rows, rows, psum[:, bank:bank + n, 0:VW], ALU.add).then_inc(sum_ps_free, 1)

            def take_p2(b, par):
                dve.tensor_copy(p2_round[par][:, :], gate_p2[:, bass.ds(2 * b, 2)]).then_inc(p2_ready, 1)

            take_p2(0, 0)
            for b in range(2):
                for op in range(HOT_OPS * NCG):
                    hot(b, op)
            for op in range(HOT_OPS * LEAD):
                hot(2, op)
            dve.wait_ge(acc_zero, 1)

            def residual(s):
                t0 = s * HS
                dve.wait_ge(sum_ps_free, (NPAIR - 1) * SPR + (s + 1) * NSL + 2)
                if s > 0:
                    dve.wait_ge(x_again_used, s)
                after(dve.tensor_scalar(den[:, 0, :], acc[:, t0:t0 + HS, D], 1e-12 * VSCALE, None, ALU.max))
                after(dve.tensor_scalar(den[:, 1, :], acc[:, t0:t0 + HS, D], 0.0, None, ALU.is_gt))
                settle()
                after(dve.reciprocal(den[:, 2, :], den[:, 0, :]))
                settle()
                after(dve.tensor_tensor(den[:, 0, :], den[:, 2, :], den[:, 1, :], ALU.mult))
                settle()
                dve.wait_ge(x_again_in[s % 2], 16 * (s // 2 + 1))
                for r in range(HS):
                    last = dve.scalar_tensor_tensor(out=acc[:, t0 + r, 0:D], in0=acc[:, t0 + r, 0:D], scalar=den[:, 0, r:r + 1],
                                                    in1=x_again[s % 2][:, r, :], op0=ALU.mult, op1=ALU.add)
                last.then_inc(x_again_used, 1)

            def norm_statistics(s):
                t0 = s * HS
                dve.wait_ge(x_again_used, s + 1)
                for r in range(HS):
                    after(dve.bn_stats(stats[:, t0 + r, :], acc[:, t0 + r, 0:D]))
                settle()
                for r in range(HS):
                    last = dve.bn_aggr(mean_var[:, t0 + r, :], stats[:, t0 + r, :])
                after(last)

            def invert_deviations(s0, s1, n):
                dve.wait_ge(std2_ready, n)
                after(dve.reciprocal(rstd[:, s0 * HS:(s1 + 1) * HS], rstd[:, s0 * HS:(s1 + 1) * HS]))
                settle()

            def prep_norm(ch):
                c, par, n, t0 = ch
                if not (isinstance(c, int) and c == 0):
                    dve.wait_ge(xt2_ps, c * KC)
                for j in range(n):
                    last = dve.tensor_scalar(xn2[:, j, :], acc[:, bass.ds(t0 + j, 1), 0:D], mean_var[:, bass.ds(t0 + j, 1), 0],
                                             rstd[:, bass.ds(t0 + j, 1)], ALU.subtract, ALU.mult)
                last.then_inc(xn2_ready, 1)

            first = chunk(0, 0)

            def body(b, par, has_next, has_next2, tiles):
                if not has_next:
                    for what, s in LAST_ORDER:
                        if what == "sum":
                            for k in range(NSL):
                                take_sum(b, s, k)
                        elif what == "rows":
                            residual(s)
                        elif what == "norm":
                            norm_statistics(s)
                            settle()
                            dve.sem_inc(var2_ready, 1)
                        else:
                            invert_deviations(0, 0, 1)
                            dve.wait_ge(hot_ready, NPAIR * NCG)
                            prep_norm(first)
                    return
                for s in range(NS):
                    for k in range(NSL):
                        take_sum(b, s, k)
                        if s == 0 and k == 0:
                            take_p2(b + 1, 1 - par)
                        slot = s * NSL + k
                        for op in range(HOT_OPS * NCG * slot // SPR, HOT_OPS * NCG * (slot + 1) // SPR):
                            later, at = divmod(op + HOT_OPS * LEAD, HOT_OPS * NCG)
                            if not isinstance(b, int) or b + 2 + later < NPAIR:
                                hot(b + 2 + later, at)
            rounds(dve, body)
            dve.wait_ge(x_again_used, NS)
            for l in range(LAYERS):
                dve.sem_inc(h_ready[l], KC)

            def prep_rest(ch):
                c, par, n, t0 = ch
                for k in range(KC):
                    dve.wait_ge(xt2_hi, c * KC + k + 1)
                    dve.tensor_tensor(xt2[par][1][:, k, 0:n * P], psum[:, 6 + k, 0:n * P], xt2[par][0][:, k, 0:n * P].bitcast(f32),
                                      ALU.subtract).then_inc(xt2_ready, 1)

            def prep_softmax(ch):
                c, par, n, t0 = ch
                dve.wait_ge(route_ps, c + 1)
                dve.tensor_tensor(logits[:, 0:n, :], psum[:, 6, 0:n * N_EXP].rearrange("p (t e) -> p t e", e=N_EXP),
                                  br_sb[:, :].unsqueeze(1).broadcast_to([P, n, N_EXP]), ALU.add).then_inc(soft, 1)
                dve.wait_ge(soft, 4 * c + 1)
                dve.tensor_reduce(out=top[:, 0:n], in_=logits[:, 0:n, :], axis=AX.X, op=ALU.max).then_inc(soft, 1)
                dve.wait_ge(soft, 4 * c + 2)
                dve.tensor_tensor(logits[:, 0:n, :], logits[:, 0:n, :], top[:, 0:n].unsqueeze(2).broadcast_to([P, n, N_EXP]),
                                  ALU.subtract).then_inc(route_shifted, 1)

            def prep_weights(ch):
                c, par, n, t0 = ch
                dve.wait_ge(route_exp, c + 1)
                dve.tensor_reduce(out=top[:, 0:n], in_=expert_w[par][:, 0:n, :], axis=AX.X, op=ALU.add).then_inc(soft, 1)
                dve.wait_ge(soft, 4 * c + 3)
                dve.reciprocal(top[:, 0:n], top[:, 0:n]).then_inc(soft, 1)
                dve.wait_ge(soft, 4 * c + 4)
                dve.tensor_tensor(expert_w[par][:, 0:n, :], expert_w[par][:, 0:n, :],
                                  top[:, 0:n].unsqueeze(2).broadcast_to([P, n, N_EXP]), ALU.mult).then_inc(route_ready, 1)

            def prep_bias(ch):
                c, par, n, t0 = ch
                dve.wait_ge(bias_ps, c + 1)
                for b in range(2):
                    m = min(2, n - 2 * b)
                    rows = acc[:, bass.ds(t0 + 2 * b, m), 0:D]
                    dve.tensor_tensor(rows, rows, psum[:, 6 + b, 0:m * D].rearrange("p (t d) -> p t d", d=D), ALU.add).then_inc(bias_read, 1)

            def rest(l, ch, e):
                c, par, n, t0 = ch
                q = c * N_EXP + e
                h = h1[e % 2] if l == 0 else h2
                for m in range(KC):
                    dve.wait_ge(layer_read[l], q * KC + m + 1 + KC)
                    dve.tensor_tensor(h[1][:, m, 0:n * P], relu_out[l][m][:, 0:n * P], h[0][:, m, 0:n * P].bitcast(f32),
                                      ALU.subtract).then_inc(h_ready[l], 1)

            def take_y(ch, e):
                c, par, n, t0 = ch
                q = c * N_EXP + e
                for j in range(n):
                    if j % 2 == 0:
                        dve.wait_ge(y_ps, 2 * q + j // 2 + 1)
                    row = acc[:, bass.ds(t0 + j, 1), 0:D]
                    last = dve.scalar_tensor_tensor(out=row, in0=psum[:, 4 + j // 2, (j % 2) * D:(j % 2 + 1) * D].unsqueeze(1),
                                                    scalar=expert_w[par][:, j, e:e + 1], in1=row, op0=ALU.mult, op1=ALU.add)
                    if j % 2 == 1 or j == n - 1:
                        last.then_inc(y_read, 1)
                if e == N_EXP - 1:
                    dve.wait_ge(y_read, 2 * q + 4)
                    dve.sem_inc(rows_ready, 1)

            prep_rest(first)
            prep_softmax(first)
            prep_weights(first)
            rest(0, first, 0)
            prep_bias(first)
            dve.wait_ge(bias_read, 4)

            def step(prev, cur, nxt, e):
                if e + 1 < N_EXP:
                    rest(0, cur, e + 1)
                elif nxt is not None:
                    rest(0, nxt, 0)
                if e > 0:
                    take_y(cur, e - 1)
                elif prev is not None:
                    take_y(prev, N_EXP - 1)
                rest(1, cur, e)
                if nxt is not None:
                    if e == 0:
                        prep_norm(nxt)
                    if e == 1:
                        prep_rest(nxt)
                    if e == 2:
                        prep_softmax(nxt)
                    if e == 3:
                        prep_weights(nxt)
                    if e == 5:
                        prep_bias(nxt)
                if isinstance(cur[0], int) and (cur[0], e) in NORM_AT:
                    norm_statistics(NORM_AT[(cur[0], e)])
                    if NORM_AT[(cur[0], e)] in [s1 for s0, s1 in NORM_END.values()]:
                        settle()
                        dve.sem_inc(var2_ready, 1)
                for i, (at, (s0, s1)) in enumerate(NORM_END.items()):
                    if isinstance(cur[0], int) and (cur[0], e) == at:
                        invert_deviations(s0, s1, 2 + i)
            chunks(dve, step)
            take_y(chunk(N_CHUNK - 1, (N_CHUNK - 1) % 2), N_EXP - 1)


_INS = ['x', 'dst', 'edges', 'L0_gnn_W1', 'L0_gnn_b1', 'L0_gnn_W2', 'L0_gnn_b2', 'L0_ffn_Wr', 'L0_ffn_br', 'L0_ffn_W1',
        'L0_ffn_b1', 'L0_ffn_g1', 'L0_ffn_be1', 'L0_ffn_m1', 'L0_ffn_v1', 'L0_ffn_W2', 'L0_ffn_b2', 'L0_ffn_g2',
        'L0_ffn_be2', 'L0_ffn_m2', 'L0_ffn_v2', 'L0_ffn_Wo', 'L0_ffn_bo']


def kernel(**inputs):
    import numpy as np
    import concourse.bacc as bacc
    from concourse.bass_utils import run_bass_kernel_spmd

    nc = bacc.Bacc("TRN2", target_bir_lowering=False, num_devices=1)
    laid = {n: np.ascontiguousarray(a) for n, a in inputs.items() if n not in ("src", "dst")}
    laid["x"] = np.zeros((NT * P, D), inputs["x"].dtype)
    laid["x"][:N_NODES] = inputs["x"]
    laid["edges"] = np.full((E_PAD, 2), DST_PAD, inputs["dst"].dtype)
    laid["edges"][:N_EDGES, 0] = inputs["dst"]
    laid["edges"][:N_EDGES, 1] = inputs["src"]
    laid["dst"] = np.full((DST_ROWS, 1), DST_PAD, inputs["dst"].dtype)
    laid["dst"][:FRONT] = -1
    laid["dst"][FRONT:FRONT + N_EDGES, 0] = inputs["dst"]
    arrays, args = {}, []
    for name in _INS:
        a = laid[name]
        arrays[f"in_{name}_dram"] = a
        args.append(nc.dram_tensor(f"in_{name}_dram", a.shape, mybir.dt.from_np(a.dtype), kind="ExternalInput").ap())
    args.append(nc.dram_tensor("out_0_dram", (NT * P, D), mybir.dt.float32, kind="ExternalOutput").ap())
    args.append(nc.dram_tensor("values_scratch", (NT * P, VROW), mybir.dt.float16).ap())
    program(nc, *args)
    r = run_bass_kernel_spmd(nc, [arrays], core_ids=[0])
    return r.results[0]["out_0_dram"][:N_NODES]
```

```python
import concourse.bass as bass
from concourse import mybir
from contextlib import ExitStack

P = 128
N_NODES = 6250
N_EDGES = 200000
D = 256
HID = 128
N_EXP = 8
KC = D // P
NT = -(-N_NODES // P)
NPAIR = (NT + 1) // 2
NT2 = 2 * NPAIR
SLOT = 64
WIN = SLOT + 1
BLK = 512
NBLK = -(-N_EDGES // BLK)
E_PAD = (NBLK + 1) * BLK
FRONT = SLOT
SORT_P = 125
SORT_N = N_EDGES // SORT_P
DST_ROWS = FRONT + E_PAD + SORT_N
SPILL_CH = -(-N_EDGES // P)
DST_PAD = 16384
GT = 7
NG = NT // GT
VW = D + 2
SG = 5
NSG = NT2 // SG
OWN_COARSE = 2
OWN_FINE = 1
BLK_BUFS = 4
COARSE = ((0, 1), (1, 3), (3, NSG))
STAT_LOTS = ((0, 2), (2, 4), (4, NG))
LG = 10
NLG = NT2 // LG
NHI = NT
NONE_HI = 127
VROW = 2 * VW + 2
VSCALE = 1024.0
CG = 16
NCG = P // CG
RING = 4
LEAD = 2
HOT_OPS = 4
UC = 4
NU = P // UC
HS = 7
NS = NHI // HS
SLOTS_OF = ((0, 2), (2, 2), (4, 2), (6, 1))
NSL = len(SLOTS_OF)
SPR = NS * NSL
EXP_BITS = 0x7F800000
LN_EPS = 1e-5
BN_EPS = 1e-3
CH = 4
N_SHORT = -NT % CH
N_CHUNK = -(-NT // CH)
LAYERS = 2
TERM_STEP = 32
N_STACK = 2 * TERM_STEP + N_EXP
N_PART = 2 * (LAYERS + 1)
STAGES = 3
LAST_ORDER = (("sum", 0), ("rows", 0), ("statistics", 0), ("sum", 1), ("sum", 2), ("rows", 1), ("normalise", 0), ("sum", 3),
              ("sum", 4), ("rows", 2), ("sum", 5), ("sum", 6), ("rows", 3), ("rows", 4), ("split", 0), ("rows", 5),
              ("shift", 0), ("rows", 6), ("weights", 0))
NORM_AT = {(0, 4): 1, (0, 5): 2, (1, 2): 3, (1, 4): 4, (1, 6): 5, (2, 2): 6}
NORM_END = {(0, 6): (1, 2), (2, 4): (3, 6)}


def program(nc, x, dst, edges, g_w1, g_b1, g_w2, g_b2, f_wr, f_br, f_w1, f_b1, f_g1, f_be1, f_m1, f_v1,
            f_w2, f_b2, f_g2, f_be2, f_m2, f_v2, f_wo, f_bo, out, values):
    f32, bf16, f16 = mybir.dt.float32, mybir.dt.bfloat16, mybir.dt.float16
    i32, u16, f32r = mybir.dt.int32, mybir.dt.uint16, mybir.dt.float32r
    ALU, ACT, AX = mybir.AluOpType, mybir.ActivationFunctionType, mybir.AxisListType

    stack = ExitStack()
    with stack:
        def sem(name):
            return stack.enter_context(nc.semaphore(name))

        def sb(where, name, shape, dt):
            return where.enter_context(nc.sbuf_tensor(name, shape, dt))

        ident = sb(stack, "ident", [P, P], f32)
        ident16 = sb(stack, "ident16", [P, P], bf16)
        ones_row = sb(stack, "ones_row", [1, P], f32)
        eps_ln = sb(stack, "eps_ln", [P, 1], f32)
        stats = sb(stack, "stats", [P, NT, 6], f32)
        mean_var = sb(stack, "mean_var", [P, NT, 2], f32)
        rstd = sb(stack, "rstd", [P, NT], f32)
        bn_cols = sb(stack, "bn_cols", [P, 2 * LAYERS, N_EXP * KC], f32)
        wr_sb = sb(stack, "wr_sb", [P, KC, N_EXP], f32)
        wr_parts = sb(stack, "wr_parts", [P, KC, 2, N_EXP], f32r)
        br_sb = sb(stack, "br_sb", [P, N_EXP], f32)
        bo_parts = sb(stack, "bo_parts", [N_STACK, D], f32r)
        eps_bn = sb(stack, "eps_bn", [P, 1], f32)
        den = sb(stack, "den", [P, 3, HS], f32)
        logits = sb(stack, "logits", [P, CH, N_EXP], f32)
        top = sb(stack, "top", [P, CH], f32)
        expert_w = [sb(stack, f"expert_w{i}", [P, CH, N_EXP], f32) for i in range(2)]
        ones_sq = sb(stack, "ones_sq", [P, P], f32)
        flags = sb(stack, "flags", [P, 2], f32)
        unsorted = sb(stack, "unsorted", [P, 1], f32)
        general = sb(stack, "general", [P, 1], f32)
        general_i = sb(stack, "general_i", [P, 1], i32)
        gate_p2 = sb(stack, "gate_p2", [P, NT2], f32)
        p2_round = [sb(stack, f"p2_round{i}", [P, 2], f32) for i in range(2)]
        lists = ExitStack()
        hi_list = sb(lists, "hi_list", [P, NPAIR, P], bf16)
        iota_lo = sb(lists, "iota_lo", [P, P, CG], bf16)
        iota_hi = sb(lists, "iota_hi", [P, 2 * NHI, CG], bf16)
        lo_list = sb(lists, "lo_list", [P, NPAIR, P], bf16)
        psum = stack.enter_context(nc.psum_tensor("psum", [P, 8, 512], f32))

        ph1 = ExitStack()
        x_sb = sb(ph1, "x_sb", [P, NT, D], f32)
        xn = [sb(ph1, f"xn{i}", [P, GT, D], f32) for i in range(2)]
        xt = sb(ph1, "xt", [P, KC, GT * P], f32)
        hid = sb(ph1, "hid", [P, GT * P], f32)
        gate = sb(ph1, "gate", [P, NT], f32)
        p2_inv = sb(ph1, "p2_inv", [P, GT], i32)
        gate_m = sb(ph1, "gate_m", [P, GT], f32)
        vf = sb(ph1, "vf", [P, GT, VW], f32)
        vs = [sb(ph1, f"vs{i}", [P, GT, VROW], f16) for i in range(2)]
        bo_sb = sb(ph1, "bo_sb", [N_STACK, D], f32)
        w1_sb = sb(ph1, "w1_sb", [P, KC, HID], f32)
        b1_sb = sb(ph1, "b1_sb", [HID, 1], f32)
        w2_sb = sb(ph1, "w2_sb", [HID, 1], f32)
        b2_neg = sb(ph1, "b2_neg", [P, 1], f32)
        b2_sb = sb(ph1, "b2_sb", [P, 1], f32)
        hi_bias = sb(ph1, "hi_bias", [P, 1], f32)
        node_i = sb(ph1, "node_i", [P, NT2], i32)
        node_id = sb(ph1, "node_id", [P, NT2], f32)
        node_cmp = sb(ph1, "node_cmp", [P, NT2], f32)
        less = sb(ph1, "less", [P, 2, BLK], bf16)
        node_half = sb(ph1, "node_half", [P, NT2], f32)
        signs = sb(ph1, "signs", [P, 2, BLK], bf16)
        n_blocks = sb(ph1, "n_blocks", [P, NT2], f32)
        block_f = sb(ph1, "block_f", [P, NT2], f32)
        block_i = sb(ph1, "block_i", [P, NT2], i32)
        n_less = sb(ph1, "n_less", [P, NT2], f32)
        sign_sum = sb(ph1, "sign_sum", [P, NT2], f32)
        row_f = sb(ph1, "row_f", [P, NT2], f32)
        row_i = sb(ph1, "row_i", [P, NT2], i32)
        blk_i = [sb(ph1, f"blk_i{i}", [P, SG, BLK], i32) for i in range(2)]
        more_blk = ExitStack()
        blk_i += [sb(more_blk, f"blk_i{i}", [P, SG, BLK], i32) for i in range(2, BLK_BUFS)]
        more_blk.close()
        slot_ok = sb(ph1, "slot_ok", [P, NT2, WIN], bf16)
        slot_hi = sb(ph1, "slot_hi", [P, LG, SLOT], i32)
        slot_lo = sb(ph1, "slot_lo", [P, LG, SLOT], i32)
        hi16 = sb(ph1, "hi16", [P, NT2, SLOT], bf16)
        lo16 = sb(ph1, "lo16", [P, NT2, SLOT], bf16)
        early = ExitStack()
        bn_rows = sb(early, "bn_rows", [N_EXP * KC, 5 * LAYERS, P], f32)
        bn_tmp = sb(early, "bn_tmp", [N_EXP * KC, 2 * LAYERS, P], f32)
        order_i = sb(early, "order_i", [SORT_P, SORT_N + 1], i32)
        samp_i = sb(early, "samp_i", [1, NBLK], i32)
        samp_f = sb(early, "samp_f", [1, NBLK], f32)
        samp = sb(early, "samp", [P, NBLK], f32)
        order_f = sb(early, "order_f", [SORT_P, SORT_N], bf16)
        early.close()
        win = sb(ph1, "win", [P, NT2, 2 * WIN], i32)
        ph1.close()
        ph2 = ExitStack()
        acc = sb(ph2, "acc", [P, NT, VW], f32)
        counts = [None, None]
        counts_t = [None, None]
        for i in (1, 0):
            counts[i] = sb(ph2, f"counts{i}", [P, 2 * NHI, P], bf16)
        for i in (1, 0):
            counts_t[i] = [sb(ph2, f"counts_t{i}{k}", [P, NHI * P], bf16) for k in range(2)]
        vring = [sb(ph2, f"vring{i}", [P, 2, 2 * VW], f16) for i in range(2)]
        hot_lo = [sb(ph2, f"hot_lo{i}", [P, P, CG], bf16) for i in range(RING)]
        hot_hi = [sb(ph2, f"hot_hi{i}", [P, 2 * NHI, CG], bf16) for i in range(RING)]
        ph2.close()
        ph2s = ExitStack()
        sb(ph2s, "acc_below3", [P, NT, VW], f32)
        sp_edge = sb(ph2s, "sp_edge", [P, 2], i32)
        sp_prev = sb(ph2s, "sp_prev", [P, 1], i32)
        sp_f = sb(ph2s, "sp_f", [P, 10], f32)
        sp_int = sb(ph2s, "sp_int", [P, 4], i32)
        sp_iota_i = sb(ph2s, "sp_iota_i", [P, P], i32)
        sp_iota = sb(ph2s, "sp_iota", [P, P], f32)
        sp_idle = sb(ph2s, "sp_idle", [P, 1], f32)
        sp_hot = sb(ph2s, "sp_hot", [P, P], f32)
        sp_rows = sb(ph2s, "sp_rows", [P, VROW], f16)
        sp_val = sb(ph2s, "sp_val", [P, VW], f32)
        sp_pick = sb(ph2s, "sp_pick", [P, HS, VW], f32)
        ph2s.close()
        lists.close()
        first_rows = ExitStack()
        sb(first_rows, "xn2_below", [P, CH, D], f32)
        x_again = [sb(first_rows, f"x_again{i}", [P, HS, D], f32) for i in range(2)]
        first_rows.close()

        ph3 = ExitStack()
        xn2 = sb(ph3, "xn2", [P, CH, D], f32)
        relu_out = [[sb(ph3, f"relu_out{l}{m}", [P, CH * P], f32) for m in range(KC)] for l in range(LAYERS)]
        expert_wt = sb(ph3, "expert_wt", [N_STACK, CH * P], f32r)
        h2_lo = sb(ph3, "h2_lo", [P, KC, CH * P], f32r)
        w_parts = sb(ph3, "w_parts", [P, CH, N_STACK], f32r)
        sb(ph3, "lists_rest", [P, 2 * NPAIR * P + (P + 2 * NHI) * CG - 2 * (CH * D + (LAYERS * KC + 1 + KC) * CH * P + CH * N_STACK)], bf16)
        sb(ph3, "acc_kept", [P, NT, VW], f32)
        w_split = [[sb(ph3, f"w{l}_{n}", [P, N_EXP, KC, D], f32r) for n in ("hi", "lo")] for l in range(LAYERS + 1)]
        xt2, h1 = [None, None], [None, None]
        stage = ExitStack()
        sb(stage, "xt2_below", [P, 2 * KC, CH * P], f32)
        w_stage = [sb(stage, f"w_stage{i}", [P, N_EXP // 2, KC, D], f32) for i in range(STAGES)]
        stage.close()
        for i in range(2):
            xt2[i] = [sb(ph3, f"xt2_{n}{i}", [P, KC, CH * P], f32r) for n in ("hi", "lo")]
            h1[i] = [sb(ph3, f"h1_{n}{i}", [P, KC, CH * P], f32r) for n in ("hi", "lo")]
        h2 = [sb(ph3, "h2_hi", [P, KC, CH * P], f32r), h2_lo]
        ph3.close()

        consts_ready = sem("consts_ready")
        cleared = sem("cleared")
        x_in = [sem(f"x_in{i}") for i in range(len(STAT_LOTS))]
        gate_w_in = sem("gate_w_in")
        samp_in = sem("samp_in")
        chain = sem("chain")
        pool_chain = sem("pool_chain")
        order_in = sem("order_in")
        order_ready = sem("order_ready")
        order_total = sem("order_total")
        general_count = sem("general_count")
        general_total = sem("general_total")
        general_ready = sem("general_ready")
        sp_iota_ready = sem("sp_iota_ready")
        sp_chain = sem("sp_chain")
        sp_edge_in = sem("sp_edge_in")
        sp_prev_in = sem("sp_prev_in")
        sp_index = sem("sp_index")
        sp_rows_in = sem("sp_rows_in")
        sp_idled = sem("sp_idled")
        sp_picked = sem("sp_picked")
        sp_ps = sem("sp_ps")
        sp_added = sem("sp_added")
        sp_chunk_done = sem("sp_chunk_done")
        var_ready = sem("var_ready")
        std_ready = sem("std_ready")
        samp_f_ready = sem("samp_f_ready")
        samp_bc = sem("samp_bc")
        samp_ready = sem("samp_ready")
        act_chain = sem("act_chain")
        block_ready = sem("block_ready")
        blk_in = [sem(f"blk_in{i}") for i in range(BLK_BUFS)]
        row_ready = sem("row_ready")
        win_in = [sem(f"win_in{g}") for g in range(NLG)]
        slots_ready = sem("slots_ready")
        lists_tp = sem("lists_tp")
        lists_ready = sem("lists_ready")
        xn_ready = sem("xn_ready")
        xt_ps = sem("xt_ps")
        xt_ready = sem("xt_ready")
        hid_ps = sem("hid_ps")
        hid_ready = sem("hid_ready")
        logit_ps = sem("logit_ps")
        gate_ready = sem("gate_ready")
        vf_ready = sem("vf_ready")
        vs_hi = sem("vs_hi")
        vs_ready = sem("vs_ready")
        vs_out = [sem(f"vs_out{i}") for i in range(2)]
        phase1_done = sem("phase1_done")
        iota_ready = sem("iota_ready")
        exp_ready = sem("exp_ready")
        acc_zero = sem("acc_zero")
        hot_ready = sem("hot_ready")
        p2_ready = sem("p2_ready")
        cnt_ps = sem("cnt_ps")
        cnt_ps_free = sem("cnt_ps_free")
        tp_ps = sem("tp_ps")
        tp_ps_free = sem("tp_ps_free")
        v_in = [sem(f"v_in{i}") for i in range(2)]
        sum_ps = sem("sum_ps")
        sum_ps_free = sem("sum_ps_free")
        fin_ready = sem("fin_ready")
        x_again_in = [sem(f"x_again_in{i}") for i in range(2)]
        x_again_used = sem("x_again_used")
        bn_in = sem("bn_in")
        bo_in = sem("bo_in")
        bo_rounded = sem("bo_rounded")
        bo_ready = sem("bo_ready")
        bn_std = sem("bn_std")
        bn_row_ready = sem("bn_row_ready")
        bn_tp = sem("bn_tp")
        bn_ready = sem("bn_ready")
        w_in = [sem(f"w_in{i}") for i in range(STAGES)]
        w_hi = sem("w_hi")
        w_ready = sem("w_ready")
        var2_ready = sem("var2_ready")
        std2_ready = sem("std2_ready")
        xn2_ready = sem("xn2_ready")
        xt2_ps = sem("xt2_ps")
        xt2_hi = sem("xt2_hi")
        xt2_ready = sem("xt2_ready")
        soft = sem("soft")
        route_ps = sem("route_ps")
        route_shifted = sem("route_shifted")
        route_exp = sem("route_exp")
        route_ready = sem("route_ready")
        route_tp = sem("route_tp")
        route_t_ready = sem("route_t_ready")
        bias_ps = sem("bias_ps")
        bias_read = sem("bias_read")
        layer_ps = [sem(f"layer_ps{l}") for l in range(LAYERS)]
        layer_read = [sem(f"layer_read{l}") for l in range(LAYERS)]
        h_ready = [sem(f"h_ready{l}") for l in range(LAYERS)]
        y_ps = sem("y_ps")
        y_read = sem("y_read")
        rows_ready = sem("rows_ready")
        out_done = sem("out_done")

        block = stack.enter_context(nc.Block())
        x_tiles = x.rearrange("(t p) d -> p t d", p=P)
        v_rows = values.rearrange("(t p) w -> p t w", p=P)

        def units_of(slot):
            return range(NU * slot // SPR, NU * (slot + 1) // SPR)

        def chunk(c, par):
            if isinstance(c, int) and c < N_SHORT:
                return c, par, CH - 1, c * (CH - 1)
            return c, par, CH, c * CH - N_SHORT

        def chunks(eng, step):
            def one(c, par, first, last):
                prev = None if first else chunk(c - 1, 1 - par)
                if isinstance(c, int) and c == N_SHORT and not first:
                    prev = chunk(N_SHORT - 1, 1 - par)
                nxt = None if last else chunk(c + 1, 1 - par)
                for e in range(N_EXP):
                    step(prev, chunk(c, par), nxt, e)
            head = N_SHORT + 1
            pairs = (N_CHUNK - head - 1) // 2
            for c in range(head):
                one(c, c % 2, c == 0, False)
            with eng.Fori(0, pairs) as i:
                for k in range(2):
                    one(2 * i + (head + k), (head + k) % 2, False, False)
            for c in range(head + 2 * pairs, N_CHUNK):
                one(c, c % 2, False, c == N_CHUNK - 1)

        def blk_buf(g):
            return g if g < BLK_BUFS else g % 2

        def blk_there(g):
            return 16 * SG * (1 if g < BLK_BUFS else 1 + (g - BLK_BUFS) // 2 + 1)

        def block_edges(g, j):
            return blk_i[blk_buf(g)][:, j, :].bitcast(u16).rearrange("p (k two) -> p k two", two=2)[:, :, 0]

        def act_counts(g):
            return (SG - OWN_COARSE) * NSG + (SG - OWN_FINE) * (g + 1)

        def weight_part(i):
            l, half = divmod(i, 2)
            e = slice(half * (N_EXP // 2), (half + 1) * (N_EXP // 2))
            return (f_w1, f_w2, f_wo)[l][e], w_split[l][0][:, e, :, :], w_split[l][1][:, e, :, :]

        def rounds(eng, body):
            with eng.Fori(0, (NPAIR - 3) // 2) as i:
                for par in range(2):
                    body(2 * i + par, par, True, True, 2)
            for b in range((NPAIR - 3) // 2 * 2, NPAIR):
                body(b, b % 2, b + 1 < NPAIR, b + 2 < NPAIR, 2 if b + 1 < NPAIR else NT - 2 * (NPAIR - 1))

        @block.sync
        def _(sp):
            sp.dma_start(samp_i[:, :], dst[FRONT:FRONT + NBLK * BLK, 0:1].rearrange("(b k) o -> o b k", k=BLK)[:, :, 0],
                         allow_slow_non_contiguous=True).then_inc(samp_in, 16)
            sp.dma_start(w1_sb[:, :, :], g_w1.rearrange("(k p) h -> p k h", p=P)).then_inc(gate_w_in, 16)
            sp.dma_start(b1_sb[:, :], g_b1.rearrange("(p o) -> p o", o=1)).then_inc(gate_w_in, 16)
            sp.dma_start(w2_sb[:, :], g_w2).then_inc(gate_w_in, 16)
            sp.dma_start(b2_sb[:, :], g_b2.rearrange("(p o) -> p o", o=1).broadcast_to([P, 1])).then_inc(gate_w_in, 16)
            for l, params in enumerate(((f_g1, f_b1, f_m1, f_be1, f_v1), (f_g2, f_b2, f_m2, f_be2, f_v2))):
                for k, prm in enumerate(params):
                    sp.dma_start(bn_rows[:, 5 * l + k, :], prm.rearrange("e (m p) -> (e m) p", p=P)).then_inc(bn_in, 16)
            sp.dma_start(wr_sb[:, :, :], f_wr.rearrange("(k p) e -> p k e", p=P)).then_inc(bn_in, 16)
            sp.dma_start(br_sb[:, :], f_br.rearrange("(o e) -> o e", o=1).broadcast_to([P, N_EXP])).then_inc(bn_in, 16)
            sp.dma_start(order_i[:, 0:SORT_N], dst[FRONT:FRONT + N_EDGES, 0:1].rearrange("(p k) o -> p (k o)", k=SORT_N)).then_inc(order_in, 16)
            sp.dma_start(order_i[:, SORT_N:SORT_N + 1],
                         dst[FRONT + SORT_N:FRONT + SORT_N + N_EDGES, 0:1].rearrange("(p k) o -> p (k o)", k=SORT_N)[:, 0:1],
                         allow_slow_non_contiguous=True).then_inc(order_in, 16)
            for b in range(NG):
                lot = [b in range(*lot) for lot in STAT_LOTS].index(True)
                if b > 0 and b == STAT_LOTS[lot][0]:
                    early = (1, BLK_BUFS - 1)[lot - 1]
                    sp.wait_ge(blk_in[blk_buf(early)], blk_there(early))
                sp.dma_start(x_sb[:, b * GT:(b + 1) * GT, :], x_tiles[:, b * GT:(b + 1) * GT, :]).then_inc(x_in[lot], 16)

            sp.wait_ge(cleared, 3)
            for i in range(3):
                sp.dma_start(bo_sb[i * TERM_STEP:i * TERM_STEP + N_EXP, :], f_bo).then_inc(bo_in, 16)

            def store(b, par):
                sp.wait_ge(vs_ready, b + 1)
                sp.dma_start(v_rows[:, bass.ds(b * GT, GT), :],
                             vs[par][:, :, :]).then_inc(vs_out[par], 16)
            with sp.Fori(0, NG // 2) as i:
                for par in range(2):
                    store(2 * i + par, par)
            store(NG - 1, 0)
            sp.wait_ge(vs_out[0], 16 * (NG // 2 + 1))
            sp.wait_ge(vs_out[1], 16 * (NG // 2))
            sp.sem_inc(phase1_done, 1)
            sp.wait_ge(phase1_done, 5)

            def load_values(b, par, tiles):
                sp.dma_start(vring[par][:, 0:tiles, :], v_rows[:, bass.ds(2 * b, tiles), 0:2 * VW]).then_inc(v_in[par], 16)
            load_values(0, 0, 2)
            load_values(1, 1, 2)

            def body(b, par, has_next, has_next2, tiles):
                if has_next2:
                    sp.wait_ge(sum_ps, SPR * (b + 1))
                    load_values(b + 2, par, 2 if not isinstance(b, int) or b + 3 < NPAIR else NT - 2 * (NPAIR - 1))
            rounds(sp, body)

            def load_rows(s):
                if s >= 2:
                    sp.wait_ge(x_again_used, s - 1)
                sp.dma_start(x_again[s % 2][:, :, :], x_tiles[:, s * HS:(s + 1) * HS, :]).then_inc(x_again_in[s % 2], 16)

            def load_weights(i):
                if i >= STAGES:
                    sp.wait_ge(w_ready, i - STAGES + 1)
                sp.dma_start(w_stage[i % STAGES][:, :, :, :],
                             weight_part(i)[0].rearrange("e (k p) h -> p e k h", p=P)).then_inc(w_in[i % STAGES], 16)
            sp.wait_ge(cnt_ps_free, NPAIR * NU + 2)
            for load, i in ((load_rows, 0), (load_rows, 1), (load_weights, 0), (load_weights, 1), (load_weights, 2),
                            (load_rows, 2), (load_weights, 3), (load_rows, 3), (load_weights, 4), (load_rows, 4),
                            (load_weights, 5), (load_rows, 5), (load_rows, 6)):
                load(i)

            out_tiles = out.rearrange("(t p) d -> p t d", p=P)

            def step(prev, cur, nxt, e):
                if e == 0 and prev is not None:
                    c, par, n, t0 = prev
                    sp.wait_ge(rows_ready, c + 1)
                    sp.dma_start(out_tiles[:, bass.ds(t0, n), :], acc[:, bass.ds(t0, n), 0:D]).then_inc(out_done, 16)
            chunks(sp, step)
            c, par, n, t0 = chunk(N_CHUNK - 1, (N_CHUNK - 1) % 2)
            sp.wait_ge(rows_ready, c + 1)
            sp.dma_start(out_tiles[:, bass.ds(t0, n), :], acc[:, bass.ds(t0, n), 0:D]).then_inc(out_done, 16)
            sp.wait_ge(out_done, 16 * N_CHUNK)

        @block.gpsimd
        def _(pool):
            pool.memset(ident[:, :], 0.0).then_inc(pool_chain, 1)
            pool.memset(ident16[:, :], 0.0).then_inc(pool_chain, 1)
            pool.iota(node_i[:, :], pattern=[[P, NT2]], base=0, channel_multiplier=1).then_inc(pool_chain, 1)
            pool.wait_ge(pool_chain, 3)
            for m in (ident, ident16):
                pool.affine_select(out=m[:, :], in_=m[:, :], compare_op=ALU.not_equal, fill=1.0, base=0,
                                   pattern=[[-1, P]], channel_multiplier=1).then_inc(consts_ready, 1)
            pool.tensor_copy(node_id[:, :], node_i[:, :]).then_inc(consts_ready, 1)
            pool.memset(hi_bias[:, :], float(NONE_HI)).then_inc(consts_ready, 1)
            pool.memset(ones_row[:, :], 1.0).then_inc(consts_ready, 1)
            pool.memset(ones_sq[:, :], 1.0).then_inc(consts_ready, 1)
            pool.memset(eps_ln[:, :], LN_EPS).then_inc(consts_ready, 1)
            pool.memset(eps_bn[:, :], BN_EPS).then_inc(consts_ready, 1)
            pool.wait_ge(consts_ready, 8)
            pool.memset(hi_bias[SLOT:P, :], float(NONE_HI + NHI)).then_inc(consts_ready, 1)

            pool.wait_ge(consts_ready, 9)
            pool.memset(vf[:, :, :], 0.0).then_inc(cleared, 1)
            pool.memset(gate_p2[:, :], 0.0).then_inc(cleared, 1)
            pool.wait_ge(cleared, 2)
            pool.memset(bo_sb[:, :], 0.0).then_inc(cleared, 1)

            def fetch_blocks(g):
                for j in range(SG):
                    pool.indirect_dma_start(out=blk_i[blk_buf(g)][:, j, :], out_offset=None, in_=dst[:, :],
                                            in_offset=bass.IndirectOffsetOnAxis(ap=block_i[:, g * SG + j:g * SG + j + 1], axis=0),
                                            ).then_inc(blk_in[blk_buf(g)], 16)

            def fetch_windows(g):
                pool.wait_ge(row_ready, g + 1)
                for t in range(g * SG, (g + 1) * SG):
                    pool.indirect_dma_start(out=win[:, t, :], out_offset=None, in_=edges[:, :],
                                            in_offset=bass.IndirectOffsetOnAxis(ap=row_i[:, t:t + 1], axis=0),
                                            ).then_inc(win_in[t // LG], 16)
            for lot, (g0, g1) in enumerate(COARSE):
                pool.wait_ge(block_ready, lot + 1)
                for g in range(g0, min(g1, BLK_BUFS)):
                    fetch_blocks(g)
            pool.iota(iota_lo[:, :, :], pattern=[[1, P], [0, CG]], base=0, channel_multiplier=0,
                      allow_small_or_imprecise_dtypes=True).then_inc(iota_ready, 1)
            pool.iota(iota_hi[:, :, :], pattern=[[1, 2 * NHI], [0, CG]], base=0, channel_multiplier=0,
                      allow_small_or_imprecise_dtypes=True).then_inc(iota_ready, 1)
            pool.wait_ge(order_ready, 1)
            pool.wait_ge(bn_tp, 1)
            ahead = BLK_BUFS
            for g in range(NSG):
                fetch_windows(g)
                while ahead < NSG and (ahead - BLK_BUFS if ahead < BLK_BUFS + 2 else ahead - 2) <= g:
                    fetch_blocks(ahead)
                    ahead += 1
            pool.drain().then_inc(phase1_done, 1)
            pool.wait_ge(phase1_done, 5)

            pool.wait_ge(general_ready, 1)
            with pool.If(pool.value_load(general_i[0:1, 0:1], min_val=0, max_val=1) > 0):
                pool.iota(sp_iota_i[:, :], pattern=[[1, P]], base=0, channel_multiplier=0).then_inc(sp_iota_ready, 1)
                pool.wait_ge(sp_iota_ready, 1)
                pool.tensor_copy(sp_iota[:, :], sp_iota_i[:, :]).then_inc(sp_iota_ready, 1)
                with pool.Fori(0, SPILL_CH) as k:
                    pool.wait_ge(sp_chunk_done, k + 1)
                    pool.dma_start(sp_edge[:, :], edges[bass.ds(k * P, P), :]).then_inc(sp_edge_in, 16)
                    pool.dma_start(sp_prev[:, :], dst[bass.ds(k * P, P), :]).then_inc(sp_prev_in, 16)
                    pool.wait_ge(sp_index, k + 1)
                    pool.tensor_tensor(sp_idle[:, :], sp_iota[:, 0:1], sp_iota[:, 0:1], ALU.subtract).then_inc(sp_idled, 1)
                    pool.indirect_dma_start(out=sp_rows[:, :], out_offset=None, in_=values[:, :],
                                            in_offset=bass.IndirectOffsetOnAxis(ap=sp_int[:, 0:1], axis=0)).then_inc(sp_rows_in, 16)

            with pool.If(pool.value_load(general_i[0:1, 0:1], min_val=0, max_val=1) < 1):
                pool.memset(acc[:, :, :], 0.0)
            pool.drain().then_inc(acc_zero, 1)

            pool.wait_ge(hot_ready, NPAIR * NCG)
            pool.memset(w_parts[:, :, :].bitcast(f32), 0.0).then_inc(cleared, 1)

            for i in range(N_PART):
                pool.wait_ge(w_hi, i + 1)
                _, hi, lo = weight_part(i)
                pool.tensor_tensor(lo, w_stage[i % STAGES][:, :, :, :], hi.bitcast(f32), ALU.subtract).then_inc(w_ready, 1)

        @block.scalar
        def _(act):
            n_counted = [0]

            def count_signs(values, t, width):
                n = n_counted[0]
                if n >= 2:
                    act.wait_ge(act_chain, n - 1)
                act.activation(signs[:, n % 2, 0:width], values, ACT.Sign, scale=-1.0,
                               bias=node_half[:, t:t + 1], accum_out=sign_sum[:, t:t + 1]).then_inc(act_chain, 1)
                n_counted[0] += 1

            def search(g):
                act.wait_ge(blk_in[blk_buf(g)], blk_there(g))
                for j in range(OWN_FINE, SG):
                    count_signs(block_edges(g, j), g * SG + j, BLK)

            def batch_norm():
                act.wait_ge(bn_in, 16 * (5 * LAYERS + 2))
                for l in range(LAYERS):
                    act.activation(bn_tmp[:, 2 * l, :], bn_rows[:, 5 * l + 4, :], ACT.Sqrt, bias=eps_bn[0:N_EXP * KC, :]).then_inc(bn_std, 1)
                act.activation(wr_parts[:, :, 0, :], wr_sb[:, :, :], ACT.Copy).then_inc(bn_std, 1)

            def take_batch_norm():
                act.wait_ge(bn_tp, 1)
                act.activation(bn_cols[:, :, :].rearrange("p a b -> p (a b)"), psum[:, 7, 0:2 * LAYERS * N_EXP * KC], ACT.Copy).then_inc(bn_ready, 1)

            def row_deviations(lot):
                tiles = slice(STAT_LOTS[lot][0] * GT, STAT_LOTS[lot][1] * GT)
                act.wait_ge(var_ready, lot + 1)
                act.activation(rstd[:, tiles], mean_var[:, tiles, 1], ACT.Sqrt, bias=eps_ln[:, :]).then_inc(std_ready, 1)

            def take_rows(b):
                act.wait_ge(xt_ps, b + 1)
                if b > 0:
                    act.wait_ge(hid_ps, b)
                for q in range(4):
                    k, lo, n = q // 2, 512 * (q % 2), (512, GT * P - 512)[q % 2]
                    act.activation(xt[:, k, lo:lo + n], psum[:, q, 0:n], ACT.Copy).then_inc(xt_ready, 1)

            def gate_layer(b):
                act.wait_ge(hid_ps, b + 1)
                for q in range(2):
                    lo, n = 512 * q, (512, GT * P - 512)[q]
                    act.activation(hid[:, lo:lo + n], psum[:, 4 + q, 0:n], ACT.Relu, bias=b1_sb[:, :]).then_inc(hid_ready, 1)

            def gate_exp(b):
                act.wait_ge(logit_ps, b + 1)
                act.activation(gate[:, b * GT:(b + 1) * GT], psum[:, 7, 0:GT], ACT.Exp, scale=-1.0, bias=b2_neg[:, :]).then_inc(gate_ready, 1)

            def round_values(b):
                act.wait_ge(vf_ready, b + 1)
                if b >= 2:
                    act.wait_ge(vs_out[b % 2], 16 * (b // 2))
                act.activation(vs[b % 2][:, :, 0:VW], vf[:, :, :], ACT.Copy).then_inc(vs_hi, 1)

            act.wait_ge(consts_ready, 10)
            act.wait_ge(samp_ready, 1)
            for g in range(NSG):
                for j in range(OWN_COARSE, SG):
                    count_signs(samp[:, :], g * SG + j, NBLK)
            batch_norm()
            act.wait_ge(block_ready, len(COARSE))
            search(0)
            row_deviations(0)
            search(1)
            take_rows(0)
            take_batch_norm()
            search(2)
            search(3)
            act.wait_ge(gate_w_in, 64)
            act.wait_ge(exp_ready, 1)
            for b in range(NG):
                gate_layer(b)
                if b + 1 < NG:
                    take_rows(b + 1)
                gate_exp(b)
                if b + 1 < len(STAT_LOTS):
                    row_deviations(b + 1)
                if b + 4 < NSG:
                    search(b + 4)
                round_values(b)
            act.wait_ge(bo_in, 48)
            act.activation(bo_parts[:, :], bo_sb[:, :], ACT.Copy).then_inc(bo_rounded, 1)
            for g in range(NLG):
                t0, w = g * LG // 2, LG // 2
                act.wait_ge(lists_tp, 2 * g + 1)
                act.activation(hi_list[:, t0:t0 + w, :].rearrange("p t c -> p (t c)"),
                               psum[:, 5, :].bitcast(bf16)[:, 0:w * P], ACT.Identity, bias=hi_bias[:, :]).then_inc(lists_ready, 1)
                act.wait_ge(lists_tp, 2 * g + 2)
                act.activation(lo_list[:, t0:t0 + w, :].rearrange("p t c -> p (t c)"),
                               psum[:, 6, :].bitcast(bf16)[:, 0:w * P], ACT.Copy).then_inc(lists_ready, 1)
            act.drain().then_inc(phase1_done, 1)
            act.wait_ge(phase1_done, 5)
            act.sem_inc(cnt_ps_free, 2)
            act.sem_inc(tp_ps_free, 2)

            def take_counts(b, par, u):
                act.wait_ge(cnt_ps, b * NU + u + 1)
                src = psum[:, u % 2, 0:UC * 2 * NHI].rearrange("p (c j) -> p j c", c=UC)
                act.activation(counts[par][:, :, u * UC:(u + 1) * UC], src, ACT.Copy).then_inc(cnt_ps_free, 1)

            def take_transposed(b, par, s, tile):
                if s == 0 and tile == 0:
                    act.wait_ge(p2_ready, b + 1)
                act.wait_ge(tp_ps, b * 2 * NS + 2 * s + tile + 1)
                act.activation(counts_t[par][tile][:, s * HS * P:(s + 1) * HS * P], psum[:, 2 + tile, :].bitcast(bf16)[:, 0:HS * P],
                               ACT.Copy, scale=p2_round[par][:, tile:tile + 1]).then_inc(tp_ps_free, 1)

            for u in range(NU):
                take_counts(0, 0, u)
            for slot in range(SPR):
                for u in units_of(slot):
                    take_counts(1, 1, u)
                if slot % 2 == 0:
                    take_transposed(0, 0, slot // NSL, slot % NSL // 2)

            def body(b, par, has_next, has_next2, tiles):
                for s in range(NS):
                    for k in range(NSL):
                        if has_next2:
                            for u in units_of(s * NSL + k):
                                take_counts(b + 2, par, u)
                        if has_next and k % 2 == 0:
                            take_transposed(b + 1, 1 - par, s, k // 2)
            rounds(act, body)

            def round_weights(i):
                act.wait_ge(w_in[i % STAGES], 16 * (i // STAGES + 1))
                act.activation(weight_part(i)[1], w_stage[i % STAGES][:, :, :, :], ACT.Copy).then_inc(w_hi, 1)

            def deviations(s0, s1, n):
                act.wait_ge(var2_ready, n)
                tiles = slice(s0 * HS, (s1 + 1) * HS)
                act.activation(rstd[:, tiles], mean_var[:, tiles, 1], ACT.Sqrt, bias=eps_ln[:, :]).then_inc(std2_ready, 1)

            act.wait_ge(sum_ps, (NPAIR - 1) * SPR)
            round_weights(0)
            round_weights(1)
            deviations(0, 0, 1)
            round_weights(2)
            round_weights(3)

            def prep_rows(ch):
                c, par, n, t0 = ch
                for k in range(KC):
                    act.wait_ge(xt2_ps, c * KC + k + 1)
                    act.activation(xt2[par][0][:, k, 0:n * P], psum[:, 6 + k, 0:n * P], ACT.Copy).then_inc(xt2_hi, 1)

            def prep_exp(ch):
                c, par, n, t0 = ch
                act.wait_ge(route_shifted, c + 1)
                act.activation(expert_w[par][:, 0:n, :], logits[:, 0:n, :], ACT.Exp).then_inc(route_exp, 1)

            def prep_wt(ch):
                c, par, n, t0 = ch
                act.wait_ge(route_tp, c + 1)
                act.activation(expert_wt[:, 0:n * P], psum[0:N_STACK, 7, 0:n * P], ACT.Copy).then_inc(route_t_ready, 1)

            def relu(layer, ch, e):
                c, par, n, t0 = ch
                q = c * N_EXP + e
                h = h1[e % 2] if layer == 0 else h2
                for m in range(KC):
                    col = e * KC + m
                    scale, shift = bn_cols[:, 2 * layer, col:col + 1], bn_cols[:, 2 * layer + 1, col:col + 1]
                    act.wait_ge(layer_ps[layer], q * KC + m + 1)
                    act.wait_ge(h_ready[layer], q * KC + m + 1)
                    act.activation(relu_out[layer][m][:, 0:n * P], psum[:, 2 * layer + m, 0:n * P], ACT.Relu,
                                   bias=shift, scale=scale)
                    act.activation(h[0][:, m, 0:n * P], psum[:, 2 * layer + m, 0:n * P], ACT.Relu,
                                   bias=shift, scale=scale).then_inc(layer_read[layer], 1)

            first = chunk(0, 0)
            prep_rows(first)
            round_weights(4)
            round_weights(5)
            prep_exp(first)
            act.wait_ge(x_again_used, NS)
            act.wait_ge(w_ready, 4)
            relu(0, first, 0)
            prep_wt(first)
            act.wait_ge(w_ready, N_PART)

            def step(prev, cur, nxt, e):
                if e + 1 < N_EXP:
                    relu(0, cur, e + 1)
                elif nxt is not None:
                    relu(0, nxt, 0)
                relu(1, cur, e)
                if nxt is not None:
                    if e == 1:
                        prep_rows(nxt)
                    if e == 3:
                        prep_exp(nxt)
                    if e == 4:
                        prep_wt(nxt)
                if isinstance(cur[0], int) and (cur[0], e) in NORM_END:
                    s0, s1 = NORM_END[(cur[0], e)]
                    deviations(s0, s1, 2 + list(NORM_END).index((cur[0], e)))
            chunks(act, step)

        @block.tensor
        def _(pe):
            pe.wait_ge(consts_ready, 9)
            pe.wait_ge(samp_f_ready, 1)
            pe.matmul(psum[:, 7, 0:NBLK], ones_row[:, :], samp_f[:, :], start=True, stop=True).then_inc(samp_bc, 1)

            def gate_rows(b, par):
                pe.wait_ge(xn_ready, b + 1)
                pe.wait_ge(xt_ready, 4 * b + 4)
                for k in range(KC):
                    for j in range(GT):
                        last = pe.transpose(psum[:, 2 * k + j // 4, (j % 4) * P:(j % 4 + 1) * P],
                                            xn[par][:, j, k * P:(k + 1) * P], ident[:, :])
                last.then_inc(xt_ps, 1)

            def gate_layer1(b):
                pe.wait_ge(xt_ready, 4 * b + 8)
                pe.wait_ge(hid_ready, 2 * b + 2)
                for q in range(2):
                    lo, n = 512 * q, (512, GT * P - 512)[q]
                    for k in range(KC):
                        last = pe.matmul(psum[:, 4 + q, 0:n], w1_sb[:, k, :], xt[:, k, lo:lo + n],
                                         start=(k == 0), stop=(k == KC - 1))
                last.then_inc(hid_ps, 1)

            def gate_layer2(b):
                pe.wait_ge(hid_ready, 2 * b + 4)
                pe.wait_ge(gate_ready, b + 1)
                for j in range(GT):
                    last = pe.matmul(psum[:, 7, j:j + 1], hid[:, j * P:(j + 1) * P], w2_sb[:, :], start=True, stop=True)
                last.then_inc(logit_ps, 1)
            pe.sem_inc(xt_ready, 4)
            pe.sem_inc(hid_ready, 2)
            pe.sem_inc(gate_ready, 1)
            gate_rows(0, 0)

            pe.wait_ge(bn_row_ready, 1)
            pe.wait_ge(bn_ready, 1)
            for k in range(2 * LAYERS):
                w = N_EXP * KC
                last = pe.transpose(psum[:, 7, k * w:(k + 1) * w], bn_tmp[:, k, :], ident[0:w, 0:w])
            last.then_inc(bn_tp, 1)

            pe.wait_ge(order_ready, 1)
            pe.wait_ge(bn_ready, 2)
            pe.matmul(psum[:, 7, 0:1], ones_sq[:, :], flags[:, 0:1], start=True, stop=True).then_inc(order_total, 1)

            pe.wait_ge(gate_w_in, 64)
            with pe.Fori(0, NG // 2) as i:
                for par in range(2):
                    gate_layer1(2 * i + par)
                    gate_rows(2 * i + (par + 1), 1 - par)
                    gate_layer2(2 * i + par)
            gate_layer1(NG - 1)
            gate_layer2(NG - 1)

            for g in range(NLG):
                for m, lst, bank in ((2 * g, hi16, 5), (2 * g + 1, lo16, 6)):
                    if m % 2 == 0:
                        pe.wait_ge(slots_ready, g + 1)
                    if m >= 2:
                        pe.wait_ge(lists_ready, m - 1)
                    for u in range(LG // 2):
                        t = g * LG + 2 * u
                        last = pe.transpose(psum[:, bank, :].bitcast(bf16)[:, u * P:(u + 1) * P],
                                            lst[:, t:t + 2, :].rearrange("p t s -> p (t s)"), ident16[:, :])
                    last.then_inc(lists_tp, 1)
            pe.wait_ge(general_count, 1)
            pe.matmul(psum[:, 7, 8:10], ones_sq[:, :], flags[:, :], start=True, stop=True).then_inc(general_total, 1)
            pe.drain().then_inc(phase1_done, 1)
            pe.wait_ge(phase1_done, 5)
            pe.wait_ge(general_ready, 1)
            with pe.If(pe.value_load(general_i[0:1, 0:1], min_val=0, max_val=1) > 0):
                with pe.Fori(0, SPILL_CH) as k:
                    with pe.Fori(0, NS) as s:
                        pe.wait_ge(sp_picked, k * NS + s + 1)
                        for r in range(HS):
                            last = pe.matmul(psum[:, r, 0:VW], sp_hot[:, :], sp_pick[:, r, :], start=True, stop=True)
                        last.then_inc(sp_ps, 1)

            def count(b, u):
                g = u // (CG // UC)
                if u % (CG // UC) == 0:
                    pe.wait_ge(hot_ready, b * NCG + g + 1)
                pe.wait_ge(cnt_ps_free, b * NU + u + 1)
                for c in range(UC):
                    col = u % (CG // UC) * UC + c
                    last = pe.matmul(psum[:, u % 2, c * 2 * NHI:(c + 1) * 2 * NHI], hot_lo[g % RING][:, :, col],
                                     hot_hi[g % RING][:, :, col], start=True, stop=True)
                last.then_inc(cnt_ps, 1)

            def transpose_counts(b, par, s, tile):
                if s == 0 and tile == 0:
                    pe.wait_ge(cnt_ps_free, (b + 1) * NU + 2)
                pe.wait_ge(tp_ps_free, b * 2 * NS + 2 * s + tile + 1)
                for r in range(HS):
                    last = pe.transpose(psum[:, 2 + tile, :].bitcast(bf16)[:, r * P:(r + 1) * P],
                                        counts[par][:, tile * NHI + s * HS + r, :], ident16[:, :])
                last.then_inc(tp_ps, 1)

            def sums(b, par, s, k, tiles):
                if k == 0:
                    pe.wait_ge(tp_ps_free, b * 2 * NS + 2 * s + 4)
                if s == 0 and k == 0:
                    pe.wait_ge(v_in[par], (b - par) * 8 + 16)
                slot = s * NSL + k
                pe.wait_ge(sum_ps_free, b * SPR + slot + 1)
                first, n = SLOTS_OF[k]
                for r in range(n):
                    hi = s * HS + first + r
                    for tile in range(tiles):
                        for half in range(2):
                            last = pe.matmul(psum[:, 4 + 2 * (slot % 2) + r, 0:VW], counts_t[par][tile][:, hi * P:(hi + 1) * P],
                                             vring[par][:, tile, half * VW:(half + 1) * VW],
                                             start=(tile == 0 and half == 0), stop=(tile == tiles - 1 and half == 1))
                last.then_inc(sum_ps, 1)

            for u in range(NU):
                count(0, u)
            for slot in range(SPR):
                for u in units_of(slot):
                    count(1, u)
                if slot % 2 == 0:
                    transpose_counts(0, 0, slot // NSL, slot % NSL // 2)

            def body(b, par, has_next, has_next2, tiles):
                for s in range(NS):
                    for k in range(NSL):
                        sums(b, par, s, k, tiles)
                        if has_next2:
                            for u in units_of(s * NSL + k):
                                count(b + 2, u)
                        if has_next and k % 2 == 0:
                            transpose_counts(b + 1, 1 - par, s, k // 2)
            rounds(pe, body)

            pe.wait_ge(sum_ps_free, NPAIR * SPR + 2)
            pe.wait_ge(cnt_ps_free, NPAIR * NU + 2)
            pe.wait_ge(tp_ps_free, NPAIR * 2 * NS + 2)
            pe.wait_ge(bo_ready, 1)
            for l in range(LAYERS):
                pe.sem_inc(layer_read[l], KC)
            pe.sem_inc(y_read, 2)
            pe.sem_inc(bias_read, 2)
            TERMS = ((0, 0), (0, 1), (1, 0))

            def prep_tp(ch):
                c, par, n, t0 = ch
                pe.wait_ge(xn2_ready, c + 1)
                pe.wait_ge(bias_read, 2 * c + 2)
                for k in range(KC):
                    for j in range(n):
                        last = pe.transpose(psum[:, 6 + k, j * P:(j + 1) * P], xn2[:, j, k * P:(k + 1) * P], ident[:, :])
                    last.then_inc(xt2_ps, 1)

            def prep_route(ch):
                c, par, n, t0 = ch
                pe.wait_ge(xt2_ready, c * KC + KC)
                for j in range(n):
                    at, rows = 2 * j * N_EXP, slice(j * P, (j + 1) * P)
                    for k in range(KC):
                        pe.matmul(psum[:, 6, at:at + 2 * N_EXP], xt2[par][0][:, k, rows],
                                  wr_parts[:, k, :, :].rearrange("p a e -> p (a e)"), start=(k == 0), stop=False)
                    for k in range(KC):
                        last = pe.matmul(psum[:, 6, at:at + N_EXP], xt2[par][1][:, k, rows], wr_parts[:, k, 0, :],
                                         start=False, stop=(k == KC - 1))
                last.then_inc(route_ps, 1)

            def prep_wt(ch):
                c, par, n, t0 = ch
                pe.wait_ge(route_ready, c + 1)
                for j in range(n):
                    last = pe.transpose(psum[0:N_STACK, 7, j * P:(j + 1) * P], w_parts[:, j, :].bitcast(f32), ident[:, :])
                last.then_inc(route_tp, 1)

            def prep_bias(ch):
                c, par, n, t0 = ch
                pe.wait_ge(route_t_ready, c + 1)
                for j in range(n):
                    last = pe.matmul(psum[:, 6 + j // 2, (j % 2) * D:(j % 2 + 1) * D], expert_wt[:, j * P:(j + 1) * P],
                                     bo_parts[:, :], start=True, stop=True)
                last.then_inc(bias_ps, 1)

            def layer(l, ch, e):
                c, par, n, t0 = ch
                q = c * N_EXP + e
                src = xt2[par] if l == 0 else h1[e % 2]
                if l == 0:
                    pe.wait_ge(xt2_ready, c * KC + KC)
                else:
                    pe.wait_ge(h_ready[0], q * KC + 2 * KC)
                for m in range(KC):
                    pe.wait_ge(layer_read[l], q * KC + m + 1)
                    for i, (a, w) in enumerate(TERMS):
                        for k in range(KC):
                            last = pe.matmul(psum[:, 2 * l + m, 0:n * P], w_split[l][w][:, e, k, m * P:(m + 1) * P],
                                             src[a][:, k, 0:n * P], start=(i == 0 and k == 0),
                                             stop=(i == len(TERMS) - 1 and k == KC - 1))
                    last.then_inc(layer_ps[l], 1)

            def layer3(ch, e):
                c, par, n, t0 = ch
                q = c * N_EXP + e
                pe.wait_ge(h_ready[1], q * KC + 2 * KC)
                for j in range(n):
                    if j % 2 == 0:
                        pe.wait_ge(y_read, 2 * q + j // 2 + 1)
                    for i, (a, w) in enumerate(TERMS):
                        for k in range(KC):
                            last = pe.matmul(psum[:, 4 + j // 2, (j % 2) * D:(j % 2 + 1) * D], h2[a][:, k, j * P:(j + 1) * P],
                                             w_split[2][w][:, e, k, :], start=(i == 0 and k == 0),
                                             stop=(i == len(TERMS) - 1 and k == KC - 1))
                    if j % 2 == 1 or j == n - 1:
                        last.then_inc(y_ps, 1)

            first = chunk(0, 0)
            prep_tp(first)
            prep_route(first)
            pe.wait_ge(w_ready, 2)
            layer(0, first, 0)
            prep_wt(first)
            prep_bias(first)

            def step(prev, cur, nxt, e):
                if e + 1 < N_EXP:
                    layer(0, cur, e + 1)
                elif nxt is not None:
                    layer(0, nxt, 0)
                if prev is None and e == 0:
                    pe.wait_ge(w_ready, 4)
                if prev is None and e == 1:
                    pe.wait_ge(w_ready, N_PART)
                if e > 0:
                    layer3(cur, e - 1)
                elif prev is not None:
                    layer3(prev, N_EXP - 1)
                layer(1, cur, e)
                if nxt is not None:
                    if e == 1:
                        prep_tp(nxt)
                    if e == 2:
                        prep_route(nxt)
                    if e == 4:
                        prep_wt(nxt)
                    if e == 5:
                        prep_bias(nxt)
            chunks(pe, step)
            layer3(chunk(N_CHUNK - 1, (N_CHUNK - 1) % 2), N_EXP - 1)

        @block.vector
        def _(dve):
            n = [0]

            def after(ins):
                n[0] += 1
                ins.then_inc(chain, 1)

            def settle():
                dve.wait_ge(chain, n[0])

            def count_less(values, t, width, out_):
                dve.wait_ge(chain, n[0] - 1)
                after(dve.tensor_scalar(less[:, n[0] % 2, 0:width], values, node_id[:, t:t + 1], None, ALU.is_lt, ALU.add,
                                        accum_out=out_[:, t:t + 1]))

            def check_order():
                dve.wait_ge(order_in, 32)
                after(dve.tensor_tensor(order_f[:, :], order_i[:, 0:SORT_N], order_i[:, 1:SORT_N + 1], ALU.is_gt))
                settle()
                dve.tensor_reduce(out=flags[0:SORT_P, 0:1], in_=order_f[:, :], axis=AX.X, op=ALU.max).then_inc(order_ready, 1)

            dve.wait_ge(samp_in, 16)
            dve.tensor_copy(samp_f[:, :], samp_i[:, :]).then_inc(samp_f_ready, 1)
            dve.wait_ge(consts_ready, 9)
            dve.tensor_scalar(node_half[:, :], node_id[:, :], -0.5, None, ALU.add).then_inc(consts_ready, 1)
            after(dve.memset(flags[:, :], 0.0))
            dve.wait_ge(samp_bc, 1)
            after(dve.tensor_copy(samp[:, :], psum[:, 7, 0:NBLK]))
            settle()
            dve.sem_inc(samp_ready, 1)
            dve.sem_inc(bn_ready, 1)
            for lot, (g0, g1) in enumerate(COARSE):
                for g in range(g0, g1):
                    for j in range(OWN_COARSE):
                        count_less(samp[:, :], g * SG + j, NBLK, n_blocks)
                if lot == len(COARSE) - 1:
                    check_order()
                dve.wait_ge(act_chain, (SG - OWN_COARSE) * g1)
                groups = [c[:, g0 * SG:g1 * SG].rearrange("p (g j) -> p g j", j=SG) for c in (n_blocks, sign_sum)]
                after(dve.tensor_scalar(groups[0][:, :, OWN_COARSE:SG], groups[1][:, :, OWN_COARSE:SG], 0.5, NBLK / 2, ALU.mult, ALU.add))
                settle()
                cols = slice(g0 * SG, g1 * SG)
                after(dve.tensor_scalar(block_f[:, cols], n_blocks[:, cols], -1.0, 0.0, ALU.add, ALU.max))
                settle()
                after(dve.tensor_scalar(block_f[:, cols], block_f[:, cols], float(BLK), None, ALU.mult))
                settle()
                dve.tensor_scalar(block_i[:, cols], block_f[:, cols], float(FRONT), None, ALU.add).then_inc(block_ready, 1)

            def search(g):
                dve.wait_ge(blk_in[blk_buf(g)], blk_there(g))
                for j in range(OWN_FINE):
                    count_less(block_edges(g, j), g * SG + j, BLK, n_less)

            def rows_of(g):
                t0, t1 = g * SG, (g + 1) * SG
                dve.wait_ge(act_chain, act_counts(g))
                after(dve.tensor_scalar(n_less[:, t0 + OWN_FINE:t1], sign_sum[:, t0 + OWN_FINE:t1], 0.5, BLK / 2, ALU.mult, ALU.add))
                settle()
                after(dve.tensor_tensor(row_f[:, t0:t1], block_f[:, t0:t1], n_less[:, t0:t1], ALU.add))
                settle()
                dve.tensor_copy(row_i[:, t0:t1], row_f[:, t0:t1]).then_inc(row_ready, 1)

            def mask_nodes():
                dve.wait_ge(order_total, 1)
                after(dve.tensor_scalar(unsorted[:, :], psum[:, 7, 0:1], 1.0, None, ALU.min))
                settle()
                after(dve.scalar_tensor_tensor(out=node_cmp[:, :], in0=node_id[:, :], scalar=1.0, in1=unsorted[:, :].broadcast_to([P, NT2]),
                                               op0=ALU.add, op1=ALU.mult))
                settle()
                after(dve.tensor_tensor(node_cmp[:, :], node_id[:, :], node_cmp[:, :], ALU.subtract))

            def fold_batch_norm():
                dve.wait_ge(bn_std, LAYERS + 1)
                rows = [[bn_rows[:, 5 * l + k, :] for k in range(4)] + [bn_tmp[:, 2 * l, :], bn_tmp[:, 2 * l + 1, :]]
                        for l in range(LAYERS)]
                for g, bb, m, be, scale, shift in rows:
                    after(dve.reciprocal(scale, scale))
                    after(dve.tensor_tensor(shift, bb, m, ALU.subtract))
                settle()
                for g, bb, m, be, scale, shift in rows:
                    after(dve.tensor_tensor(scale, scale, g, ALU.mult))
                settle()
                for g, bb, m, be, scale, shift in rows:
                    after(dve.tensor_tensor(shift, shift, scale, ALU.mult))
                settle()
                for g, bb, m, be, scale, shift in rows:
                    after(dve.tensor_tensor(shift, shift, be, ALU.add))
                after(dve.tensor_tensor(wr_parts[:, :, 1, :], wr_sb[:, :, :], wr_parts[:, :, 0, :].bitcast(f32), ALU.subtract))
                settle()
                dve.sem_inc(bn_row_ready, 1)
                dve.wait_ge(gate_w_in, 64)
                dve.tensor_scalar(b2_neg[:, :], b2_sb[:, :], -1.0, None, ALU.mult).then_inc(exp_ready, 1)

            def statistics(lot):
                t0, t1 = STAT_LOTS[lot][0] * GT, STAT_LOTS[lot][1] * GT
                dve.wait_ge(x_in[lot], 16 * (t1 - t0) // GT)
                for t in range(t0, t1):
                    after(dve.bn_stats(stats[:, t, :], x_sb[:, t, :]))
                settle()
                for t in range(t0, t1):
                    last = dve.bn_aggr(mean_var[:, t, :], stats[:, t, :])
                last.then_inc(var_ready, 1)

            def invert(lot):
                tiles = slice(STAT_LOTS[lot][0] * GT, STAT_LOTS[lot][1] * GT)
                dve.wait_ge(std_ready, lot + 1)
                after(dve.reciprocal(rstd[:, tiles], rstd[:, tiles]))
                settle()

            def normalise(b):
                for j in range(GT):
                    last = dve.tensor_scalar(xn[b % 2][:, j, :], x_sb[:, b * GT + j, :], mean_var[:, b * GT + j, 0:1],
                                             rstd[:, b * GT + j:b * GT + j + 1], ALU.subtract, ALU.mult)
                last.then_inc(xn_ready, 1)

            def weigh(b):
                par = b % 2
                dve.wait_ge(gate_ready, b + 2)
                w = gate[:, b * GT:(b + 1) * GT]
                p2 = gate_p2[:, b * GT:(b + 1) * GT]
                after(dve.tensor_scalar(w, w, 1.0, None, ALU.add))
                settle()
                after(dve.reciprocal(w, w))
                settle()
                after(dve.tensor_scalar(p2.bitcast(i32), w.bitcast(i32), EXP_BITS, None, ALU.bitwise_and))
                settle()
                after(dve.tensor_scalar(p2_inv[:, :], p2.bitcast(i32), -1.0, float(254 << 23), ALU.mult, ALU.add))
                settle()
                after(dve.scalar_tensor_tensor(out=gate_m[:, :], in0=w, scalar=VSCALE, in1=p2_inv[:, :].bitcast(f32),
                                               op0=ALU.mult, op1=ALU.mult))
                settle()
                if b >= 1:
                    dve.wait_ge(vs_ready, b)
                for j in range(GT):
                    after(dve.tensor_scalar(vf[:, j, 0:D], xn[par][:, j, :], gate_m[:, j:j + 1], None, ALU.mult))
                after(dve.tensor_copy(vf[:, :, D], gate_m[:, :]))
                settle()
                dve.sem_inc(vf_ready, 1)

            def rest_of_values(b):
                par = b % 2
                dve.wait_ge(vs_hi, b + 1)
                dve.tensor_copy(vs[par][:, :, 2 * VW:VROW].bitcast(f32)[:, :, 0], gate_p2[:, b * GT:(b + 1) * GT])
                dve.tensor_tensor(vs[par][:, :, VW:2 * VW], vf[:, :, :], vs[par][:, :, 0:VW], ALU.subtract).then_inc(vs_ready, 1)

            def fill_slots(g):
                t0, t1 = g * LG, (g + 1) * LG
                dve.wait_ge(win_in[g], 16 * LG)
                source = win[:, t0:t1, :].rearrange("p t (s two) -> p t s two", two=2)[:, :, 0:SLOT, 1]
                dest = win[:, t0:t1, :].bitcast(u16).rearrange("p t (s four) -> p t s four", four=4)[:, :, :, 0]
                settle()
                after(dve.tensor_scalar(slot_hi[:, :, :], source, 7, None, ALU.arith_shift_right))
                after(dve.tensor_scalar(slot_lo[:, :, :], source, P - 1, None, ALU.bitwise_and))
                after(dve.tensor_tensor(slot_ok[:, t0:t1, :], dest, node_cmp[:, t0:t1].unsqueeze(2).broadcast_to([P, LG, WIN]), ALU.is_equal))
                settle()
                after(dve.tensor_copy(lo16[:, t0:t1, :], slot_lo[:, :, :]))
                after(dve.scalar_tensor_tensor(out=hi16[:, t0:t1, :], in0=slot_hi[:, :, :], scalar=-float(NONE_HI),
                                               in1=slot_ok[:, t0:t1, 0:SLOT], op0=ALU.add, op1=ALU.mult))
                settle()
                dve.sem_inc(slots_ready, 1)

            statistics(0)
            search(0)
            invert(0)
            normalise(0)
            fold_batch_norm()
            rows_of(0)
            search(1)
            mask_nodes()
            normalise(1)
            rows_of(1)
            statistics(1)
            search(2)
            search(3)
            rows_of(2)
            rows_of(3)
            dve.wait_ge(cleared, 2)
            for b in range(NG):
                weigh(b)
                if b == 0:
                    invert(1)
                if b == 2:
                    invert(2)
                if b + 2 < NG:
                    normalise(b + 2)
                if b == 0:
                    statistics(2)
                if b + 4 < NSG:
                    search(b + 4)
                if b in (1, 3, 5):
                    fill_slots(b // 2)
                if b + 4 < NSG:
                    rows_of(b + 4)
                rest_of_values(b)
            fill_slots(3)
            dve.wait_ge(bo_rounded, 1)
            last_term = slice(2 * TERM_STEP, N_STACK)
            dve.tensor_tensor(bo_parts[last_term, :], bo_sb[last_term, :], bo_parts[last_term, :].bitcast(f32),
                              ALU.subtract).then_inc(bo_ready, 1)
            fill_slots(4)
            dve.tensor_reduce(out=flags[:, 1:2], in_=slot_ok[:, :, SLOT], axis=AX.X, op=ALU.max).then_inc(general_count, 1)
            dve.wait_ge(general_total, 1)
            after(dve.tensor_tensor(general[:, :], psum[:, 7, 9:10], unsorted[:, :], ALU.add))
            settle()
            after(dve.tensor_scalar(general[:, :], general[:, :], 1.0, None, ALU.min))
            settle()
            dve.tensor_copy(general_i[:, :], general[:, :]).then_inc(general_ready, 1)
            dve.drain().then_inc(phase1_done, 1)
            dve.wait_ge(phase1_done, 5)
            dve.wait_ge(general_ready, 1)
            dve.sem_inc(sum_ps_free, 2)

            with dve.If(dve.value_load(general_i[0:1, 0:1], min_val=0, max_val=1) > 0):
                dve.memset(acc[:, :, :], 0.0).then_inc(sp_chain, 1)
                dve.wait_ge(sp_chain, 1)
                dve.wait_ge(sp_iota_ready, 2)
                dve.sem_inc(sp_chunk_done, 1)
                with dve.Fori(0, SPILL_CH) as k:
                    dve.wait_ge(sp_edge_in, 16 * k + 16)
                    dve.wait_ge(sp_prev_in, 16 * k + 16)
                    DST, PREV, LO, HI, TAKE, REAL, CLIP, SAME, SCALE = (sp_f[:, c:c + 1] for c in range(9))
                    CHAIN = 5
                    dve.tensor_copy(DST, sp_edge[:, 0:1])
                    dve.tensor_copy(PREV, sp_prev[:, :])
                    dve.tensor_scalar(sp_int[:, 1:2], sp_edge[:, 1:2], 7, None, ALU.arith_shift_right)
                    dve.tensor_scalar(sp_int[:, 2:3], sp_edge[:, 1:2], P - 1, None, ALU.bitwise_and).then_inc(sp_chain, 1)
                    dve.wait_ge(sp_chain, CHAIN * k + 2)
                    dve.tensor_scalar(CLIP, DST, float(N_NODES - 1), None, ALU.min)
                    dve.tensor_tensor(SAME, DST, PREV, ALU.is_equal)
                    dve.tensor_scalar(REAL, DST, float(DST_PAD), None, ALU.is_lt)
                    dve.tensor_copy(HI, sp_int[:, 1:2])
                    dve.tensor_copy(LO, sp_int[:, 2:3]).then_inc(sp_chain, 1)
                    dve.wait_ge(sp_chain, CHAIN * k + 3)
                    dve.tensor_copy(sp_int[:, 0:1], CLIP).then_inc(sp_index, 1)
                    dve.scalar_tensor_tensor(out=TAKE, in0=SAME, scalar=unsorted[:, :], in1=REAL, op0=ALU.max, op1=ALU.mult).then_inc(sp_chain, 1)
                    dve.wait_ge(sp_chain, CHAIN * k + 4)
                    dve.wait_ge(sp_idled, k + 1)
                    dve.wait_ge(sp_rows_in, 16 * k + 16)
                    dve.tensor_copy(SCALE, sp_rows[:, 2 * VW:VROW].bitcast(f32))
                    dve.tensor_tensor(sp_val[:, :], sp_rows[:, 0:VW], sp_rows[:, VW:2 * VW], ALU.add).then_inc(sp_chain, 1)
                    dve.wait_ge(sp_chain, CHAIN * k + 5)
                    dve.tensor_tensor(TAKE, TAKE, SCALE, ALU.mult).then_inc(sp_chain, 1)
                    dve.wait_ge(sp_chain, CHAIN * k + 6)
                    dve.tensor_scalar(sp_hot[:, :], sp_iota[:, :], LO, TAKE, ALU.is_equal, ALU.mult)
                    with dve.Fori(0, NS) as s:
                        for r in range(HS):
                            last = dve.scalar_tensor_tensor(out=sp_pick[:, r, :], in0=sp_iota[:, bass.ds(s * HS + r, 1)].broadcast_to([P, VW]),
                                                            scalar=HI, in1=sp_val[:, :], op0=ALU.is_equal, op1=ALU.mult)
                        last.then_inc(sp_picked, 1)
                        dve.wait_ge(sp_ps, k * NS + s + 1)
                        rows = acc[:, bass.ds(s * HS, HS), :]
                        dve.tensor_tensor(rows, rows, psum[:, 0:HS, 0:VW], ALU.add).then_inc(sp_added, 1)
                        dve.wait_ge(sp_added, k * NS + s + 1)
                    dve.sem_inc(sp_chunk_done, 1)
            dve.wait_ge(iota_ready, 2)

            def hot(b, op):
                g, kind, half = op // HOT_OPS, op % HOT_OPS // 2, op % 2
                if op % HOT_OPS == 0 and not (isinstance(b, int) and b == 0 and g < RING):
                    dve.wait_ge(cnt_ps, b * NU + (g + 1 - RING) * (CG // UC))
                src, out_, iota, w = ((lo_list, hot_lo, iota_lo, P), (hi_list, hot_hi, iota_hi, 2 * NHI))[kind]
                n, c0 = CG // 2, half * (CG // 2)
                last = dve.tensor_tensor(out_[g % RING][:, :, c0:c0 + n],
                                         src[:, bass.ds(b, 1), g * CG + c0:g * CG + c0 + n].broadcast_to([P, w, n]),
                                         iota[:, :, c0:c0 + n], ALU.is_equal)
                if op % HOT_OPS == HOT_OPS - 1:
                    last.then_inc(hot_ready, 1)

            def take_sum(b, s, k):
                slot = s * NSL + k
                first, n = SLOTS_OF[k]
                rows = acc[:, s * HS + first:s * HS + first + n, :]
                dve.wait_ge(sum_ps, b * SPR + slot + 1)
                bank = 4 + 2 * (slot % 2)
                dve.tensor_tensor(rows, rows, psum[:, bank:bank + n, 0:VW], ALU.add).then_inc(sum_ps_free, 1)

            def take_p2(b, par):
                dve.tensor_copy(p2_round[par][:, :], gate_p2[:, bass.ds(2 * b, 2)]).then_inc(p2_ready, 1)

            take_p2(0, 0)
            for b in range(2):
                for op in range(HOT_OPS * NCG):
                    hot(b, op)
            for op in range(HOT_OPS * LEAD):
                hot(2, op)
            dve.wait_ge(acc_zero, 1)

            def residual(s):
                t0 = s * HS
                dve.wait_ge(sum_ps_free, (NPAIR - 1) * SPR + (s + 1) * NSL + 2)
                if s > 0:
                    dve.wait_ge(x_again_used, s)
                after(dve.tensor_scalar(den[:, 0, :], acc[:, t0:t0 + HS, D], 1e-12 * VSCALE, None, ALU.max))
                after(dve.tensor_scalar(den[:, 1, :], acc[:, t0:t0 + HS, D], 0.0, None, ALU.is_gt))
                settle()
                after(dve.reciprocal(den[:, 2, :], den[:, 0, :]))
                settle()
                after(dve.tensor_tensor(den[:, 0, :], den[:, 2, :], den[:, 1, :], ALU.mult))
                settle()
                dve.wait_ge(x_again_in[s % 2], 16 * (s // 2 + 1))
                for r in range(HS):
                    last = dve.scalar_tensor_tensor(out=acc[:, t0 + r, 0:D], in0=acc[:, t0 + r, 0:D], scalar=den[:, 0, r:r + 1],
                                                    in1=x_again[s % 2][:, r, :], op0=ALU.mult, op1=ALU.add)
                last.then_inc(x_again_used, 1)

            def norm_statistics(s):
                t0 = s * HS
                dve.wait_ge(x_again_used, s + 1)
                for r in range(HS):
                    after(dve.bn_stats(stats[:, t0 + r, :], acc[:, t0 + r, 0:D]))
                settle()
                for r in range(HS):
                    last = dve.bn_aggr(mean_var[:, t0 + r, :], stats[:, t0 + r, :])
                after(last)

            def invert_deviations(s0, s1, n):
                dve.wait_ge(std2_ready, n)
                after(dve.reciprocal(rstd[:, s0 * HS:(s1 + 1) * HS], rstd[:, s0 * HS:(s1 + 1) * HS]))
                settle()

            def prep_norm(ch):
                c, par, n, t0 = ch
                if not (isinstance(c, int) and c == 0):
                    dve.wait_ge(xt2_ps, c * KC)
                for j in range(n):
                    last = dve.tensor_scalar(xn2[:, j, :], acc[:, bass.ds(t0 + j, 1), 0:D], mean_var[:, bass.ds(t0 + j, 1), 0],
                                             rstd[:, bass.ds(t0 + j, 1)], ALU.subtract, ALU.mult)
                last.then_inc(xn2_ready, 1)

            def prep_rest(ch):
                c, par, n, t0 = ch
                for k in range(KC):
                    dve.wait_ge(xt2_hi, c * KC + k + 1)
                    dve.tensor_tensor(xt2[par][1][:, k, 0:n * P], psum[:, 6 + k, 0:n * P], xt2[par][0][:, k, 0:n * P].bitcast(f32),
                                      ALU.subtract).then_inc(xt2_ready, 1)

            def prep_softmax(ch):
                c, par, n, t0 = ch
                dve.wait_ge(route_ps, c + 1)
                parts = psum[:, 6, 0:2 * n * N_EXP].rearrange("p (t a e) -> p t a e", a=2, e=N_EXP)
                dve.tensor_tensor(logits[:, 0:n, :], parts[:, :, 0, :], br_sb[:, :].unsqueeze(1).broadcast_to([P, n, N_EXP]), ALU.add).then_inc(soft, 1)
                dve.wait_ge(soft, 7 * c + 1)
                dve.tensor_tensor(logits[:, 0:n, :], logits[:, 0:n, :], parts[:, :, 1, :], ALU.add).then_inc(soft, 1)
                dve.wait_ge(soft, 7 * c + 2)
                dve.tensor_reduce(out=top[:, 0:n], in_=logits[:, 0:n, :], axis=AX.X, op=ALU.max).then_inc(soft, 1)
                dve.wait_ge(soft, 7 * c + 3)
                dve.tensor_tensor(logits[:, 0:n, :], logits[:, 0:n, :], top[:, 0:n].unsqueeze(2).broadcast_to([P, n, N_EXP]),
                                  ALU.subtract).then_inc(route_shifted, 1)

            def prep_weights(ch):
                c, par, n, t0 = ch
                dve.wait_ge(route_exp, c + 1)
                dve.tensor_reduce(out=top[:, 0:n], in_=expert_w[par][:, 0:n, :], axis=AX.X, op=ALU.add).then_inc(soft, 1)
                dve.wait_ge(soft, 7 * c + 4)
                dve.reciprocal(top[:, 0:n], top[:, 0:n]).then_inc(soft, 1)
                dve.wait_ge(soft, 7 * c + 5)
                dve.tensor_tensor(expert_w[par][:, 0:n, :], expert_w[par][:, 0:n, :],
                                  top[:, 0:n].unsqueeze(2).broadcast_to([P, n, N_EXP]), ALU.mult).then_inc(soft, 1)
                if isinstance(c, int) and c == 0:
                    dve.wait_ge(cleared, 4)
                dve.wait_ge(soft, 7 * c + 6)
                if not (isinstance(c, int) and c == 0):
                    dve.wait_ge(route_tp, c)
                terms = w_parts[:, 0:n, :].rearrange("p t (g e) -> p t g e", e=N_EXP)
                step = TERM_STEP // N_EXP
                dve.tensor_copy(terms[:, :, 0:2 * step + 1:2 * step, :],
                                expert_w[par][:, 0:n, :].unsqueeze(2).broadcast_to([P, n, 2, N_EXP])).then_inc(soft, 1)
                dve.wait_ge(soft, 7 * c + 7)
                dve.tensor_tensor(terms[:, :, step, :], expert_w[par][:, 0:n, :], terms[:, :, 0, :].bitcast(f32),
                                  ALU.subtract).then_inc(route_ready, 1)

            first = chunk(0, 0)

            def body(b, par, has_next, has_next2, tiles):
                if not has_next:
                    for what, s in LAST_ORDER:
                        if what == "sum":
                            for k in range(NSL):
                                take_sum(b, s, k)
                        elif what == "rows":
                            residual(s)
                        elif what == "statistics":
                            norm_statistics(s)
                            settle()
                            dve.sem_inc(var2_ready, 1)
                        elif what == "normalise":
                            invert_deviations(0, 0, 1)
                            dve.wait_ge(hot_ready, NPAIR * NCG)
                            prep_norm(first)
                        elif what == "split":
                            prep_rest(first)
                        elif what == "shift":
                            prep_softmax(first)
                        else:
                            prep_weights(first)
                    return
                for s in range(NS):
                    for k in range(NSL):
                        take_sum(b, s, k)
                        if s == 0 and k == 0:
                            take_p2(b + 1, 1 - par)
                        slot = s * NSL + k
                        for op in range(HOT_OPS * NCG * slot // SPR, HOT_OPS * NCG * (slot + 1) // SPR):
                            later, at = divmod(op + HOT_OPS * LEAD, HOT_OPS * NCG)
                            if not isinstance(b, int) or b + 2 + later < NPAIR:
                                hot(b + 2 + later, at)
            rounds(dve, body)
            dve.wait_ge(x_again_used, NS)
            for l in range(LAYERS):
                dve.sem_inc(h_ready[l], KC)

            def prep_bias(ch):
                c, par, n, t0 = ch
                dve.wait_ge(bias_ps, c + 1)
                for b in range(2):
                    m = min(2, n - 2 * b)
                    rows = acc[:, bass.ds(t0 + 2 * b, m), 0:D]
                    dve.tensor_tensor(rows, rows, psum[:, 6 + b, 0:m * D].rearrange("p (t d) -> p t d", d=D), ALU.add).then_inc(bias_read, 1)

            def rest(l, ch, e):
                c, par, n, t0 = ch
                q = c * N_EXP + e
                h = h1[e % 2] if l == 0 else h2
                for m in range(KC):
                    dve.wait_ge(layer_read[l], q * KC + m + 1 + KC)
                    dve.tensor_tensor(h[1][:, m, 0:n * P], relu_out[l][m][:, 0:n * P], h[0][:, m, 0:n * P].bitcast(f32),
                                      ALU.subtract).then_inc(h_ready[l], 1)

            def take_y(ch, e):
                c, par, n, t0 = ch
                q = c * N_EXP + e
                for j in range(n):
                    if j % 2 == 0:
                        dve.wait_ge(y_ps, 2 * q + j // 2 + 1)
                    row = acc[:, bass.ds(t0 + j, 1), 0:D]
                    last = dve.scalar_tensor_tensor(out=row, in0=psum[:, 4 + j // 2, (j % 2) * D:(j % 2 + 1) * D].unsqueeze(1),
                                                    scalar=expert_w[par][:, j, e:e + 1], in1=row, op0=ALU.mult, op1=ALU.add)
                    if j % 2 == 1 or j == n - 1:
                        last.then_inc(y_read, 1)
                if e == N_EXP - 1:
                    dve.wait_ge(y_read, 2 * q + 4)
                    dve.sem_inc(rows_ready, 1)

            rest(0, first, 0)
            prep_bias(first)
            dve.wait_ge(bias_read, 4)

            def step(prev, cur, nxt, e):
                if e + 1 < N_EXP:
                    rest(0, cur, e + 1)
                elif nxt is not None:
                    rest(0, nxt, 0)
                if e > 0:
                    take_y(cur, e - 1)
                elif prev is not None:
                    take_y(prev, N_EXP - 1)
                rest(1, cur, e)
                if nxt is not None:
                    if e == 0:
                        prep_norm(nxt)
                    if e == 1:
                        prep_rest(nxt)
                    if e == 2:
                        prep_softmax(nxt)
                    if e == 3:
                        prep_weights(nxt)
                    if e == 5:
                        prep_bias(nxt)
                if isinstance(cur[0], int) and (cur[0], e) in NORM_AT:
                    norm_statistics(NORM_AT[(cur[0], e)])
                    if NORM_AT[(cur[0], e)] in [s1 for s0, s1 in NORM_END.values()]:
                        settle()
                        dve.sem_inc(var2_ready, 1)
                for i, (at, (s0, s1)) in enumerate(NORM_END.items()):
                    if isinstance(cur[0], int) and (cur[0], e) == at:
                        invert_deviations(s0, s1, 2 + i)
            chunks(dve, step)
            take_y(chunk(N_CHUNK - 1, (N_CHUNK - 1) % 2), N_EXP - 1)


_INS = ['x', 'dst', 'edges', 'L0_gnn_W1', 'L0_gnn_b1', 'L0_gnn_W2', 'L0_gnn_b2', 'L0_ffn_Wr', 'L0_ffn_br', 'L0_ffn_W1',
        'L0_ffn_b1', 'L0_ffn_g1', 'L0_ffn_be1', 'L0_ffn_m1', 'L0_ffn_v1', 'L0_ffn_W2', 'L0_ffn_b2', 'L0_ffn_g2',
        'L0_ffn_be2', 'L0_ffn_m2', 'L0_ffn_v2', 'L0_ffn_Wo', 'L0_ffn_bo']


def kernel(**inputs):
    import numpy as np
    import concourse.bacc as bacc
    from concourse.bass_utils import run_bass_kernel_spmd

    nc = bacc.Bacc("TRN2", target_bir_lowering=False, num_devices=1)
    laid = {n: np.ascontiguousarray(a) for n, a in inputs.items() if n not in ("src", "dst")}
    laid["x"] = np.zeros((NT * P, D), inputs["x"].dtype)
    laid["x"][:N_NODES] = inputs["x"]
    laid["edges"] = np.full((E_PAD, 2), DST_PAD, inputs["dst"].dtype)
    laid["edges"][:N_EDGES, 0] = inputs["dst"]
    laid["edges"][:N_EDGES, 1] = inputs["src"]
    laid["dst"] = np.full((DST_ROWS, 1), DST_PAD, inputs["dst"].dtype)
    laid["dst"][:FRONT] = -1
    laid["dst"][FRONT:FRONT + N_EDGES, 0] = inputs["dst"]
    arrays, args = {}, []
    for name in _INS:
        a = laid[name]
        arrays[f"in_{name}_dram"] = a
        args.append(nc.dram_tensor(f"in_{name}_dram", a.shape, mybir.dt.from_np(a.dtype), kind="ExternalInput").ap())
    args.append(nc.dram_tensor("out_0_dram", (NT * P, D), mybir.dt.float32, kind="ExternalOutput").ap())
    args.append(nc.dram_tensor("values_scratch", (NT * P, VROW), mybir.dt.float16).ap())
    program(nc, *args)
    r = run_bass_kernel_spmd(nc, [arrays], core_ids=[0])
    return r.results[0]["out_0_dram"][:N_NODES]
```
